# Optimizing a Trainium2 kernel written in Bass

```python
import numpy as np
import jax
import jax.numpy as jnp

def _softmax(x, axis=-1):
    return jax.nn.softmax(x, axis=axis)
def _gelu(x):
    return jax.nn.gelu(x, approximate=True)
def _silu(x):
    return jax.nn.silu(x)
def _sigmoid(x):
    return jax.nn.sigmoid(x)
def _layernorm(x, axis=-1, eps=1e-5):
    m = jnp.mean(x, axis=axis, keepdims=True)
    v = jnp.var(x, axis=axis, keepdims=True)
    return (x - m) / jnp.sqrt(v + eps)
def _scatter_add(tgt, idx, src, axis=0):
    return tgt.at[idx].add(src)
def _segment_sum(src, seg, n):
    return jax.ops.segment_sum(src, seg, n)

kernel_name = 'mk_adj_resnorm_d1_adj_512_120819'

def setup_inputs(seed: int = 0):
    np.random.seed(seed)
    _w = jnp.asarray
    def _rec_inputs():
        import jax
        import jax.numpy as jnp
        _gk = jax.random.key(seed)
        x = -0.0005207 + 1.001 * jax.random.normal(jax.random.fold_in(_gk, 1), (4096, 512), jnp.float32)
        _a = jax.random.bernoulli(jax.random.fold_in(_gk, 2), 0.0078125, (4096, 4096))
        adj = _a.astype(jnp.int32)
        _nm = jnp.ones((4096,), dtype=bool)
        nodemask = jnp.where(_nm, 1.0, 0.0).astype(jnp.int32)
        return x, adj, nodemask
    x, adj, nodemask = _rec_inputs()
    def _L0_gnn_setup():
        import jax, jax.numpy as jnp
        import numpy as np
        D = 512
        H = 8
        HD = D // H
        EPS = 1e-05
        NEG = -1e+30

        def layer_norm(x, scale, bias):
            mu = jnp.mean(x, axis=-1, keepdims=True)
            var = jnp.mean(jnp.square(x - mu), axis=-1, keepdims=True)
            return (x - mu) * jax.lax.rsqrt(var + EPS) * scale + bias
        key = jax.random.key(seed)
        ks = jax.random.split(key, 16)
        S = T = 4096
        inp = {'h_source': jax.random.normal(ks[0], (S, D), jnp.float32), 'h_target': jax.random.normal(ks[1], (T, D), jnp.float32), 'edge_mask': jax.random.randint(ks[2], (T, S), 0, 2, jnp.int32), 'source_mask': jnp.ones((S,), jnp.int32), 'target_mask': jnp.ones((T,), jnp.int32), 'ln1_scale': jnp.ones((D,), jnp.float32), 'ln1_bias': jnp.zeros((D,), jnp.float32), 'Wq': jax.random.normal(ks[3], (D, D), jnp.float32) / np.sqrt(D), 'bq': jnp.zeros((D,), jnp.float32), 'Wk': jax.random.normal(ks[4], (D, D), jnp.float32) / np.sqrt(D), 'bk': jnp.zeros((D,), jnp.float32), 'Wv': jax.random.normal(ks[5], (D, D), jnp.float32) / np.sqrt(D), 'bv': jnp.zeros((D,), jnp.float32), 'Wo': jax.random.normal(ks[6], (D, D), jnp.float32) / np.sqrt(D), 'bo': jnp.zeros((D,), jnp.float32), 'ln2_scale': jnp.ones((D,), jnp.float32), 'ln2_bias': jnp.zeros((D,), jnp.float32), 'W1': jax.random.normal(ks[7], (D, 4 * D), jnp.float32) / np.sqrt(D), 'W2': jax.random.normal(ks[8], (4 * D, D), jnp.float32) / np.sqrt(4 * D)}
        return inp
    _L0_gnn_all = _L0_gnn_setup()
    _L0_gnn_in = {k: v for k, v in _L0_gnn_all.items() if k in ('h_target', 'ln1_scale', 'ln1_bias', 'Wq', 'bq', 'Wk', 'bk', 'Wv', 'bv', 'Wo', 'bo', 'ln2_scale', 'ln2_bias', 'W1', 'W2', )}
    del _L0_gnn_all

    return {
        "x": x,
        "adj": adj,
        "nodemask": nodemask,
        "L0_gnn_h_target": _L0_gnn_in["h_target"],
        "L0_gnn_ln1_scale": _L0_gnn_in["ln1_scale"],
        "L0_gnn_ln1_bias": _L0_gnn_in["ln1_bias"],
        "L0_gnn_Wq": _L0_gnn_in["Wq"],
        "L0_gnn_bq": _L0_gnn_in["bq"],
        "L0_gnn_Wk": _L0_gnn_in["Wk"],
        "L0_gnn_bk": _L0_gnn_in["bk"],
        "L0_gnn_Wv": _L0_gnn_in["Wv"],
        "L0_gnn_bv": _L0_gnn_in["bv"],
        "L0_gnn_Wo": _L0_gnn_in["Wo"],
        "L0_gnn_bo": _L0_gnn_in["bo"],
        "L0_gnn_ln2_scale": _L0_gnn_in["ln2_scale"],
        "L0_gnn_ln2_bias": _L0_gnn_in["ln2_bias"],
        "L0_gnn_W1": _L0_gnn_in["W1"],
        "L0_gnn_W2": _L0_gnn_in["W2"],
    }

def reference(x, adj, nodemask, L0_gnn_h_target, L0_gnn_ln1_scale, L0_gnn_ln1_bias, L0_gnn_Wq, L0_gnn_bq, L0_gnn_Wk, L0_gnn_bk, L0_gnn_Wv, L0_gnn_bv, L0_gnn_Wo, L0_gnn_bo, L0_gnn_ln2_scale, L0_gnn_ln2_bias, L0_gnn_W1, L0_gnn_W2):
    import jax
    import jax.numpy as jnp
    def _L0_gnn_ref(h_source, h_target, edge_mask, source_mask, target_mask, ln1_scale, ln1_bias, Wq, bq, Wk, bk, Wv, bv, Wo, bo, ln2_scale, ln2_bias, W1, W2):
        import jax, jax.numpy as jnp
        import numpy as np
        D = 512
        H = 8
        HD = D // H
        EPS = 1e-05
        NEG = -1e+30

        def layer_norm(x, scale, bias):
            mu = jnp.mean(x, axis=-1, keepdims=True)
            var = jnp.mean(jnp.square(x - mu), axis=-1, keepdims=True)
            return (x - mu) * jax.lax.rsqrt(var + EPS) * scale + bias
        smask = (source_mask == 1)[:, None]
        tmask = (target_mask == 1)[:, None]
        hs = layer_norm(h_source, ln1_scale, ln1_bias)
        ht = layer_norm(h_target, ln1_scale, ln1_bias)
        hs = jnp.where(smask, hs, 0.0)
        ht = jnp.where(tmask, ht, 0.0)
        T, S = (ht.shape[0], hs.shape[0])
        q = (ht @ Wq + bq).reshape(T, H, HD) / jnp.sqrt(jnp.float32(HD))
        k = (hs @ Wk + bk).reshape(S, H, HD)
        v = (hs @ Wv + bv).reshape(S, H, HD)
        logits = jnp.einsum('thd,shd->hts', q, k)
        logits = jnp.where(edge_mask[None] != 0, logits, NEG)
        probs = jax.nn.softmax(logits, axis=-1)
        ctx = jnp.einsum('hts,shd->thd', probs, v).reshape(T, D)
        attn = ctx @ Wo + bo
        attn = jnp.where(tmask, attn, 0.0)
        ht = ht + attn
        ht = layer_norm(ht, ln2_scale, ln2_bias)
        ht = jnp.where(tmask, ht, 0.0)
        ff = jax.nn.gelu(ht @ W1) @ W2
        return ht + ff

    x = _layernorm(x + _L0_gnn_ref(x, L0_gnn_h_target, adj, nodemask, nodemask, L0_gnn_ln1_scale, L0_gnn_ln1_bias, L0_gnn_Wq, L0_gnn_bq, L0_gnn_Wk, L0_gnn_bk, L0_gnn_Wv, L0_gnn_bv, L0_gnn_Wo, L0_gnn_bo, L0_gnn_ln2_scale, L0_gnn_ln2_bias, L0_gnn_W1, L0_gnn_W2), axis=-1)
    return x


_drawn_inputs = setup_inputs


def setup_inputs(seed=0):
    import zlib

    import numpy as np

    out = dict(_drawn_inputs(seed))
    spreads = {'L0_gnn_ln1_scale': (1.0, 0.2),
     'L0_gnn_ln1_bias': (0.0, 0.1),
     'L0_gnn_bq': (0.0, 0.533),
     'L0_gnn_bk': (0.0, 0.8),
     'L0_gnn_bv': (0.0, 0.1),
     'L0_gnn_bo': (0.0, 0.1),
     'L0_gnn_ln2_scale': (1.0, 0.2),
     'L0_gnn_ln2_bias': (0.0, 0.1)}
    factors = {}
    for name, (base, spread) in spreads.items():
        noise = np.random.default_rng([zlib.crc32(name.encode()), seed]).standard_normal(out[name].shape)
        drawn = base * np.exp(spread * noise) if base else spread * noise
        out[name] = jnp.asarray(drawn.astype(out[name].dtype))
    for name, factor in factors.items():
        out[name] = (out[name] * factor).astype(out[name].dtype)
    return out
```

```python
from contextlib import ExitStack

import concourse.bass as bass
from concourse import mybir

ALU = mybir.AluOpType
ACT = mybir.ActivationFunctionType
AX_X = mybir.AxisListType.X
F32 = mybir.dt.float32
F32R = mybir.dt.float32r
BF16 = mybir.dt.bfloat16
I32 = mybir.dt.int32
U8 = mybir.dt.uint8
RMAX = bass.bass_isa.ReduceOp.max

P = 128
N = 4096
D = 512
H = 8
HD = D // H
F = 4 * D
KT = D // P
CH = 512
NC = N // CH
QT = CH // P
ST = N // P
PAIRS = H // 2
FT = F // P
EPS = 1e-5
NEG = -1e30
QSCALE = HD ** -0.5
BOUND_MAX = 40.0
NORM_SLACK = 1.05
CLAMP = 60.0


def start_holds(ready, count=16):
    def hold(eng, s, value):
        if isinstance(value, int):
            if value > 0:
                eng.wait_ge(s, value)
            return
        eng.compute_val(value)
        eng.wait_ge(ready, count)
        eng.wait_ge(s, value)
    return hold


def project(nc, io, scr, keep):
    with ExitStack() as ctx:
        def sb(name, shape, dt):
            return ctx.enter_context(nc.sbuf_tensor(name, shape, dt))

        def ps(name, shape, dt):
            return ctx.enter_context(nc.psum_tensor(name, shape, dt))

        sem = nc.alloc_semaphore

        wk, wv, wq = (sb(n, [P, KT, D], F32) for n in ("wk", "wv", "wq"))
        scale_b, bias_b, bv_b = (sb(n, [P, D], F32) for n in ("ln1_scale_b", "ln1_bias_b", "bv_b"))
        bk_col, bq_col, bqs_col = (sb(n, [P, PAIRS], F32) for n in ("bk_col", "bq_col", "bqs_col"))
        nm_i = sb("nodemask_i", [P, ST], I32)
        nm = sb("nodemask_f", [P, ST], F32)
        ident = sb("ident", [P, P], F32)
        ident_h = sb("ident_h", [P, P], BF16)
        halves = sb("halves", [P, P], BF16)
        minus_half = sb("minus_half", [P, QT], F32)
        eps_t = sb("eps", [P, QT], F32)
        xin = [sb(f"xin{s}", [P, QT, D], F32) for s in range(2)]
        z = [sb(f"z{s}", [P, QT, D], F32) for s in range(2)]
        zt = [sb(f"zt{s}", [P, KT, CH], F32) for s in range(2)]
        stats = sb("stats", [P, 2, QT, 6], F32)
        mv = sb("mv", [P, 2, QT, 2], F32)
        var_e = sb("var_e", [P, 2, QT], F32)
        rstd = sb("rstd", [P, 2, QT], F32)
        rstd_m = sb("rstd_m", [P, 2, QT], F32)
        adj = sb("adj_rows", [P, 2, N], I32)
        edge = sb("edge", [P, 2, N], BF16)
        edge_any = sb("edge_any", [P, QT], F32)
        lone = sb("lone", [P, QT], F32)
        edge_t = sb("edge_t", [P, ST, CH], U8)
        kq = sb("kq", [P, 2, CH], F32)
        kq_hi = sb("kq_hi", [P, 2, CH], F32R)
        kq_lo = sb("kq_lo", [P, 2, CH], F32R)
        kq_sq = sb("kq_sq", [P, 2, CH], BF16)
        norm_max = sb("norm_max", [P, 2, 1], F32)
        norm_new = sb("norm_new", [P, 2], F32)
        vv = sb("vv", [P, 2, D], F32)
        v_sum = sb("v_sum", [P, D], F32)
        bnd = sb("bnd", [P, 4], F32)
        all_max = sb("all_max", [P, 2], F32)

        turn_ps = ps("turn_ps", [P, 2, KT, P], F32)
        proj_ps = ps("proj_ps", [P, 2, CH], F32)
        edge_ps = ps("edge_ps", [P, 2, 8, P], BF16)
        norm_ps = ps("norm_ps", [P, CH], F32)

        consts_in = sem("consts_in")
        x_in = [sem(f"x_in{s}") for s in range(2)]
        adj_in = [sem(f"adj_in{b}") for b in range(2)]
        ident_ok, ident_zero = sem("ident_ok"), sem("ident_zero")
        consts_ok, halves_ok = sem("consts_ok"), sem("halves_ok")
        stats_ok, mv_ok, var_ok, rstd_ok, z_step, z_ok = (sem(n) for n in (
            "stats_ok", "mv_ok", "var_ok", "rstd_ok", "z_step", "z_ok"))
        turned, zt_ok = sem("turned"), sem("zt_ok")
        proj_ok, kq_ok, v_ok, lo_ok = sem("proj_ok"), sem("kq_ok"), sem("v_ok"), sem("lo_ok")
        norm_ok, norm_read, norm_max_ok = sem("norm_ok"), sem("norm_read"), sem("norm_max_ok")
        sq_ok = sem("sq_ok")
        kq_out = [sem(f"kq_out{b}") for b in range(2)]
        v_out = [sem(f"v_out{b}") for b in range(2)]
        v_sum_ok = sem("v_sum_ok")
        ht_out = sem("ht_out")
        edge_ok, lone_ok, edge_turned, edge_t_ok, edge_out, lone_out = (sem(n) for n in (
            "edge_ok", "lone_ok", "edge_turned", "edge_t_ok", "edge_out", "lone_out"))
        v_sum_out = sem("v_sum_out")
        bnd_ok, red_ok, pool_ok = sem("bnd_ok"), sem("red_ok"), sem("pool_ok")

        x_rows = [io["x"].rearrange("(c q p) d -> c p q d", p=P, q=QT),
                  io["h_target"].rearrange("(c q p) d -> c p q d", p=P, q=QT)]
        adj_rows = io["adj"].rearrange("(b p) s -> b p s", p=P)
        ht_rows = scr["ht"].rearrange("(c q p) d -> c p q d", p=P, q=QT)
        v_rows = scr["v"].rearrange("(b p) d -> b p d", p=P)
        lone_rows = scr["lone"].rearrange("(c q p) -> c p q", p=P, q=QT)
        n_consts = 10

        def wait(eng, s, value):
            if not isinstance(value, int) or value > 0:
                eng.wait_ge(s, value)

        def over_chunks(eng, body):
            body(0)
            with eng.Fori(1, NC - 1) as c:
                body(c)
            body(NC - 1)

        block = ctx.enter_context(nc.Block())
        hold = start_holds(x_in[0])

        @block.sync
        def _(sp):
            def load_x(c, s):
                sp.dma_start(xin[s][:], x_rows[s][c]).then_inc(x_in[s], 16)

            def load_adj(b, slot):
                sp.dma_start(adj[:, slot, :], adj_rows[b]).then_inc(adj_in[slot], 16)

            load_x(0, 0)
            sp.dma_start(scale_b[:], io["ln1_scale"].partition_broadcast(P)).then_inc(consts_in, 16)
            sp.dma_start(bias_b[:], io["ln1_bias"].partition_broadcast(P)).then_inc(consts_in, 16)
            sp.dma_start(nm_i[:], io["nodemask"].rearrange("(t p) -> p t", p=P), allow_slow_non_contiguous=True).then_inc(consts_in, 16)
            sp.dma_start(bk_col[:], io["bk"].rearrange("(m p) -> p m", p=P), allow_slow_non_contiguous=True).then_inc(consts_in, 16)
            sp.dma_start(bq_col[:], io["bq"].rearrange("(m p) -> p m", p=P), allow_slow_non_contiguous=True).then_inc(consts_in, 16)
            sp.dma_start(bv_b[:], io["bv"].partition_broadcast(P)).then_inc(consts_in, 16)
            for t, w in ((wk, "Wk"), (wv, "Wv"), (wq, "Wq")):
                sp.dma_start(t[:], io[w].rearrange("(k p) n -> p k n", p=P)).then_inc(consts_in, 16)
            load_x(0, 1)
            load_adj(0, 0)
            load_adj(1, 1)

            def store_kq(c, i, side):
                b, m = i % 2, i % PAIRS
                hi, lo = (scr["k_hi"], scr["k_lo"]) if side == 0 else (scr["q_hi"], scr["q_lo"])
                hold(sp, lo_ok, 8 * c + i + 1)
                cols = bass.ts(c, CH)
                sp.dma_start(hi[m * P:(m + 1) * P, cols], kq_hi[:, b, :].bitcast(F32)).then_inc(kq_out[b], 16)
                sp.dma_start(lo[m * P:(m + 1) * P, cols], kq_lo[:, b, :].bitcast(F32)).then_inc(kq_out[b], 16)

            def body(c):
                more = not (isinstance(c, int) and c == NC - 1)
                if more:
                    hold(sp, z_ok, 8 * c + 4)
                    load_x(c + 1, 0)
                hold(sp, edge_ok, 4 * c + 1)
                load_adj(4 * c + 2, 0)
                for i in range(4):
                    store_kq(c, i, 0)
                hold(sp, edge_ok, 4 * c + 2)
                load_adj(4 * c + 3, 1)
                for q in range(QT):
                    hold(sp, v_ok, 4 * c + q + 1)
                    sp.dma_start(v_rows[4 * c + q], vv[:, q % 2, :]).then_inc(v_out[q % 2], 16)
                hold(sp, z_ok, 8 * c + 8)
                if more:
                    load_x(c + 1, 1)
                sp.dma_start(ht_rows[c], z[1][:]).then_inc(ht_out, 16)
                for i in range(4, 8):
                    store_kq(c, i, 1)
                if more:
                    hold(sp, edge_ok, 4 * c + 3)
                    load_adj(4 * c + 4, 0)
                hold(sp, edge_t_ok, 16 * c + 16)
                sp.dma_start(scr["edge_t"][c], edge_t[:]).then_inc(edge_out, 16)
                hold(sp, lone_ok, c + 1)
                sp.dma_start(lone_rows[c], lone[:], allow_slow_non_contiguous=True).then_inc(lone_out, 16)
                if more:
                    hold(sp, edge_ok, 4 * c + 4)
                    load_adj(4 * c + 5, 1)

            over_chunks(sp, body)
            hold(sp, v_sum_ok, N // P)
            sp.dma_start(scr["v_sum"], v_sum[:]).then_inc(v_sum_out, 16)
            for b in range(2):
                hold(sp, kq_out[b], 2 * 16 * 4 * NC)
                hold(sp, v_out[b], 16 * 2 * NC)
            for s in (ht_out, edge_out, lone_out):
                hold(sp, s, 16 * NC)
            hold(sp, v_sum_out, 16)

        @block.gpsimd
        def _(pool):
            for t in (ident, ident_h):
                pool.memset(t[:], 0.0).then_inc(ident_zero, 1)
            pool.memset(minus_half[:], -0.5).then_inc(ident_zero, 1)
            pool.memset(eps_t[:], EPS).then_inc(ident_zero, 1)
            pool.memset(v_sum[:], 0.0).then_inc(ident_zero, 1)
            pool.wait_ge(ident_zero, 5)
            for t in (ident, ident_h):
                pool.affine_select(out=t[:], in_=t[:], compare_op=ALU.not_equal, fill=1.0, base=0,
                                   pattern=[[-1, P]], channel_multiplier=1).then_inc(ident_ok, 1)

            def body(c):
                for s in range(2):
                    pool.wait_ge(mv_ok, 8 * c + 4 * s + 4)
                    pool.tensor_tensor(var_e[:, s, :], mv[:, s, :, 1], eps_t[:], ALU.add).then_inc(var_ok, 1)
                    pool.wait_ge(var_ok, 2 * c + s + 1)
                    pool.tensor_tensor(rstd[:, s, :], var_e[:, s, :], minus_half[:], ALU.pow).then_inc(rstd_ok, 1)
                    if s == 0:
                        continue
                    for q in range(QT):
                        pool.wait_ge(v_ok, 4 * c + q + 1)
                        wait(pool, v_sum_ok, 4 * c + q)
                        pool.tensor_tensor(v_sum[:], v_sum[:], vv[:, q % 2, :], ALU.add).then_inc(v_sum_ok, 1)

            over_chunks(pool, body)
            pool.wait_ge(norm_max_ok, 8 * NC)
            for s in range(2):
                pool.partition_all_reduce(all_max[:, s:s + 1], norm_max[:, s, :], P, RMAX).then_inc(pool_ok, 1)

        @block.scalar
        def _(act):
            def body(c):
                def turned_rows(s):
                    for q in range(QT):
                        n = 4 * s + q
                        act.wait_ge(turned, 8 * c + n + 1)
                        if q == 0:
                            wait(act, proj_ok, 12 * (c - 1) + (8 if s == 0 else 12))
                        act.copy(zt[s][:, :, q * P:(q + 1) * P], turn_ps[:, n % 2, :, :]).then_inc(zt_ok, 1)

                def keys_or_queries(s):
                    for m in range(PAIRS):
                        i = 4 * s + m
                        b = i % 2
                        act.wait_ge(proj_ok, 12 * c + (m if s == 0 else 8 + m) + 1)
                        wait(act, kq_out[b], 32 * (4 * c + i // 2))
                        bias = bk_col[:, m:m + 1] if s == 0 else bqs_col[:, m:m + 1]
                        scale = 1.0 if s == 0 else QSCALE
                        act.activation(kq[:, b, :], proj_ps[:, i % 2, :], ACT.Identity, bias=bias, scale=scale)
                        act.activation(kq_hi[:, b, :], proj_ps[:, i % 2, :], ACT.Identity, bias=bias,
                                       scale=scale).then_inc(kq_ok, 1)

                def mask_tiles(k):
                    for g in range(4):
                        n = 4 * k + g
                        act.wait_ge(edge_turned, 16 * c + n + 1)
                        if n == 0:
                            wait(act, edge_out, 16 * c)
                        act.copy(edge_t[:, 8 * g:8 * g + 8, k * P:(k + 1) * P],
                                 edge_ps[:, n % 2, :, :]).then_inc(edge_t_ok, 1)

                turned_rows(0)
                mask_tiles(0)
                keys_or_queries(0)
                mask_tiles(1)
                turned_rows(1)
                mask_tiles(2)
                keys_or_queries(1)
                mask_tiles(3)

            act.wait_ge(consts_ok, 1)
            over_chunks(act, body)
            act.wait_ge(bnd_ok, 1)
            act.activation(bnd[:, 1:2], bnd[:, 0:1], ACT.Sqrt).then_inc(red_ok, 1)

        @block.vector
        def _(dve):
            dve.memset(halves[:], 0.0).then_inc(halves_ok, 1)
            dve.wait_ge(halves_ok, 1)
            dve.memset(halves[0:HD, 0:HD], 1.0).then_inc(halves_ok, 1)
            dve.memset(halves[HD:P, HD:P], 1.0).then_inc(halves_ok, 1)
            dve.wait_ge(consts_in, 16 * 9)
            dve.tensor_scalar(nm[:], nm_i[:], 1, None, ALU.is_equal)
            dve.memset(norm_max[:], 0.0)
            dve.tensor_scalar(bqs_col[:], bq_col[:], QSCALE, None, ALU.mult).then_inc(consts_ok, 1)
            dve.wait_ge(consts_ok, 1)

            def body(c):
                def layer_norm(s):
                    dve.wait_ge(x_in[s], 16 * (c + 1))
                    for q in range(QT):
                        dve.bn_stats(stats[:, s, q, :], xin[s][:, q, :]).then_inc(stats_ok, 1)
                    for q in range(QT):
                        count = 8 * c + 4 * s + q + 1
                        dve.compute_val(count)
                        dve.wait_ge(consts_ok, 1)
                        dve.wait_ge(stats_ok, count)
                        dve.bn_aggr(mv[:, s, q, :], stats[:, s, q, :]).then_inc(mv_ok, 1)

                def scale_rows(s):
                    dve.wait_ge(rstd_ok, 2 * c + s + 1)
                    dve.tensor_tensor(rstd_m[:, s, :], rstd[:, s, :],
                                      nm[:, bass.ts(c, QT)], ALU.mult).then_inc(z_step, 1)
                    wait(dve, turned, 8 * (c - 1) + 4 * s + 4)
                    if s == 1:
                        wait(dve, ht_out, 16 * c)
                    dve.wait_ge(z_step, 18 * c + 9 * s + 1)
                    for q in range(QT):
                        dve.tensor_scalar(z[s][:, q, :], xin[s][:, q, :], mv[:, s, q, 0:1],
                                          rstd_m[:, s, q:q + 1], ALU.subtract, ALU.mult).then_inc(z_step, 1)
                    for q in range(QT):
                        dve.wait_ge(z_step, 18 * c + 9 * s + 2 + q)
                        dve.tensor_tensor(z[s][:, q, :], z[s][:, q, :], scale_b[:], ALU.mult).then_inc(z_step, 1)
                    for q in range(QT):
                        dve.wait_ge(z_step, 18 * c + 9 * s + 6 + q)
                        dve.scalar_tensor_tensor(z[s][:, q, :], bias_b[:], nm[:, bass.ds(c * QT + q, 1)],
                                                 z[s][:, q, :], ALU.mult, ALU.add).then_inc(z_ok, 1)

                def edges(k):
                    b = k % 2
                    dve.wait_ge(adj_in[b], 16 * (2 * c + k // 2 + 1))
                    wait(dve, edge_turned, 4 * (4 * c + k - 1))
                    if k == 0:
                        wait(dve, lone_ok, c)
                    dve.tensor_scalar(edge[:, b, :], adj[:, b, :], 0, 0.0, ALU.not_equal, ALU.max,
                                      accum_out=edge_any[:, k:k + 1]).then_inc(edge_ok, 1)

                def split(s, m):
                    i = 4 * s + m
                    b = i % 2
                    dve.wait_ge(kq_ok, 8 * c + i + 1)
                    dve.tensor_tensor(kq_lo[:, b, :], kq[:, b, :], kq_hi[:, b, :].bitcast(F32),
                                      ALU.subtract).then_inc(lo_ok, 1)
                    wait(dve, norm_ok, 8 * c + i - 1)
                    dve.tensor_tensor(kq_sq[:, b, :], kq[:, b, :], kq[:, b, :], ALU.mult).then_inc(sq_ok, 1)
                    if i > 0 or not isinstance(c, int) or c > 0:
                        fold_norm(8 * c + i - 1, 0 if 1 <= i <= 4 else 1)

                def fold_norm(n, which):
                    dve.wait_ge(norm_ok, n + 1)
                    wait(dve, norm_max_ok, n)
                    dve.reduce_max(norm_new[:, which:which + 1], norm_ps[:], AX_X).then_inc(norm_read, 1)
                    dve.wait_ge(norm_read, n + 1)
                    dve.tensor_tensor(norm_max[:, which, :], norm_max[:, which, :],
                                      norm_new[:, which:which + 1], ALU.max).then_inc(norm_max_ok, 1)

                layer_norm(0)
                edges(0)
                scale_rows(0)
                layer_norm(1)
                edges(1)
                for m in range(PAIRS):
                    split(0, m)
                scale_rows(1)
                for q in range(QT):
                    n = 4 + q
                    dve.wait_ge(proj_ok, 12 * c + n + 1)
                    wait(dve, v_out[q % 2], 16 * (2 * c + q // 2))
                    wait(dve, v_sum_ok, 4 * c + q - 1)
                    dve.tensor_tensor(vv[:, q % 2, :], proj_ps[:, n % 2, :], bv_b[:], ALU.add).then_inc(v_ok, 1)
                edges(2)
                for m in range(PAIRS):
                    split(1, m)
                edges(3)
                dve.wait_ge(edge_ok, 4 * c + 4)
                wait(dve, lone_out, 16 * c)
                dve.tensor_scalar(lone[:], edge_any[:], -1.0, 1.0, ALU.mult, ALU.add).then_inc(lone_ok, 1)
                if isinstance(c, int) and c == NC - 1:
                    fold_norm(8 * c + 7, 1)

            over_chunks(dve, body)
            dve.wait_ge(pool_ok, 2)
            dve.tensor_tensor(bnd[:, 0:1], all_max[:, 0:1], all_max[:, 1:2], ALU.mult).then_inc(bnd_ok, 1)
            dve.wait_ge(red_ok, 1)
            dve.tensor_scalar(keep["minus_bound"][:], bnd[:, 1:2], -NORM_SLACK, None, ALU.mult).then_inc(bnd_ok, 1)
            dve.wait_ge(bnd_ok, 2)
            dve.tensor_scalar(keep["bounded_f"][:], keep["minus_bound"][0:1, 0:1], -BOUND_MAX, None,
                              ALU.is_ge).then_inc(bnd_ok, 1)
            dve.wait_ge(bnd_ok, 3)
            dve.tensor_copy(keep["bounded_i"][:], keep["bounded_f"][:]).then_inc(bnd_ok, 1)
            dve.wait_ge(bnd_ok, 4)

        @block.tensor
        def _(pe):
            def body(c):
                def turn(s):
                    for q in range(QT):
                        n = 4 * s + q
                        pe.wait_ge(z_ok, 8 * c + n + 1)
                        wait(pe, zt_ok, 8 * c + n - 1)
                        for k in range(KT):
                            last = pe.transpose(turn_ps[:, n % 2, k, :], z[s][:, q, k * P:(k + 1) * P], ident[:])
                        last.then_inc(turned, 1)

                def keys_or_queries(s, w):
                    pe.wait_ge(zt_ok, 8 * c + 4 * s + 4)
                    for m in range(PAIRS):
                        if s == 0:
                            wait(pe, kq_ok, 8 * c + m - 1)
                        elif m < 2:
                            wait(pe, v_ok, 4 * c + 3 + m)
                        else:
                            wait(pe, kq_ok, 8 * c + 3 + m)
                        for k in range(KT):
                            last = pe.matmul(proj_ps[:, m % 2, :], w[:, k, m * P:(m + 1) * P], zt[s][:, k, :],
                                             start=(k == 0), stop=(k == KT - 1))
                        last.then_inc(proj_ok, 1)
                        i = 4 * s + m
                        if i > 0 or not isinstance(c, int) or c > 0:
                            norms(8 * c + i - 1, (i - 1) % 2)

                def norms(n, b):
                    pe.wait_ge(sq_ok, n + 1)
                    wait(pe, norm_read, n)
                    pe.matmul(norm_ps[:], halves[:], kq_sq[:, b, :], start=True, stop=True).then_inc(norm_ok, 1)

                def values():
                    for q in range(QT):
                        if q < 2:
                            wait(pe, kq_ok, 8 * c + 3 + q)
                        else:
                            wait(pe, v_ok, 4 * c + q - 1)
                        for k in range(KT):
                            last = pe.matmul(proj_ps[:, q % 2, :], zt[0][:, k, q * P:(q + 1) * P], wv[:, k, :],
                                             start=(k == 0), stop=(k == KT - 1))
                        last.then_inc(proj_ok, 1)

                def turn_edges(k):
                    pe.wait_ge(edge_ok, 4 * c + k + 1)
                    for g in range(4):
                        n = 4 * k + g
                        wait(pe, edge_t_ok, 16 * c + n - 1)
                        for t in range(8):
                            at = (8 * g + t) * P
                            last = pe.transpose(edge_ps[:, n % 2, t, :], edge[:, k % 2, at:at + P], ident_h[:])
                        last.then_inc(edge_turned, 1)

                turn(0)
                turn_edges(0)
                keys_or_queries(0, wk)
                turn_edges(1)
                values()
                turn(1)
                turn_edges(2)
                keys_or_queries(1, wq)
                turn_edges(3)
                if isinstance(c, int) and c == NC - 1:
                    norms(8 * c + 7, 1)

            pe.wait_ge(ident_ok, 2)
            pe.wait_ge(halves_ok, 3)
            pe.wait_ge(consts_in, 16 * 9)
            over_chunks(pe, body)


LAG = 3
PR = 8
GR = 4


def attend(nc, io, scr, keep):
    STEPS = PAIRS * NC
    with ExitStack() as ctx:
        def sb(name, shape, dt):
            return ctx.enter_context(nc.sbuf_tensor(name, shape, dt))

        def ps(name, shape, dt):
            return ctx.enter_context(nc.psum_tensor(name, shape, dt))

        sem = nc.alloc_semaphore

        k_st = sb("k_stack", [P, 2, N], F32R)
        v_sb = sb("v_pair", [P, ST, P], F32)
        q_a = sb("q_hi_lo", [P, 2, 2, CH], F32R)
        q_b = sb("q_lo_hi", [P, 2, 2, CH], F32R)
        edge = sb("edge_st", [P, 2, ST, CH], U8)
        lone = sb("lone_b", [P, 2, CH], F32)
        v_sum = sb("v_sum_pair", [P, 2, P], F32)
        prob = sb("prob", [P, PR, 2, CH], F32)
        psum2 = sb("prob_sums", [P, GR, 2, CH], F32)
        den_sb = sb("den_sb", [P, CH], F32)
        out_sb = sb("out_sb", [P, CH], F32)
        rden = sb("rden", [P, CH], F32)
        ctx_sb = sb("ctx_sb", [P, CH], F32)
        ones = sb("ones32", [P, 32], F32)
        c32 = sb("c32", [P, 32], F32)
        pick = sb("pick", [P, P], F32)

        ones_sq = sb("ones_sq", [P, P], F32)
        spread = sb("spread", [P, P], F32R)
        shift = sb("shift", [P, 2, CH], F32R)
        part_max = sb("part_max", [P, N // CH], F32)
        top = sb("top", [P, 2, QT], F32)
        minus_max = sb("minus_max", [P, 2, QT], F32)
        adj_rows = prob[:, PR // 2:PR].rearrange("p a b c -> p (a b c)").bitcast(I32)
        bias = edge[:, 1].rearrange("p a b -> p (a b)").bitcast(F32)

        sc = ps("scores", [P, 3, 2, CH], F32)
        po = ps("pv", [P, CH], F32)
        pl = ps("den", [P, CH], F32)

        consts_ok, pick_ok = sem("a_consts_ok"), sem("pick_ok")
        k_in = [sem(f"k_in{i}") for i in range(4)]
        v_in = [sem(f"v_in{i}") for i in range(4)]
        q_in = [sem(f"q_in{b}") for b in range(2)]
        edge_in = [sem(f"edge_in{b}") for b in range(2)]
        lone_in = [sem(f"lone_in{b}") for b in range(2)]
        scores_ok, exp_ok, masked_ok, sums_ok, pv_ok, den_ok = (sem(n) for n in (
            "scores_ok", "exp_ok", "masked_ok", "sums_ok", "pv_ok", "den_ok"))
        step_ok, den_copied, out_copied, den_whole, rden_ok, ctx_ok, ctx_out = (sem(n) for n in (
            "step_ok", "den_copied", "out_copied", "den_whole", "rden_ok", "ctx_ok", "ctx_out"))

        cf = {n: sem(n) for n in (
            "cf_in", "cf_adj", "cf_rough", "cf_minus", "shift_out", "shift_in", "cf_shift", "cf_scores", "cf_exp",
            "cf_masked", "cf_step", "cf_den_sb", "cf_taken", "cf_den", "cf_rden", "cf_out", "pre_bias", "pre_added",
            "pre_max", "pre_top", "pre_clamped", "pre_pv", "pre_ctx")}
        (cf_in, cf_adj, cf_rough, cf_minus, shift_out, shift_in, cf_shift, cf_scores, cf_exp, cf_masked, cf_step,
         cf_den_sb, cf_taken, cf_den, cf_rden, cf_out, pre_bias, pre_added, pre_max, pre_top, pre_clamped, pre_pv,
         pre_ctx) = cf.values()

        qk = {n: scr[n].rearrange("(m h d) t -> m d h t", m=PAIRS, h=2) for n in ("k_hi", "k_lo", "q_hi", "q_lo")}
        v_rows = scr["v"].rearrange("(t p) (m c) -> m p t c", p=P, m=PAIRS)
        v_sums = scr["v_sum"].rearrange("p (m c) -> m p c", m=PAIRS)
        ctx_rows = scr["ctx"].rearrange("(m p) t -> m p t", p=P)
        lone_row = scr["lone"].rearrange("(c t) -> c t", t=CH)
        adj_blocks = io["adj"].rearrange("(b p) s -> b p s", p=P)
        shift_row = scr["shift"].rearrange("h q p -> h (q p)")
        shift_cols = scr["shift"].rearrange("h q p -> p h q")

        def wait(eng, s, value):
            if not isinstance(value, int) or value > 0:
                eng.wait_ge(s, value)

        def over_steps(eng, body):
            body(0, 0)
            body(1, 1)
            with eng.Fori(1, STEPS // 2) as i:
                body(2 * i, 0)
                body(2 * i + 1, 1)

        hold = start_holds(k_in[0])

        def load_k(sp, m, i):
            cols = slice(i * N // 4, (i + 1) * N // 4)
            sp.dma_start(k_st[0:HD, :, cols].bitcast(F32), qk["k_hi"][m][:, :, cols]).then_inc(k_in[i], 16)
            sp.dma_start(k_st[HD:P, :, cols].bitcast(F32), qk["k_lo"][m][:, :, cols]).then_inc(k_in[i], 16)

        def load_v(sp, m, i):
            t = slice(i * ST // 4, (i + 1) * ST // 4)
            sp.dma_start(v_sb[:, t, :], v_rows[m][:, t, :]).then_inc(v_in[i], 16)

        def load_q(sp, m, c, b):
            cols = bass.ts(c, CH)
            for t, top, low in ((q_a, "q_hi", "q_lo"), (q_b, "q_lo", "q_hi")):
                sp.dma_start(t[0:HD, b].bitcast(F32), qk[top][m][:, :, cols]).then_inc(q_in[b], 16)
                sp.dma_start(t[HD:P, b].bitcast(F32), qk[low][m][:, :, cols]).then_inc(q_in[b], 16)

        def load_edge(sp, c, b):
            sp.dma_start(edge[:, b], scr["edge_t"][c]).then_inc(edge_in[b], 16)

        def load_lone(sp, m, c, b):
            sp.dma_start(lone[:, b, :], lone_row[c].partition_broadcast(P)).then_inc(lone_in[b], 16)
            sp.dma_start(v_sum[:, b, :], v_sums[m]).then_inc(lone_in[b], 16)

        def bounded_sync(sp):
            for i in range(4):
                load_k(sp, 0, i)
                if i == 0:
                    load_q(sp, 0, 0, 0)
                    load_edge(sp, 0, 0)
                load_v(sp, 0, i)
            load_lone(sp, 0, 0, 0)

            def step(m, c, b):
                s = NC * m + c
                first = isinstance(s, int) and s == 0
                last = isinstance(s, int) and s == STEPS - 1
                ends_pair = isinstance(c, int) and c == NC - 1
                if not last:
                    nm, ncn = (m + 1, 0) if ends_pair else (m, c + 1)
                    hold(sp, scores_ok, ST * s)
                    load_q(sp, nm, ncn, 1 - b)
                    hold(sp, masked_ok, ST * s)
                    load_edge(sp, ncn, 1 - b)
                    hold(sp, step_ok, s)
                    load_lone(sp, nm, ncn, 1 - b)
                if not first:
                    pm, pc = (m - 1, NC - 1) if isinstance(c, int) and c == 0 else (m, c - 1)
                    hold(sp, ctx_ok, s)
                    sp.dma_start(ctx_rows[pm][:, bass.ts(pc, CH)], ctx_sb[:]).then_inc(ctx_out, 16)
                if ends_pair and not last:
                    for i in range(4):
                        hold(sp, scores_ok, ST * s + 8 * (i + 1))
                        load_k(sp, m + 1, i)
                        hold(sp, pv_ok, ST * s + 8 * (i + 1))
                        load_v(sp, m + 1, i)

            def pair(m):
                step(m, 0, 0)
                step(m, 1, 1)
                with sp.Fori(1, NC // 2 - 1) as i:
                    step(m, 2 * i, 0)
                    step(m, 2 * i + 1, 1)
                step(m, NC - 2, 0)
                step(m, NC - 1, 1)

            pair(0)
            with sp.Fori(1, PAIRS - 1) as m:
                pair(m)
            pair(PAIRS - 1)
            hold(sp, ctx_ok, STEPS)
            sp.dma_start(ctx_rows[PAIRS - 1][:, (NC - 1) * CH:], ctx_sb[:]).then_inc(ctx_out, 16)
            hold(sp, ctx_out, 16 * STEPS)

        def bounded_tensor(pe):
            def pv(s, b, j):
                pe.wait_ge(masked_ok, ST * s + j + 1)
                if j % 8 == 0:
                    pe.wait_ge(v_in[j // 8], 16 * (s // NC + 1))
                if j == 0:
                    wait(pe, out_copied, s)
                for h in range(2):
                    last = pe.matmul(po[h * HD:(h + 1) * HD, :], v_sb[:, j, h * HD:(h + 1) * HD],
                                     prob[:, j % PR, h, :], start=(j == 0), stop=False)
                last.then_inc(pv_ok, 1)
                if j % 4 == 3:
                    g = j // 4
                    pe.wait_ge(sums_ok, ST // 2 * s + 2 * g + 2)
                    if g == 0:
                        wait(pe, rden_ok, s)
                    for i in range(4):
                        last = pe.matmul(pl[32 * i:32 * i + 32, :], ones[:], psum2[:, (2 * g + i // 2) % GR, i % 2, :],
                                         start=(g == 0), stop=(g == ST // 4 - 1 and i > 1))
                    last.then_inc(den_ok, 1)

            def lone_tile(s, b):
                pe.wait_ge(lone_in[b], 32 * (s // 2 + 1))
                for h in range(2):
                    pe.matmul(po[h * HD:(h + 1) * HD, :], v_sum[:, b, h * HD:(h + 1) * HD], lone[:, b, :],
                              start=False, stop=True)
                for h in range(2):
                    last = pe.matmul(pl[32 * h:32 * h + 32, :], c32[:], lone[:, b, :], start=False, stop=True)
                last.then_inc(step_ok, 1)

            def whole_den(s):
                pe.wait_ge(den_copied, s + 1)
                pe.matmul(pl[:], pick[:], den_sb[:], start=True, stop=True).then_inc(den_whole, 1)

            def body(s, b):
                first = isinstance(s, int) and s == 0
                for j in range(ST):
                    if j == 0:
                        pe.wait_ge(q_in[b], 64 * (s // 2 + 1))
                    if j % 8 == 0:
                        pe.wait_ge(k_in[j // 8], 32 * (s // NC + 1))
                    wait(pe, exp_ok, ST * s + (j - 2 if j >= 2 else j - 1))
                    for h in range(2):
                        k_tile = k_st[:, h, j * P:(j + 1) * P]
                        pe.matmul(sc[:, j % 3, h, :], k_tile, q_a[:, b, h, :], start=True, stop=False)
                        last = pe.matmul(sc[:, j % 3, h, :], k_tile, q_b[:, b, h, :], start=False, stop=True)
                    last.then_inc(scores_ok, 1)
                    if j >= LAG:
                        pv(s, b, j - LAG)
                    elif not first:
                        pv(s - 1, 1 - b, ST + j - LAG)
                        if j == LAG - 1:
                            lone_tile(s - 1, 1 - b)
                    if j == LAG + 1 and not first:
                        whole_den(s - 1)

            over_steps(pe, body)
            for j in range(ST - LAG, ST):
                pv(STEPS - 1, 1, j)
            lone_tile(STEPS - 1, 1)
            whole_den(STEPS - 1)

        def bounded_scalar(act):
            def take(s):
                act.wait_ge(step_ok, s + 1)
                wait(act, den_whole, s)
                act.copy(den_sb[:], pl[:]).then_inc(den_copied, 1)
                wait(act, ctx_ok, s)
                act.copy(out_sb[:], po[:]).then_inc(out_copied, 1)

            def body(s, b):
                first = isinstance(s, int) and s == 0
                for j in range(ST):
                    act.wait_ge(scores_ok, ST * s + j + 1)
                    wait(act, pv_ok, ST * s + j - PR + 1)
                    wait(act, sums_ok, ST // 2 * s + (j - PR) // 2 + 1)
                    act.activation(prob[:, j % PR], sc[:, j % 3], ACT.Exp,
                                   bias=keep["minus_bound"][:, 0:1]).then_inc(exp_ok, 1)
                    if j == LAG - 1 and not first:
                        take(s - 1)

            over_steps(act, body)
            take(STEPS - 1)

        def bounded_vector(dve):
            def finish(s):
                dve.wait_ge(den_whole, s + 1)
                dve.reciprocal(rden[:], pl[:]).then_inc(rden_ok, 1)
                dve.wait_ge(rden_ok, s + 1)
                dve.wait_ge(out_copied, s + 1)
                wait(dve, ctx_out, 16 * s)
                dve.tensor_tensor(ctx_sb[:], out_sb[:], rden[:], ALU.mult).then_inc(ctx_ok, 1)

            def body(s, b):
                first = isinstance(s, int) and s == 0
                dve.wait_ge(edge_in[b], 16 * (s // 2 + 1))
                for j in range(ST):
                    dve.wait_ge(exp_ok, ST * s + j + 1)
                    dve.tensor_tensor(prob[:, j % PR], prob[:, j % PR],
                                      edge[:, b, j, :].unsqueeze(1).broadcast_to([P, 2, CH]),
                                      ALU.mult).then_inc(masked_ok, 1)
                    if j % 2 == 1:
                        r = j // 2
                        dve.wait_ge(masked_ok, ST * s + j + 1)
                        wait(dve, den_ok, ST // 4 * s + (r - GR) // 2 + 1)
                        dve.tensor_tensor(psum2[:, r % GR], prob[:, (j - 1) % PR], prob[:, j % PR],
                                          ALU.add).then_inc(sums_ok, 1)
                    if j == LAG + 2 and not first:
                        finish(s - 1)

            over_steps(dve, body)
            finish(STEPS - 1)

        hold_cf = start_holds(pick_ok, 1)

        def careful_sync(sp):
            with sp.Fori(0, PAIRS) as m:
                with sp.Fori(0, NC) as c:
                    s = NC * m + c
                    for half, part in ((slice(0, HD), "k_hi"), (slice(HD, P), "k_lo")):
                        sp.dma_start(k_st[half].bitcast(F32), qk[part][m]).then_inc(cf_in, 16)
                    for t, top, low in ((q_a, "q_hi", "q_lo"), (q_b, "q_lo", "q_hi")):
                        for half, part in ((slice(0, HD), top), (slice(HD, P), low)):
                            sp.dma_start(t[half, 0].bitcast(F32),
                                         qk[part][m][:, :, bass.ts(c, CH)]).then_inc(cf_in, 16)
                    sp.dma_start(v_sb[:], v_rows[m]).then_inc(cf_in, 16)
                    sp.dma_start(edge[:, 0], scr["edge_t"][c]).then_inc(cf_in, 16)
                    sp.dma_start(lone[:, 0, :], lone_row[c].partition_broadcast(P)).then_inc(cf_in, 16)
                    sp.dma_start(v_sum[:, 0, :], v_sums[m]).then_inc(cf_in, 16)
                    for q in range(QT):
                        hold_cf(sp, pre_bias, QT * s + q + 1)
                        sp.dma_start(adj_rows, adj_blocks[QT * c + q]).then_inc(cf_adj, 16)
                    hold_cf(sp, cf_minus, s + 1)
                    sp.dma_start(shift_cols, minus_max[:], allow_slow_non_contiguous=True).then_inc(shift_out, 16)
                    hold_cf(sp, shift_out, 16 * s + 16)
                    sp.dma_start(psum2[:, 0], shift_row.partition_broadcast(P)).then_inc(shift_in, 16)
                    hold_cf(sp, pre_ctx, s + 2)
                    sp.dma_start(ctx_rows[m][:, bass.ts(c, CH)], ctx_sb[:]).then_inc(cf_out, 16)
                    hold_cf(sp, cf_out, 16 * s + 16)

        def careful_tensor(pe):
            with pe.Fori(0, STEPS) as s:
                pe.wait_ge(cf_in, 160 * s + 160)
                for q in range(QT):
                    for h in range(2):
                        for n in range(N // CH):
                            at = (2 * q + h) * (N // CH) + n
                            pe.wait_ge(pre_added, 64 * s + at + 1)
                            pe.matmul(sc[:, n % 2, 0, :], q_a[:, 0, h, q * P:(q + 1) * P],
                                      k_st[:, h, n * CH:(n + 1) * CH], start=True, stop=True).then_inc(cf_rough, 1)
                pe.wait_ge(cf_shift, s + 1)
                for j in range(ST):
                    pe.wait_ge(pre_clamped, ST * s + j + 1)
                    for h in range(2):
                        k_tile = k_st[:, h, j * P:(j + 1) * P]
                        pe.matmul(sc[:, 2, h, :], k_tile, q_a[:, 0, h, :], start=True, stop=False)
                        pe.matmul(sc[:, 2, h, :], k_tile, q_b[:, 0, h, :], start=False, stop=False)
                        last = pe.matmul(sc[:, 2, h, :], spread[:], shift[:, h, :], start=False, stop=True)
                    last.then_inc(cf_scores, 1)
                    pe.wait_ge(cf_masked, ST * s + j + 1)
                    for h in range(2):
                        i = h + 2 * (j % 2)
                        pe.matmul(po[h * HD:(h + 1) * HD, :], v_sb[:, j, h * HD:(h + 1) * HD], prob[:, 0, h, :],
                                  start=(j == 0), stop=False)
                        last = pe.matmul(pl[32 * i:32 * i + 32, :], ones[:], prob[:, 0, h, :],
                                         start=(j < 2), stop=(j == ST - 1))
                    last.then_inc(pre_pv, 1)
                for h in range(2):
                    pe.matmul(po[h * HD:(h + 1) * HD, :], v_sum[:, 0, h * HD:(h + 1) * HD], lone[:, 0, :],
                              start=False, stop=True)
                    last = pe.matmul(pl[32 * h:32 * h + 32, :], c32[:], lone[:, 0, :], start=False, stop=True)
                last.then_inc(cf_step, 1)
                pe.wait_ge(cf_taken, s + 1)
                pe.matmul(pl[:], pick[:], den_sb[:], start=True, stop=True).then_inc(cf_den, 1)

        def careful_scalar(act):
            with act.Fori(0, STEPS) as s:
                for j in range(ST):
                    act.wait_ge(pre_clamped, ST * s + j + 2)
                    act.activation(prob[:, 0], prob[:, 0], ACT.Exp).then_inc(cf_exp, 1)
                act.wait_ge(cf_step, s + 1)
                act.copy(den_sb[:], pl[:]).then_inc(cf_den_sb, 1)
                act.copy(out_sb[:], po[:]).then_inc(cf_taken, 1)

        def careful_vector(dve):
            for t, count in ((pre_bias, 1), (pre_added, 2), (pre_max, 1), (pre_top, 1), (pre_clamped, 1), (pre_pv, 1),
                             (pre_ctx, 1)):
                dve.sem_inc(t, count)
            with dve.Fori(0, STEPS) as s:
                for q in range(QT):
                    dve.wait_ge(cf_adj, 16 * QT * s + 16 * q + 16)
                    dve.wait_ge(pre_added, 64 * s + 16 * q + 2)
                    dve.tensor_scalar(bias[:], adj_rows, 0, NEG, ALU.is_equal, ALU.mult).then_inc(pre_bias, 1)
                    dve.wait_ge(pre_bias, QT * s + q + 2)
                    for h in range(2):
                        i = 2 * q + h
                        for n in range(N // CH):
                            at = i * (N // CH) + n
                            dve.wait_ge(cf_rough, 64 * s + at + 1)
                            dve.wait_ge(pre_max, 64 * s + at + 1)
                            dve.tensor_tensor(psum2[:, 1, 0, :], sc[:, n % 2, 0, :], bias[:, n * CH:(n + 1) * CH],
                                              ALU.add).then_inc(pre_added, 1)
                            dve.wait_ge(pre_added, 64 * s + at + 3)
                            if n == 0:
                                dve.wait_ge(pre_top, 8 * s + i + 1)
                            dve.reduce_max(part_max[:, n:n + 1], psum2[:, 1, 0, :], AX_X).then_inc(pre_max, 1)
                        dve.wait_ge(pre_max, 64 * s + 8 * i + 9)
                        dve.reduce_max(top[:, h, q:q + 1], part_max[:], AX_X).then_inc(pre_top, 1)
                dve.wait_ge(pre_top, 8 * s + 9)
                dve.tensor_scalar(minus_max[:], top[:], -1.0, None, ALU.mult).then_inc(cf_minus, 1)
                dve.wait_ge(shift_in, 16 * s + 16)
                dve.tensor_copy(shift[:], psum2[:, 0]).then_inc(cf_shift, 1)
                for j in range(ST):
                    dve.wait_ge(cf_scores, ST * s + j + 1)
                    dve.wait_ge(pre_pv, ST * s + j + 1)
                    dve.tensor_scalar(prob[:, 0], sc[:, 2], CLAMP, None, ALU.min).then_inc(pre_clamped, 1)
                    dve.wait_ge(cf_exp, ST * s + j + 1)
                    dve.tensor_tensor(prob[:, 0], prob[:, 0],
                                      edge[:, 0, j, :].unsqueeze(1).broadcast_to([P, 2, CH]),
                                      ALU.mult).then_inc(cf_masked, 1)
                dve.wait_ge(cf_den, s + 1)
                dve.reciprocal(rden[:], pl[:]).then_inc(cf_rden, 1)
                dve.wait_ge(cf_rden, s + 1)
                dve.tensor_tensor(ctx_sb[:], out_sb[:], rden[:], ALU.mult).then_inc(pre_ctx, 1)

        def branch(eng, bounded, careful):
            flag = eng.value_load(keep["bounded_i"][0:1, 0:1], min_val=0, max_val=1)
            with eng.If(flag > 0):
                bounded(eng)
            with eng.Else():
                careful(eng)

        block = ctx.enter_context(nc.Block())

        @block.sync
        def _(sp):
            branch(sp, bounded_sync, careful_sync)

        @block.gpsimd
        def _(pool):
            pool.memset(ones[:], 1.0).then_inc(consts_ok, 1)
            pool.memset(c32[:], float(N // P)).then_inc(consts_ok, 1)

        @block.scalar
        def _(act):
            branch(act, bounded_scalar, careful_scalar)

        @block.vector
        def _(dve):
            dve.memset(ones_sq[:], 1.0 / P).then_inc(pick_ok, 1)
            dve.wait_ge(pick_ok, 1)
            dve.tensor_copy(spread[:], ones_sq[:]).then_inc(pick_ok, 1)
            dve.memset(pick[:], 0.0).then_inc(pick_ok, 1)
            dve.wait_ge(pick_ok, 3)
            for i in range(4):
                h = i % 2
                dve.memset(pick[32 * i:32 * i + 1, h * HD:(h + 1) * HD], 1.0).then_inc(pick_ok, 1)
            branch(dve, bounded_vector, careful_vector)

        @block.tensor
        def _(pe):
            pe.wait_ge(consts_ok, 2)
            pe.wait_ge(pick_ok, 7)
            branch(pe, bounded_tensor, careful_tensor)


def feed(nc, io, scr, keep):
    with ExitStack() as ctx:
        def sb(name, shape, dt):
            return ctx.enter_context(nc.sbuf_tensor(name, shape, dt))

        def ps(name, shape, dt):
            return ctx.enter_context(nc.psum_tensor(name, shape, dt))

        sem = nc.alloc_semaphore

        wo = sb("wo", [P, KT, D], F32)
        w1 = sb("w1", [P, KT, F], F32)
        w2 = sb("w2", [P, FT, D], F32)
        bo_b, scale_b, bias_b = (sb(n, [P, D], F32) for n in ("bo_b", "ln2_scale_b", "ln2_bias_b"))
        nm_i = sb("nodemask2_i", [P, ST], I32)
        nm = sb("nodemask2_f", [P, ST], F32)
        ident = sb("ident2", [P, P], F32)
        minus_half = sb("minus_half2", [P, QT], F32)
        eps_t = sb("eps2", [P, QT], F32)
        ctxt = sb("ctx_in", [P, KT, CH], F32)
        ht = sb("ht_in", [P, QT, D], F32)
        xr = sb("x_in", [P, QT, D], F32)
        h2 = sb("h2", [P, 2, QT, D], F32)
        h2t = sb("h2t", [P, KT, CH], F32)
        g = sb("gelu_t", [P, FT, CH], F32)
        y = sb("y", [P, QT, D], F32)
        stats = sb("stats2", [P, 2, QT, 6], F32)
        mv = sb("mv2", [P, 2, QT, 2], F32)
        var_e = sb("var_e2", [P, 2, QT], F32)
        rstd = sb("rstd2", [P, 2, QT], F32)
        rstd_m = sb("rstd_m2", [P, QT], F32)

        attn_ps = ps("attn_ps", [P, 2, D], F32)
        turn_ps = ps("turn2_ps", [P, 2, KT, P], F32)
        up_ps = ps("up_ps", [P, 2, CH], F32)
        down_ps = ps("down_ps", [P, 2, D], F32)

        consts_in, w1_in, w2_in = sem("f_consts_in"), sem("w1_in"), sem("w2_in")
        ctx_in, ht_in, xr_in = sem("ctx_in"), sem("ht_in"), sem("xr_in")
        ident_zero, ident_ok, consts_ok = sem("f_ident_zero"), sem("f_ident_ok"), sem("f_consts_ok")
        attn_ok, h1_step, h1_ok, h2_step, h2_ok = (sem(n) for n in ("attn_ok", "h1_step", "h1_ok", "h2_step", "h2_ok"))
        stats_ok, mv_ok, var_ok, rstd_ok = (sem("f_" + n) for n in ("stats_ok", "mv_ok", "var_ok", "rstd_ok"))
        turned, h2t_ok, up_ok, gelu_ok, down_ok = (sem(n) for n in ("f_turned", "h2t_ok", "up_ok", "gelu_ok", "down_ok"))
        y_step, y_ok, out_ok, out_done = (sem(n) for n in ("y_step", "y_ok", "out_ok", "out_done"))

        x_rows = io["x"].rearrange("(c q p) d -> c p q d", p=P, q=QT)
        ht_rows = scr["ht"].rearrange("(c q p) d -> c p q d", p=P, q=QT)
        out_rows = io["out"].rearrange("(c q p) d -> c p q d", p=P, q=QT)
        ctx_rows = scr["ctx"].rearrange("(k p) t -> p k t", p=P)

        def wait(eng, s, value):
            if not isinstance(value, int) or value > 0:
                eng.wait_ge(s, value)

        def is_last(c):
            return isinstance(c, int) and c == NC - 1

        def over_chunks(eng, body):
            body(0, 0)
            body(1, 1)
            with eng.Fori(1, NC // 2 - 1) as i:
                body(2 * i, 0)
                body(2 * i + 1, 1)
            body(NC - 2, 0)
            body(NC - 1, 1)

        def order_h1(c):
            return 0 if isinstance(c, int) and c == 0 else 2 * c - 1

        def order_y(c):
            return 2 * NC - 1 if is_last(c) else 2 * c + 2

        block = ctx.enter_context(nc.Block())
        hold = start_holds(ctx_in)

        @block.sync
        def _(sp):
            def load(c):
                sp.dma_start(ctxt[:], ctx_rows[:, :, bass.ts(c, CH)]).then_inc(ctx_in, 16)

            def load_ht(c):
                sp.dma_start(ht[:], ht_rows[c]).then_inc(ht_in, 16)

            load(0)
            sp.dma_start(wo[:], io["Wo"].rearrange("(k p) n -> p k n", p=P)).then_inc(consts_in, 16)
            load_ht(0)
            sp.dma_start(bo_b[:], io["bo"].partition_broadcast(P)).then_inc(consts_in, 16)
            sp.dma_start(scale_b[:], io["ln2_scale"].partition_broadcast(P)).then_inc(consts_in, 16)
            sp.dma_start(bias_b[:], io["ln2_bias"].partition_broadcast(P)).then_inc(consts_in, 16)
            sp.dma_start(nm_i[:], io["nodemask"].rearrange("(t p) -> p t", p=P), allow_slow_non_contiguous=True).then_inc(consts_in, 16)
            sp.dma_start(w1[:], io["W1"].rearrange("(k p) n -> p k n", p=P)).then_inc(w1_in, 16)
            sp.dma_start(w2[:], io["W2"].rearrange("(k p) n -> p k n", p=P)).then_inc(w2_in, 16)
            sp.dma_start(xr[:], x_rows[0]).then_inc(xr_in, 16)

            def body(c, b):
                if not is_last(c):
                    hold(sp, attn_ok, 4 * c + 4)
                    load(c + 1)
                    hold(sp, h1_ok, 4 * c + 4)
                    load_ht(c + 1)
                hold(sp, out_ok, 4 * c + 4)
                sp.dma_start(out_rows[c], y[:]).then_inc(out_done, 16)
                if not is_last(c):
                    load_x(c + 1)

            def load_x(c):
                sp.dma_start(xr[:], x_rows[c]).then_inc(xr_in, 16)

            over_chunks(sp, body)
            hold(sp, out_done, 16 * NC)

        @block.gpsimd
        def _(pool):
            pool.memset(ident[:], 0.0).then_inc(ident_zero, 1)
            pool.memset(minus_half[:], -0.5).then_inc(ident_zero, 1)
            pool.memset(eps_t[:], EPS).then_inc(ident_zero, 1)
            pool.wait_ge(ident_zero, 3)
            pool.affine_select(out=ident[:], in_=ident[:], compare_op=ALU.not_equal, fill=1.0, base=0,
                               pattern=[[-1, P]], channel_multiplier=1).then_inc(ident_ok, 1)

            def inverse_std(n, which):
                pool.wait_ge(mv_ok, 4 * n + 4)
                pool.tensor_tensor(var_e[:, which, :], mv[:, which, :, 1], eps_t[:], ALU.add).then_inc(var_ok, 1)
                pool.wait_ge(var_ok, n + 1)
                pool.tensor_tensor(rstd[:, which, :], var_e[:, which, :], minus_half[:], ALU.pow).then_inc(rstd_ok, 1)

            inverse_std(0, 0)

            def body(c, b):
                if not is_last(c):
                    inverse_std(order_h1(c + 1), 0)
                inverse_std(order_y(c), 1)

            over_chunks(pool, body)

        @block.scalar
        def _(act):
            def body(c, b):
                for q in range(QT):
                    act.wait_ge(turned, 4 * c + q + 1)
                    if q == 0:
                        wait(act, up_ok, FT * c)
                    act.copy(h2t[:, :, q * P:(q + 1) * P], turn_ps[:, q % 2, :, :]).then_inc(h2t_ok, 1)
                for f in range(FT):
                    act.wait_ge(up_ok, FT * c + f + 1)
                    if f == 0:
                        wait(act, down_ok, 4 * c)
                    act.activation(g[:, f, :], up_ps[:, f % 2, :], ACT.Gelu_apprx_tanh).then_inc(gelu_ok, 1)

            over_chunks(act, body)

        @block.vector
        def _(dve):
            dve.wait_ge(consts_in, 16 * 5)
            dve.tensor_scalar(nm[:], nm_i[:], 1, None, ALU.is_equal).then_inc(consts_ok, 1)
            dve.wait_ge(consts_ok, 1)

            def norm_h1(c, b):
                n = order_h1(c)
                dve.wait_ge(ht_in, 16 * (c + 1))
                for q in range(QT):
                    col = nm[:, bass.ds(c * QT + q, 1)]
                    dve.wait_ge(attn_ok, 4 * c + q + 1)
                    dve.tensor_tensor(h2[:, b, q, :], attn_ps[:, q % 2, :], bo_b[:], ALU.add).then_inc(h1_step, 1)
                    dve.wait_ge(h1_step, 4 * c + q + 1)
                    dve.scalar_tensor_tensor(h2[:, b, q, :], h2[:, b, q, :], col, ht[:, q, :],
                                             ALU.mult, ALU.add).then_inc(h1_ok, 1)
                for q in range(QT):
                    dve.wait_ge(h1_ok, 4 * c + q + 1)
                    dve.bn_stats(stats[:, 0, q, :], h2[:, b, q, :]).then_inc(stats_ok, 1)
                for q in range(QT):
                    count = 4 * n + q + 1
                    dve.compute_val(count)
                    dve.wait_ge(consts_ok, 1)
                    dve.wait_ge(stats_ok, count)
                    dve.bn_aggr(mv[:, 0, q, :], stats[:, 0, q, :]).then_inc(mv_ok, 1)
                dve.wait_ge(rstd_ok, n + 1)
                dve.tensor_tensor(rstd_m[:], rstd[:, 0, :], nm[:, bass.ts(c, QT)], ALU.mult).then_inc(h2_step, 1)
                dve.wait_ge(h2_step, 9 * c + 1)
                for q in range(QT):
                    dve.tensor_scalar(h2[:, b, q, :], h2[:, b, q, :], mv[:, 0, q, 0:1],
                                      rstd_m[:, q:q + 1], ALU.subtract, ALU.mult).then_inc(h2_step, 1)
                for q in range(QT):
                    dve.wait_ge(h2_step, 9 * c + 2 + q)
                    dve.tensor_tensor(h2[:, b, q, :], h2[:, b, q, :], scale_b[:], ALU.mult).then_inc(h2_step, 1)
                for q in range(QT):
                    dve.wait_ge(h2_step, 9 * c + 6 + q)
                    dve.scalar_tensor_tensor(h2[:, b, q, :], bias_b[:], nm[:, bass.ds(c * QT + q, 1)],
                                             h2[:, b, q, :], ALU.mult, ALU.add).then_inc(h2_ok, 1)

            def norm_y(c, b):
                n = order_y(c)
                dve.wait_ge(xr_in, 16 * (c + 1))
                wait(dve, out_done, 16 * c)
                for q in range(QT):
                    dve.wait_ge(down_ok, 4 * c + q + 1)
                    dve.tensor_tensor(y[:, q, :], down_ps[:, q % 2, :], h2[:, b, q, :], ALU.add).then_inc(y_step, 1)
                    dve.wait_ge(y_step, 4 * c + q + 1)
                    dve.tensor_tensor(y[:, q, :], y[:, q, :], xr[:, q, :], ALU.add).then_inc(y_ok, 1)
                    dve.wait_ge(y_ok, 4 * c + q + 1)
                    dve.bn_stats(stats[:, 1, q, :], y[:, q, :]).then_inc(stats_ok, 1)
                    count = 4 * n + q + 1
                    dve.compute_val(count)
                    dve.wait_ge(consts_ok, 1)
                    dve.wait_ge(stats_ok, count)
                    dve.bn_aggr(mv[:, 1, q, :], stats[:, 1, q, :]).then_inc(mv_ok, 1)
                dve.wait_ge(rstd_ok, n + 1)
                for q in range(QT):
                    dve.tensor_scalar(y[:, q, :], y[:, q, :], mv[:, 1, q, 0:1], rstd[:, 1, q:q + 1],
                                      ALU.subtract, ALU.mult).then_inc(out_ok, 1)

            norm_h1(0, 0)

            def body(c, b):
                if not is_last(c):
                    norm_h1(c + 1, 1 - b)
                norm_y(c, b)

            over_chunks(dve, body)

        @block.tensor
        def _(pe):
            def attn(c):
                pe.wait_ge(ctx_in, 16 * (c + 1))
                for q in range(QT):
                    wait(pe, h1_step, 4 * c + q - 1)
                    for k in range(KT):
                        last = pe.matmul(attn_ps[:, q % 2, :], ctxt[:, k, q * P:(q + 1) * P], wo[:, k, :],
                                         start=(k == 0), stop=(k == KT - 1))
                    last.then_inc(attn_ok, 1)

            def body(c, b):
                for q in range(QT):
                    pe.wait_ge(h2_ok, 4 * c + q + 1)
                    wait(pe, h2t_ok, 4 * c + q - 1)
                    for k in range(KT):
                        last = pe.transpose(turn_ps[:, q % 2, k, :], h2[:, b, q, k * P:(k + 1) * P], ident[:])
                    last.then_inc(turned, 1)
                pe.wait_ge(w1_in, 16)
                pe.wait_ge(h2t_ok, 4 * c + 4)
                for f in range(FT):
                    wait(pe, gelu_ok, FT * c + f - 1)
                    for k in range(KT):
                        last = pe.matmul(up_ps[:, f % 2, :], w1[:, k, f * P:(f + 1) * P], h2t[:, k, :],
                                         start=(k == 0), stop=(k == KT - 1))
                    last.then_inc(up_ok, 1)
                if not is_last(c):
                    attn(c + 1)
                pe.wait_ge(w2_in, 16)
                pe.wait_ge(gelu_ok, FT * c + FT)
                for q in range(QT):
                    wait(pe, y_step, 4 * c + q - 1)
                    for f in range(FT):
                        last = pe.matmul(down_ps[:, q % 2, :], g[:, f, q * P:(q + 1) * P], w2[:, f, :],
                                         start=(f == 0), stop=(f == FT - 1))
                    last.then_inc(down_ok, 1)

            pe.wait_ge(ident_ok, 1)
            pe.wait_ge(consts_in, 16 * 5)
            attn(0)
            over_chunks(pe, body)


def program(nc, io):
    def scratch(name, shape, dt=F32):
        return nc.dram_tensor(name, shape, dt, kind="Internal").ap()

    scr = {n: scratch("scr_" + n, (D, N)) for n in ("k_hi", "k_lo", "q_hi", "q_lo", "ctx")}
    scr["v"] = scratch("scr_v", (N, D))
    scr["ht"] = scratch("scr_ht", (N, D))
    scr["v_sum"] = scratch("scr_v_sum", (P, D))
    scr["shift"] = scratch("scr_shift", (2, QT, P))
    scr["lone"] = scratch("scr_lone", (N,))
    scr["edge_t"] = scratch("scr_edge_t", (NC, P, ST, CH), U8)
    with ExitStack() as ctx:
        keep = {"minus_bound": ctx.enter_context(nc.sbuf_tensor("minus_bound", [P, 1], F32)),
                "bounded_f": ctx.enter_context(nc.sbuf_tensor("bounded_f", [1, 1], F32)),
                "bounded_i": ctx.enter_context(nc.sbuf_tensor("bounded_i", [1, 1], I32))}
        project(nc, io, scr, keep)
        attend(nc, io, scr, keep)
        feed(nc, io, scr, keep)


_INS = ["x", "adj", "nodemask", "h_target", "ln1_scale", "ln1_bias", "Wq", "bq", "Wk", "bk", "Wv", "bv",
        "Wo", "bo", "ln2_scale", "ln2_bias", "W1", "W2"]


def kernel(**inputs):
    import numpy as np
    import concourse.bacc as bacc
    from concourse.bass_utils import run_bass_kernel_spmd

    nc = bacc.Bacc("TRN2", target_bir_lowering=False, num_devices=1)
    arrays, io = {}, {}
    for name in _INS:
        a = np.ascontiguousarray(inputs.get(name, inputs.get("L0_gnn_" + name)))
        arrays["in_" + name] = a
        io[name] = nc.dram_tensor("in_" + name, a.shape, mybir.dt.from_np(a.dtype), kind="ExternalInput").ap()
    io["out"] = nc.dram_tensor("out", (N, D), F32, kind="ExternalOutput").ap()
    program(nc, io)
    return run_bass_kernel_spmd(nc, [arrays], core_ids=[0]).results[0]["out"]
```

```python
from contextlib import ExitStack

import concourse.bass as bass
from concourse import mybir

ALU = mybir.AluOpType
ACT = mybir.ActivationFunctionType
AX_X = mybir.AxisListType.X
F32 = mybir.dt.float32
F32R = mybir.dt.float32r
BF16 = mybir.dt.bfloat16
I32 = mybir.dt.int32
U8 = mybir.dt.uint8
RMAX = bass.bass_isa.ReduceOp.max

P = 128
N = 4096
D = 512
H = 8
HD = D // H
F = 4 * D
KT = D // P
CH = 512
NC = N // CH
QT = CH // P
ST = N // P
PAIRS = H // 2
FT = F // P
EPS = 1e-5
NEG = -1e30
QSCALE = HD ** -0.5
BOUND_MAX = 40.0
NORM_SLACK = 1.05
CLAMP = 60.0


def start_holds(ready, count=16):
    def hold(eng, s, value):
        if isinstance(value, int):
            if value > 0:
                eng.wait_ge(s, value)
            return
        eng.compute_val(value)
        eng.wait_ge(ready, count)
        eng.wait_ge(s, value)
    return hold


def project(nc, io, scr, keep):
    with ExitStack() as ctx:
        def sb(name, shape, dt):
            return ctx.enter_context(nc.sbuf_tensor(name, shape, dt))

        def ps(name, shape, dt):
            return ctx.enter_context(nc.psum_tensor(name, shape, dt))

        sem = nc.alloc_semaphore

        wk, wv, wq = (sb(n, [P, KT, D], F32) for n in ("wk", "wv", "wq"))
        scale_b, bias_b, bv_b = (sb(n, [P, D], F32) for n in ("ln1_scale_b", "ln1_bias_b", "bv_b"))
        bk_col, bq_col, bqs_col = (sb(n, [P, PAIRS], F32) for n in ("bk_col", "bq_col", "bqs_col"))
        nm_i = sb("nodemask_i", [P, ST], I32)
        nm = sb("nodemask_f", [P, ST], F32)
        ident = sb("ident", [P, P], F32)
        ident_h = sb("ident_h", [P, P], BF16)
        halves = sb("halves", [P, P], BF16)
        minus_half = sb("minus_half", [P, QT], F32)
        eps_t = sb("eps", [P, QT], F32)
        xin = [sb(f"xin{s}", [P, QT, D], F32) for s in range(2)]
        z = [sb(f"z{s}", [P, QT, D], F32) for s in range(2)]
        zt = [sb(f"zt{s}", [P, KT, CH], F32) for s in range(2)]
        stats = sb("stats", [P, 2, QT, 6], F32)
        mv = sb("mv", [P, 2, QT, 2], F32)
        var_e = sb("var_e", [P, 2, QT], F32)
        rstd = sb("rstd", [P, 2, QT], F32)
        rstd_m = sb("rstd_m", [P, 2, QT], F32)
        adj = sb("adj_rows", [P, 2, N], I32)
        edge = sb("edge", [P, 2, N], BF16)
        edge_t = sb("edge_t", [P, ST, CH], U8)
        kq = sb("kq", [P, 2, CH], F32)
        kq_hi = sb("kq_hi", [P, 2, CH], F32R)
        kq_lo = sb("kq_lo", [P, 2, CH], F32R)
        kq_sq = sb("kq_sq", [P, 2, CH], BF16)
        norm_max = sb("norm_max", [P, 2, 1], F32)
        norm_new = sb("norm_new", [P, 2], F32)
        vv = sb("vv", [P, 2, D], F32)
        v_sum = sb("v_sum", [P, D], F32)
        one_col = sb("one_col", [P, 1], F32)
        bnd = sb("bnd", [P, 4], F32)
        all_max = sb("all_max", [P, 2], F32)

        turn_ps = ps("turn_ps", [P, 2, KT, P], F32)
        proj_ps = ps("proj_ps", [P, 2, CH], F32)
        edge_ps = ps("edge_ps", [P, 2, 8, P], BF16)
        norm_ps = ps("norm_ps", [P, CH], F32)

        consts_in = sem("consts_in")
        x_in = [sem(f"x_in{s}") for s in range(2)]
        adj_in = [sem(f"adj_in{b}") for b in range(2)]
        ident_ok, ident_zero = sem("ident_ok"), sem("ident_zero")
        consts_ok, halves_ok = sem("consts_ok"), sem("halves_ok")
        stats_ok, mv_ok, var_ok, rstd_ok, z_step, z_ok = (sem(n) for n in (
            "stats_ok", "mv_ok", "var_ok", "rstd_ok", "z_step", "z_ok"))
        turned, zt_ok = sem("turned"), sem("zt_ok")
        proj_ok, kq_ok, v_ok, lo_ok = sem("proj_ok"), sem("kq_ok"), sem("v_ok"), sem("lo_ok")
        norm_ok, norm_read, norm_max_ok = sem("norm_ok"), sem("norm_read"), sem("norm_max_ok")
        sq_ok = sem("sq_ok")
        kq_out = [sem(f"kq_out{b}") for b in range(2)]
        v_out = [sem(f"v_out{b}") for b in range(2)]
        v_sum_ok = sem("v_sum_ok")
        ht_out = sem("ht_out")
        edge_ok, edge_turned, edge_t_ok, edge_out = (sem(n) for n in (
            "edge_ok", "edge_turned", "edge_t_ok", "edge_out"))
        v_tot_ok, v_tot_kept = sem("v_tot_ok"), sem("v_tot_kept")
        bnd_ok, red_ok, pool_ok = sem("bnd_ok"), sem("red_ok"), sem("pool_ok")

        x_rows = [io["x"].rearrange("(c q p) d -> c p q d", p=P, q=QT),
                  io["h_target"].rearrange("(c q p) d -> c p q d", p=P, q=QT)]
        adj_rows = io["adj"].rearrange("(b p) s -> b p s", p=P)
        ht_rows = scr["ht"].rearrange("(c q p) d -> c p q d", p=P, q=QT)
        v_rows = scr["v"].rearrange("(b p) d -> b p d", p=P)

        def wait(eng, s, value):
            if not isinstance(value, int) or value > 0:
                eng.wait_ge(s, value)

        def over_chunks(eng, body):
            body(0)
            with eng.Fori(1, NC - 1) as c:
                body(c)
            body(NC - 1)

        block = ctx.enter_context(nc.Block())
        hold = start_holds(x_in[0])

        @block.sync
        def _(sp):
            def load_x(c, s):
                sp.dma_start(xin[s][:], x_rows[s][c]).then_inc(x_in[s], 16)

            def load_adj(b, slot):
                sp.dma_start(adj[:, slot, :], adj_rows[b]).then_inc(adj_in[slot], 16)

            load_x(0, 0)
            sp.dma_start(scale_b[:], io["ln1_scale"].partition_broadcast(P)).then_inc(consts_in, 16)
            sp.dma_start(bias_b[:], io["ln1_bias"].partition_broadcast(P)).then_inc(consts_in, 16)
            sp.dma_start(nm_i[:], io["nodemask"].rearrange("(t p) -> p t", p=P), allow_slow_non_contiguous=True).then_inc(consts_in, 16)
            sp.dma_start(bk_col[:], io["bk"].rearrange("(m p) -> p m", p=P), allow_slow_non_contiguous=True).then_inc(consts_in, 16)
            sp.dma_start(bq_col[:], io["bq"].rearrange("(m p) -> p m", p=P), allow_slow_non_contiguous=True).then_inc(consts_in, 16)
            sp.dma_start(bv_b[:], io["bv"].partition_broadcast(P)).then_inc(consts_in, 16)
            for t, w in ((wk, "Wk"), (wv, "Wv"), (wq, "Wq")):
                sp.dma_start(t[:], io[w].rearrange("(k p) n -> p k n", p=P)).then_inc(consts_in, 16)
            load_x(0, 1)
            load_adj(0, 0)
            load_adj(1, 1)

            def store_kq(c, i, side):
                b, m = i % 2, i % PAIRS
                hi, lo = (scr["k_hi"], scr["k_lo"]) if side == 0 else (scr["q_hi"], scr["q_lo"])
                hold(sp, lo_ok, 8 * c + i + 1)
                cols = bass.ts(c, CH)
                sp.dma_start(hi[m * P:(m + 1) * P, cols], kq_hi[:, b, :].bitcast(F32)).then_inc(kq_out[b], 16)
                sp.dma_start(lo[m * P:(m + 1) * P, cols], kq_lo[:, b, :].bitcast(F32)).then_inc(kq_out[b], 16)

            def body(c):
                more = not (isinstance(c, int) and c == NC - 1)
                if more:
                    hold(sp, z_ok, 8 * c + 4)
                    load_x(c + 1, 0)
                hold(sp, edge_ok, 4 * c + 1)
                load_adj(4 * c + 2, 0)
                for i in range(4):
                    store_kq(c, i, 0)
                hold(sp, edge_ok, 4 * c + 2)
                load_adj(4 * c + 3, 1)
                for q in range(QT):
                    hold(sp, v_ok, 4 * c + q + 1)
                    sp.dma_start(v_rows[4 * c + q], vv[:, q % 2, :]).then_inc(v_out[q % 2], 16)
                hold(sp, z_ok, 8 * c + 8)
                if more:
                    load_x(c + 1, 1)
                sp.dma_start(ht_rows[c], z[1][:]).then_inc(ht_out, 16)
                for i in range(4, 8):
                    store_kq(c, i, 1)
                if more:
                    hold(sp, edge_ok, 4 * c + 3)
                    load_adj(4 * c + 4, 0)
                hold(sp, edge_t_ok, 16 * c + 16)
                sp.dma_start(scr["edge_t"][c], edge_t[:]).then_inc(edge_out, 16)
                if more:
                    hold(sp, edge_ok, 4 * c + 4)
                    load_adj(4 * c + 5, 1)

            over_chunks(sp, body)
            for b in range(2):
                hold(sp, kq_out[b], 2 * 16 * 4 * NC)
                hold(sp, v_out[b], 16 * 2 * NC)
            for s in (ht_out, edge_out):
                hold(sp, s, 16 * NC)

        @block.gpsimd
        def _(pool):
            for t in (ident, ident_h):
                pool.memset(t[:], 0.0).then_inc(ident_zero, 1)
            pool.memset(minus_half[:], -0.5).then_inc(ident_zero, 1)
            pool.memset(eps_t[:], EPS).then_inc(ident_zero, 1)
            pool.memset(v_sum[:], 0.0).then_inc(ident_zero, 1)
            pool.wait_ge(ident_zero, 5)
            for t in (ident, ident_h):
                pool.affine_select(out=t[:], in_=t[:], compare_op=ALU.not_equal, fill=1.0, base=0,
                                   pattern=[[-1, P]], channel_multiplier=1).then_inc(ident_ok, 1)

            def body(c):
                for s in range(2):
                    pool.wait_ge(mv_ok, 8 * c + 4 * s + 4)
                    pool.tensor_tensor(var_e[:, s, :], mv[:, s, :, 1], eps_t[:], ALU.add).then_inc(var_ok, 1)
                    pool.wait_ge(var_ok, 2 * c + s + 1)
                    pool.tensor_tensor(rstd[:, s, :], var_e[:, s, :], minus_half[:], ALU.pow).then_inc(rstd_ok, 1)
                    if s == 0:
                        continue
                    for q in range(QT):
                        pool.wait_ge(v_ok, 4 * c + q + 1)
                        wait(pool, v_sum_ok, 4 * c + q)
                        pool.tensor_tensor(v_sum[:], v_sum[:], vv[:, q % 2, :], ALU.add).then_inc(v_sum_ok, 1)

            over_chunks(pool, body)
            pool.wait_ge(norm_max_ok, 8 * NC)
            for s in range(2):
                pool.partition_all_reduce(all_max[:, s:s + 1], norm_max[:, s, :], P, RMAX).then_inc(pool_ok, 1)

        @block.scalar
        def _(act):
            def body(c):
                def turned_rows(s):
                    for q in range(QT):
                        n = 4 * s + q
                        act.wait_ge(turned, 8 * c + n + 1)
                        if q == 0:
                            wait(act, proj_ok, 12 * (c - 1) + (8 if s == 0 else 12))
                        act.copy(zt[s][:, :, q * P:(q + 1) * P], turn_ps[:, n % 2, :, :]).then_inc(zt_ok, 1)

                def keys_or_queries(s):
                    for m in range(PAIRS):
                        i = 4 * s + m
                        b = i % 2
                        act.wait_ge(proj_ok, 12 * c + (m if s == 0 else 8 + m) + 1)
                        wait(act, kq_out[b], 32 * (4 * c + i // 2))
                        bias = bk_col[:, m:m + 1] if s == 0 else bqs_col[:, m:m + 1]
                        scale = 1.0 if s == 0 else QSCALE
                        act.activation(kq[:, b, :], proj_ps[:, i % 2, :], ACT.Identity, bias=bias, scale=scale)
                        act.activation(kq_hi[:, b, :], proj_ps[:, i % 2, :], ACT.Identity, bias=bias,
                                       scale=scale).then_inc(kq_ok, 1)

                def mask_tiles(k):
                    for g in range(4):
                        n = 4 * k + g
                        act.wait_ge(edge_turned, 16 * c + n + 1)
                        if n == 0:
                            wait(act, edge_out, 16 * c)
                        act.copy(edge_t[:, 8 * g:8 * g + 8, k * P:(k + 1) * P],
                                 edge_ps[:, n % 2, :, :]).then_inc(edge_t_ok, 1)

                turned_rows(0)
                mask_tiles(0)
                keys_or_queries(0)
                mask_tiles(1)
                turned_rows(1)
                mask_tiles(2)
                keys_or_queries(1)
                mask_tiles(3)

            act.wait_ge(consts_ok, 1)
            over_chunks(act, body)
            act.wait_ge(bnd_ok, 1)
            act.activation(bnd[:, 1:2], bnd[:, 0:1], ACT.Sqrt).then_inc(red_ok, 1)

        @block.vector
        def _(dve):
            dve.memset(one_col[:], 1.0)
            dve.memset(halves[:], 0.0).then_inc(halves_ok, 1)
            dve.wait_ge(halves_ok, 1)
            dve.memset(halves[0:HD, 0:HD], 1.0).then_inc(halves_ok, 1)
            dve.memset(halves[HD:P, HD:P], 1.0).then_inc(halves_ok, 1)
            dve.wait_ge(consts_in, 16 * 9)
            dve.tensor_scalar(nm[:], nm_i[:], 1, None, ALU.is_equal)
            dve.memset(norm_max[:], 0.0)
            dve.tensor_scalar(bqs_col[:], bq_col[:], QSCALE, None, ALU.mult).then_inc(consts_ok, 1)
            dve.wait_ge(consts_ok, 1)

            def body(c):
                def layer_norm(s):
                    dve.wait_ge(x_in[s], 16 * (c + 1))
                    for q in range(QT):
                        dve.bn_stats(stats[:, s, q, :], xin[s][:, q, :]).then_inc(stats_ok, 1)
                    for q in range(QT):
                        count = 8 * c + 4 * s + q + 1
                        dve.compute_val(count)
                        dve.wait_ge(consts_ok, 1)
                        dve.wait_ge(stats_ok, count)
                        dve.bn_aggr(mv[:, s, q, :], stats[:, s, q, :]).then_inc(mv_ok, 1)

                def scale_rows(s):
                    dve.wait_ge(rstd_ok, 2 * c + s + 1)
                    dve.tensor_tensor(rstd_m[:, s, :], rstd[:, s, :],
                                      nm[:, bass.ts(c, QT)], ALU.mult).then_inc(z_step, 1)
                    wait(dve, turned, 8 * (c - 1) + 4 * s + 4)
                    if s == 1:
                        wait(dve, ht_out, 16 * c)
                    dve.wait_ge(z_step, 18 * c + 9 * s + 1)
                    for q in range(QT):
                        dve.tensor_scalar(z[s][:, q, :], xin[s][:, q, :], mv[:, s, q, 0:1],
                                          rstd_m[:, s, q:q + 1], ALU.subtract, ALU.mult).then_inc(z_step, 1)
                    for q in range(QT):
                        dve.wait_ge(z_step, 18 * c + 9 * s + 2 + q)
                        dve.tensor_tensor(z[s][:, q, :], z[s][:, q, :], scale_b[:], ALU.mult).then_inc(z_step, 1)
                    for q in range(QT):
                        dve.wait_ge(z_step, 18 * c + 9 * s + 6 + q)
                        dve.scalar_tensor_tensor(z[s][:, q, :], bias_b[:], nm[:, bass.ds(c * QT + q, 1)],
                                                 z[s][:, q, :], ALU.mult, ALU.add).then_inc(z_ok, 1)

                def edges(k):
                    b = k % 2
                    dve.wait_ge(adj_in[b], 16 * (2 * c + k // 2 + 1))
                    wait(dve, edge_turned, 4 * (4 * c + k - 1))
                    dve.tensor_scalar(edge[:, b, :], adj[:, b, :], 0, None, ALU.not_equal).then_inc(edge_ok, 1)

                def split(s, m):
                    i = 4 * s + m
                    b = i % 2
                    dve.wait_ge(kq_ok, 8 * c + i + 1)
                    dve.tensor_tensor(kq_lo[:, b, :], kq[:, b, :], kq_hi[:, b, :].bitcast(F32),
                                      ALU.subtract).then_inc(lo_ok, 1)
                    wait(dve, norm_ok, 8 * c + i - 1)
                    dve.tensor_tensor(kq_sq[:, b, :], kq[:, b, :], kq[:, b, :], ALU.mult).then_inc(sq_ok, 1)
                    if i > 0 or not isinstance(c, int) or c > 0:
                        fold_norm(8 * c + i - 1, 0 if 1 <= i <= 4 else 1)

                def fold_norm(n, which):
                    dve.wait_ge(norm_ok, n + 1)
                    wait(dve, norm_max_ok, n)
                    dve.reduce_max(norm_new[:, which:which + 1], norm_ps[:], AX_X).then_inc(norm_read, 1)
                    dve.wait_ge(norm_read, n + 1)
                    dve.tensor_tensor(norm_max[:, which, :], norm_max[:, which, :],
                                      norm_new[:, which:which + 1], ALU.max).then_inc(norm_max_ok, 1)

                layer_norm(0)
                edges(0)
                scale_rows(0)
                layer_norm(1)
                edges(1)
                for m in range(PAIRS):
                    split(0, m)
                scale_rows(1)
                for q in range(QT):
                    n = 4 + q
                    dve.wait_ge(proj_ok, 12 * c + n + 1)
                    wait(dve, v_out[q % 2], 16 * (2 * c + q // 2))
                    wait(dve, v_sum_ok, 4 * c + q - 1)
                    dve.tensor_tensor(vv[:, q % 2, :], proj_ps[:, n % 2, :], bv_b[:], ALU.add).then_inc(v_ok, 1)
                edges(2)
                for m in range(PAIRS):
                    split(1, m)
                edges(3)
                if isinstance(c, int) and c == NC - 1:
                    fold_norm(8 * c + 7, 1)

            over_chunks(dve, body)
            dve.wait_ge(v_tot_ok, 1)
            dve.tensor_copy(keep["v_tot"][:], norm_ps[:, 0:PAIRS]).then_inc(v_tot_kept, 1)
            dve.wait_ge(pool_ok, 2)
            dve.tensor_tensor(bnd[:, 0:1], all_max[:, 0:1], all_max[:, 1:2], ALU.mult).then_inc(bnd_ok, 1)
            dve.wait_ge(red_ok, 1)
            dve.tensor_scalar(keep["minus_bound"][:], bnd[:, 1:2], -NORM_SLACK, None, ALU.mult).then_inc(bnd_ok, 1)
            dve.wait_ge(bnd_ok, 2)
            dve.tensor_scalar(keep["bounded_f"][:], keep["minus_bound"][0:1, 0:1], -BOUND_MAX, None,
                              ALU.is_ge).then_inc(bnd_ok, 1)
            dve.wait_ge(bnd_ok, 3)
            dve.tensor_copy(keep["bounded_i"][:], keep["bounded_f"][:]).then_inc(bnd_ok, 1)
            dve.wait_ge(bnd_ok, 4)

        @block.tensor
        def _(pe):
            def body(c):
                def turn(s):
                    for q in range(QT):
                        n = 4 * s + q
                        pe.wait_ge(z_ok, 8 * c + n + 1)
                        wait(pe, zt_ok, 8 * c + n - 1)
                        for k in range(KT):
                            last = pe.transpose(turn_ps[:, n % 2, k, :], z[s][:, q, k * P:(k + 1) * P], ident[:])
                        last.then_inc(turned, 1)

                def keys_or_queries(s, w):
                    pe.wait_ge(zt_ok, 8 * c + 4 * s + 4)
                    for m in range(PAIRS):
                        if s == 0:
                            wait(pe, kq_ok, 8 * c + m - 1)
                        elif m < 2:
                            wait(pe, v_ok, 4 * c + 3 + m)
                        else:
                            wait(pe, kq_ok, 8 * c + 3 + m)
                        for k in range(KT):
                            last = pe.matmul(proj_ps[:, m % 2, :], w[:, k, m * P:(m + 1) * P], zt[s][:, k, :],
                                             start=(k == 0), stop=(k == KT - 1))
                        last.then_inc(proj_ok, 1)
                        i = 4 * s + m
                        if i > 0 or not isinstance(c, int) or c > 0:
                            norms(8 * c + i - 1, (i - 1) % 2)

                def norms(n, b):
                    pe.wait_ge(sq_ok, n + 1)
                    wait(pe, norm_read, n)
                    pe.matmul(norm_ps[:], halves[:], kq_sq[:, b, :], start=True, stop=True).then_inc(norm_ok, 1)

                def values():
                    for q in range(QT):
                        if q < 2:
                            wait(pe, kq_ok, 8 * c + 3 + q)
                        else:
                            wait(pe, v_ok, 4 * c + q - 1)
                        for k in range(KT):
                            last = pe.matmul(proj_ps[:, q % 2, :], zt[0][:, k, q * P:(q + 1) * P], wv[:, k, :],
                                             start=(k == 0), stop=(k == KT - 1))
                        last.then_inc(proj_ok, 1)

                def turn_edges(k):
                    pe.wait_ge(edge_ok, 4 * c + k + 1)
                    for g in range(4):
                        n = 4 * k + g
                        wait(pe, edge_t_ok, 16 * c + n - 1)
                        for t in range(8):
                            at = (8 * g + t) * P
                            last = pe.transpose(edge_ps[:, n % 2, t, :], edge[:, k % 2, at:at + P], ident_h[:])
                        last.then_inc(edge_turned, 1)

                turn(0)
                turn_edges(0)
                keys_or_queries(0, wk)
                turn_edges(1)
                values()
                turn(1)
                turn_edges(2)
                keys_or_queries(1, wq)
                turn_edges(3)
                if isinstance(c, int) and c == NC - 1:
                    norms(8 * c + 7, 1)

            pe.wait_ge(ident_ok, 2)
            pe.wait_ge(halves_ok, 3)
            pe.wait_ge(consts_in, 16 * 9)
            over_chunks(pe, body)
            pe.wait_ge(v_sum_ok, ST)
            pe.wait_ge(norm_read, 8 * NC)
            for m in range(PAIRS):
                last = pe.matmul(norm_ps[:, m:m + 1], v_sum[:, m * P:(m + 1) * P], one_col[:],
                                 start=True, stop=True)
            last.then_inc(v_tot_ok, 1)


LAG = 3
PR = 8
GR = 4


def attend(nc, io, scr, keep):
    STEPS = PAIRS * NC
    with ExitStack() as ctx:
        def sb(name, shape, dt):
            return ctx.enter_context(nc.sbuf_tensor(name, shape, dt))

        def ps(name, shape, dt):
            return ctx.enter_context(nc.psum_tensor(name, shape, dt))

        sem = nc.alloc_semaphore

        k_st = sb("k_stack", [P, 2, N], F32R)
        v_sb = sb("v_pair", [P, ST, P], F32)
        q_a = sb("q_hi_lo", [P, 2, 2, CH], F32R)
        q_b = sb("q_lo_hi", [P, 2, 2, CH], F32R)
        edge = sb("edge_st", [P, 2, ST, CH], U8)
        prob = sb("prob", [P, PR, 2, CH], F32)
        psum2 = sb("prob_sums", [P, GR, 2, CH], F32)
        den_sb = sb("den_sb", [P, CH], F32)
        out_sb = sb("out_sb", [P, CH], F32)
        den_all = sb("den_all", [P, CH], F32)
        lone = sb("lone", [P, CH], F32)
        rden = sb("rden", [P, CH], F32)
        ctx_sb = sb("ctx_sb", [P, CH], F32)
        ones = sb("ones32", [P, 32], F32)
        pick = sb("pick", [P, P], F32)
        w_raw = sb("w_raw", [P, CH], F32)
        w_hi, w_lo = (sb(n, [P, CH], F32R) for n in ("w_hi", "w_lo"))

        ones_sq = sb("ones_sq", [P, P], F32)
        spread = sb("spread", [P, P], F32R)
        shift = sb("shift", [P, 2, CH], F32R)
        part_max = sb("part_max", [P, N // CH], F32)
        top = sb("top", [P, 2, QT], F32)
        minus_max = sb("minus_max", [P, 2, QT], F32)
        adj_rows = prob[:, PR // 2:PR].rearrange("p a b c -> p (a b c)").bitcast(I32)
        bias = edge[:, 1].rearrange("p a b -> p (a b)").bitcast(F32)

        sc = ps("scores", [P, 3, 2, CH], F32)
        po = ps("pv", [P, CH], F32)
        pl = ps("den", [P, CH], F32)

        consts_ok, pick_ok = sem("a_consts_ok"), sem("pick_ok")
        w_raw_in, w_hi_ok, w_lo_ok, w_out = (sem(n) for n in ("w_raw_in", "w_hi_ok", "w_lo_ok", "w_out"))
        k_in = [sem(f"k_in{i}") for i in range(4)]
        v_in = [sem(f"v_in{i}") for i in range(4)]
        q_in = [sem(f"q_in{b}") for b in range(2)]
        edge_in = [sem(f"edge_in{b}") for b in range(2)]
        scores_ok, exp_ok, masked_ok, sums_ok, pv_ok, den_ok = (sem(n) for n in (
            "scores_ok", "exp_ok", "masked_ok", "sums_ok", "pv_ok", "den_ok"))
        step_ok, den_copied, out_copied, den_whole, den_taken, finish_step, ctx_ok, ctx_out = (sem(n) for n in (
            "step_ok", "den_copied", "out_copied", "den_whole", "den_taken", "finish_step", "ctx_ok", "ctx_out"))

        cf = {n: sem(n) for n in (
            "cf_in", "cf_adj", "cf_rough", "cf_minus", "shift_out", "shift_in", "cf_shift", "cf_scores", "cf_exp",
            "cf_masked", "cf_out_sb", "cf_taken", "cf_den", "cf_den_all", "cf_fin", "cf_out", "pre_bias", "pre_added",
            "pre_max", "pre_top", "pre_clamped", "pre_pv", "pre_ctx")}
        (cf_in, cf_adj, cf_rough, cf_minus, shift_out, shift_in, cf_shift, cf_scores, cf_exp, cf_masked, cf_out_sb,
         cf_taken, cf_den, cf_den_all, cf_fin, cf_out, pre_bias, pre_added, pre_max, pre_top, pre_clamped, pre_pv,
         pre_ctx) = cf.values()

        qk = {n: scr[n].rearrange("(m h d) t -> m d h t", m=PAIRS, h=2) for n in ("k_hi", "k_lo", "q_hi", "q_lo")}
        v_rows = scr["v"].rearrange("(t p) (m c) -> m p t c", p=P, m=PAIRS)
        ctx_rows = scr["ctx"].rearrange("(m p) t -> m p t", p=P)
        adj_blocks = io["adj"].rearrange("(b p) s -> b p s", p=P)
        shift_row = scr["shift"].rearrange("h q p -> h (q p)")
        shift_cols = scr["shift"].rearrange("h q p -> p h q")

        def wait(eng, s, value):
            if not isinstance(value, int) or value > 0:
                eng.wait_ge(s, value)

        def over_steps(eng, body):
            body(0, 0)
            body(1, 1)
            with eng.Fori(1, STEPS // 2) as i:
                body(2 * i, 0)
                body(2 * i + 1, 1)

        hold = start_holds(k_in[0])

        def load_k(sp, m, i):
            cols = slice(i * N // 4, (i + 1) * N // 4)
            sp.dma_start(k_st[0:HD, :, cols].bitcast(F32), qk["k_hi"][m][:, :, cols]).then_inc(k_in[i], 16)
            sp.dma_start(k_st[HD:P, :, cols].bitcast(F32), qk["k_lo"][m][:, :, cols]).then_inc(k_in[i], 16)

        def load_v(sp, m, i):
            t = slice(i * ST // 4, (i + 1) * ST // 4)
            sp.dma_start(v_sb[:, t, :], v_rows[m][:, t, :]).then_inc(v_in[i], 16)

        def load_q(sp, m, c, b):
            cols = bass.ts(c, CH)
            for t, top, low in ((q_a, "q_hi", "q_lo"), (q_b, "q_lo", "q_hi")):
                sp.dma_start(t[0:HD, b].bitcast(F32), qk[top][m][:, :, cols]).then_inc(q_in[b], 16)
                sp.dma_start(t[HD:P, b].bitcast(F32), qk[low][m][:, :, cols]).then_inc(q_in[b], 16)

        def load_edge(sp, c, b):
            sp.dma_start(edge[:, b], scr["edge_t"][c]).then_inc(edge_in[b], 16)

        FINISH = 8

        def finish_op(dve, s, k, pair, fin, den_sem, out_sem, done):
            base = (FINISH - 1) * s
            if k == 0:
                dve.wait_ge(den_sem, s + 1)
                dve.tensor_scalar(lone[:], den_all[:], 0.0, None, ALU.is_equal).then_inc(fin, 1)
            elif k == 1:
                dve.wait_ge(fin, base + 1)
                dve.scalar_tensor_tensor(den_all[:], lone[:], float(N), den_all[:], ALU.mult, ALU.add).then_inc(fin, 1)
            elif k < 6:
                q = slice((k - 2) * P, (k - 1) * P)
                dve.wait_ge(fin, base + 2)
                dve.reciprocal(rden[:, q], den_all[:, q]).then_inc(fin, 1)
            elif k == 6:
                dve.wait_ge(out_sem, s + 1)
                dve.scalar_tensor_tensor(out_sb[:], lone[:], keep["v_tot"][:, bass.ds(pair, 1)], out_sb[:],
                                         ALU.mult, ALU.add).then_inc(fin, 1)
            else:
                dve.wait_ge(fin, base + 7)
                if not (isinstance(s, int) and s == 0) and done is ctx_ok:
                    dve.wait_ge(ctx_out, 16 * s)
                dve.tensor_tensor(ctx_sb[:], out_sb[:], rden[:], ALU.mult).then_inc(done, 1)

        def bounded_sync(sp):
            for i in range(4):
                load_k(sp, 0, i)
                if i == 0:
                    load_q(sp, 0, 0, 0)
                    load_edge(sp, 0, 0)
                load_v(sp, 0, i)

            def step(m, c, b):
                s = NC * m + c
                first = isinstance(s, int) and s == 0
                last = isinstance(s, int) and s == STEPS - 1
                ends_pair = isinstance(c, int) and c == NC - 1
                if not last:
                    nm, ncn = (m + 1, 0) if ends_pair else (m, c + 1)
                    hold(sp, scores_ok, ST * s)
                    load_q(sp, nm, ncn, 1 - b)
                    hold(sp, masked_ok, ST * s)
                    load_edge(sp, ncn, 1 - b)
                if not first:
                    pm, pc = (m - 1, NC - 1) if isinstance(c, int) and c == 0 else (m, c - 1)
                    hold(sp, ctx_ok, s)
                    sp.dma_start(ctx_rows[pm][:, bass.ts(pc, CH)], ctx_sb[:]).then_inc(ctx_out, 16)
                if ends_pair and not last:
                    for i in range(4):
                        hold(sp, scores_ok, ST * s + 8 * (i + 1))
                        load_k(sp, m + 1, i)
                        hold(sp, pv_ok, ST * s + 8 * (i + 1))
                        load_v(sp, m + 1, i)

            def pair(m):
                step(m, 0, 0)
                step(m, 1, 1)
                with sp.Fori(1, NC // 2 - 1) as i:
                    step(m, 2 * i, 0)
                    step(m, 2 * i + 1, 1)
                step(m, NC - 2, 0)
                step(m, NC - 1, 1)

            pair(0)
            with sp.Fori(1, PAIRS - 1) as m:
                pair(m)
            pair(PAIRS - 1)
            hold(sp, ctx_ok, STEPS)
            sp.dma_start(ctx_rows[PAIRS - 1][:, (NC - 1) * CH:], ctx_sb[:]).then_inc(ctx_out, 16)
            hold(sp, ctx_out, 16 * STEPS)

        def bounded_tensor(pe):
            def pv(s, b, j):
                pe.wait_ge(masked_ok, ST * s + j + 1)
                if j % 8 == 0:
                    pe.wait_ge(v_in[j // 8], 16 * (s // NC + 1))
                if j == 0:
                    wait(pe, out_copied, s)
                for h in range(2):
                    last = pe.matmul(po[h * HD:(h + 1) * HD, :], v_sb[:, j, h * HD:(h + 1) * HD],
                                     prob[:, j % PR, h, :], start=(j == 0), stop=(j == ST - 1))
                last.then_inc(pv_ok, 1)
                if j % 4 == 3:
                    g = j // 4
                    pe.wait_ge(sums_ok, ST // 2 * s + 2 * g + 2)
                    if g == 0:
                        wait(pe, den_taken, s)
                    for i in range(4):
                        last = pe.matmul(pl[32 * i:32 * i + 32, :], ones[:], psum2[:, (2 * g + i // 2) % GR, i % 2, :],
                                         start=(g == 0), stop=(g == ST // 4 - 1))
                    last.then_inc(den_ok, 1)

            def whole_den(s):
                pe.wait_ge(den_copied, s + 1)
                pe.matmul(pl[:], pick[:], den_sb[:], start=True, stop=True).then_inc(den_whole, 1)

            def body(s, b):
                first = isinstance(s, int) and s == 0
                for j in range(ST):
                    if j == 0:
                        pe.wait_ge(q_in[b], 64 * (s // 2 + 1))
                    if j % 8 == 0:
                        pe.wait_ge(k_in[j // 8], 32 * (s // NC + 1))
                    wait(pe, exp_ok, ST * s + (j - 2 if j >= 2 else j - 1))
                    for h in range(2):
                        k_tile = k_st[:, h, j * P:(j + 1) * P]
                        pe.matmul(sc[:, j % 3, h, :], k_tile, q_a[:, b, h, :], start=True, stop=False)
                        last = pe.matmul(sc[:, j % 3, h, :], k_tile, q_b[:, b, h, :], start=False, stop=True)
                    last.then_inc(scores_ok, 1)
                    if j >= LAG:
                        pv(s, b, j - LAG)
                    elif not first:
                        pv(s - 1, 1 - b, ST + j - LAG)
                    if j == LAG + 1 and not first:
                        whole_den(s - 1)

            over_steps(pe, body)
            for j in range(ST - LAG, ST):
                pv(STEPS - 1, 1, j)
            whole_den(STEPS - 1)

        def bounded_scalar(act):
            def take(s):
                act.wait_ge(pv_ok, ST * s + ST)
                wait(act, ctx_ok, s)
                act.copy(out_sb[:], po[:]).then_inc(out_copied, 1)
                act.wait_ge(den_ok, ST // 4 * s + ST // 4)
                wait(act, den_whole, s)
                act.copy(den_sb[:], pl[:]).then_inc(den_copied, 1)

            def take_whole(s):
                act.wait_ge(den_whole, s + 1)
                wait(act, ctx_ok, s)
                act.copy(den_all[:], pl[:]).then_inc(den_taken, 1)

            def body(s, b):
                first = isinstance(s, int) and s == 0
                for j in range(ST):
                    act.wait_ge(scores_ok, ST * s + j + 1)
                    wait(act, pv_ok, ST * s + j - PR + 1)
                    wait(act, sums_ok, ST // 2 * s + (j - PR) // 2 + 1)
                    act.activation(prob[:, j % PR], sc[:, j % 3], ACT.Exp,
                                   bias=keep["minus_bound"][:, 0:1]).then_inc(exp_ok, 1)
                    if j == LAG - 1 and not first:
                        take(s - 1)
                    if j == LAG + 1 and not first:
                        take_whole(s - 1)

            over_steps(act, body)
            take(STEPS - 1)
            take_whole(STEPS - 1)

        def bounded_vector(dve):
            def finish(s, k):
                finish_op(dve, s, k, s // NC, finish_step, den_taken, out_copied, ctx_ok)

            def body(s, b):
                first = isinstance(s, int) and s == 0
                dve.wait_ge(edge_in[b], 16 * (s // 2 + 1))
                for j in range(ST):
                    dve.wait_ge(exp_ok, ST * s + j + 1)
                    dve.tensor_tensor(prob[:, j % PR], prob[:, j % PR],
                                      edge[:, b, j, :].unsqueeze(1).broadcast_to([P, 2, CH]),
                                      ALU.mult).then_inc(masked_ok, 1)
                    if j % 2 == 1:
                        r = j // 2
                        dve.wait_ge(masked_ok, ST * s + j + 1)
                        wait(dve, den_ok, ST // 4 * s + (r - GR) // 2 + 1)
                        dve.tensor_tensor(psum2[:, r % GR], prob[:, (j - 1) % PR], prob[:, j % PR],
                                          ALU.add).then_inc(sums_ok, 1)
                    if 0 <= j - LAG - 3 < FINISH and not first:
                        finish(s - 1, j - LAG - 3)

            over_steps(dve, body)
            for k in range(FINISH):
                finish(STEPS - 1, k)

        hold_cf = start_holds(pick_ok, 1)

        def careful_sync(sp):
            with sp.Fori(0, PAIRS) as m:
                with sp.Fori(0, NC) as c:
                    s = NC * m + c
                    for half, part in ((slice(0, HD), "k_hi"), (slice(HD, P), "k_lo")):
                        sp.dma_start(k_st[half].bitcast(F32), qk[part][m]).then_inc(cf_in, 16)
                    for t, top, low in ((q_a, "q_hi", "q_lo"), (q_b, "q_lo", "q_hi")):
                        for half, part in ((slice(0, HD), top), (slice(HD, P), low)):
                            sp.dma_start(t[half, 0].bitcast(F32),
                                         qk[part][m][:, :, bass.ts(c, CH)]).then_inc(cf_in, 16)
                    sp.dma_start(v_sb[:], v_rows[m]).then_inc(cf_in, 16)
                    sp.dma_start(edge[:, 0], scr["edge_t"][c]).then_inc(cf_in, 16)
                    for q in range(QT):
                        hold_cf(sp, pre_bias, QT * s + q + 1)
                        sp.dma_start(adj_rows, adj_blocks[QT * c + q]).then_inc(cf_adj, 16)
                    hold_cf(sp, cf_minus, s + 1)
                    sp.dma_start(shift_cols, minus_max[:], allow_slow_non_contiguous=True).then_inc(shift_out, 16)
                    hold_cf(sp, shift_out, 16 * s + 16)
                    sp.dma_start(psum2[:, 0], shift_row.partition_broadcast(P)).then_inc(shift_in, 16)
                    hold_cf(sp, pre_ctx, s + 2)
                    sp.dma_start(ctx_rows[m][:, bass.ts(c, CH)], ctx_sb[:]).then_inc(cf_out, 16)
                    hold_cf(sp, cf_out, 16 * s + 16)

        def careful_tensor(pe):
            with pe.Fori(0, STEPS) as s:
                pe.wait_ge(cf_in, 128 * s + 128)
                for q in range(QT):
                    for h in range(2):
                        for n in range(N // CH):
                            at = (2 * q + h) * (N // CH) + n
                            pe.wait_ge(pre_added, 64 * s + at + 1)
                            pe.matmul(sc[:, n % 2, 0, :], q_a[:, 0, h, q * P:(q + 1) * P],
                                      k_st[:, h, n * CH:(n + 1) * CH], start=True, stop=True).then_inc(cf_rough, 1)
                pe.wait_ge(cf_shift, s + 1)
                for j in range(ST):
                    pe.wait_ge(pre_clamped, ST * s + j + 1)
                    for h in range(2):
                        k_tile = k_st[:, h, j * P:(j + 1) * P]
                        pe.matmul(sc[:, 2, h, :], k_tile, q_a[:, 0, h, :], start=True, stop=False)
                        pe.matmul(sc[:, 2, h, :], k_tile, q_b[:, 0, h, :], start=False, stop=False)
                        last = pe.matmul(sc[:, 2, h, :], spread[:], shift[:, h, :], start=False, stop=True)
                    last.then_inc(cf_scores, 1)
                    pe.wait_ge(cf_masked, ST * s + j + 1)
                    for h in range(2):
                        i = h + 2 * (j % 2)
                        pe.matmul(po[h * HD:(h + 1) * HD, :], v_sb[:, j, h * HD:(h + 1) * HD], prob[:, 0, h, :],
                                  start=(j == 0), stop=(j == ST - 1))
                        last = pe.matmul(pl[32 * i:32 * i + 32, :], ones[:], prob[:, 0, h, :],
                                         start=(j < 2), stop=(j >= ST - 2))
                    last.then_inc(pre_pv, 1)
                pe.wait_ge(cf_taken, s + 1)
                pe.matmul(pl[:], pick[:], den_sb[:], start=True, stop=True).then_inc(cf_den, 1)

        def careful_scalar(act):
            with act.Fori(0, STEPS) as s:
                for j in range(ST):
                    act.wait_ge(pre_clamped, ST * s + j + 2)
                    act.activation(prob[:, 0], prob[:, 0], ACT.Exp).then_inc(cf_exp, 1)
                act.wait_ge(pre_pv, ST * s + ST + 1)
                act.copy(out_sb[:], po[:]).then_inc(cf_out_sb, 1)
                act.copy(den_sb[:], pl[:]).then_inc(cf_taken, 1)
                act.wait_ge(cf_den, s + 1)
                act.copy(den_all[:], pl[:]).then_inc(cf_den_all, 1)

        def careful_vector(dve):
            for t, count in ((pre_bias, 1), (pre_added, 2), (pre_max, 1), (pre_top, 1), (pre_clamped, 1), (pre_pv, 1),
                             (pre_ctx, 1)):
                dve.sem_inc(t, count)
            with dve.Fori(0, STEPS) as s:
                for q in range(QT):
                    dve.wait_ge(cf_adj, 16 * QT * s + 16 * q + 16)
                    dve.wait_ge(pre_added, 64 * s + 16 * q + 2)
                    dve.tensor_scalar(bias[:], adj_rows, 0, NEG, ALU.is_equal, ALU.mult).then_inc(pre_bias, 1)
                    dve.wait_ge(pre_bias, QT * s + q + 2)
                    for h in range(2):
                        i = 2 * q + h
                        for n in range(N // CH):
                            at = i * (N // CH) + n
                            dve.wait_ge(cf_rough, 64 * s + at + 1)
                            dve.wait_ge(pre_max, 64 * s + at + 1)
                            dve.tensor_tensor(psum2[:, 1, 0, :], sc[:, n % 2, 0, :], bias[:, n * CH:(n + 1) * CH],
                                              ALU.add).then_inc(pre_added, 1)
                            dve.wait_ge(pre_added, 64 * s + at + 3)
                            if n == 0:
                                dve.wait_ge(pre_top, 8 * s + i + 1)
                            dve.reduce_max(part_max[:, n:n + 1], psum2[:, 1, 0, :], AX_X).then_inc(pre_max, 1)
                        dve.wait_ge(pre_max, 64 * s + 8 * i + 9)
                        dve.reduce_max(top[:, h, q:q + 1], part_max[:], AX_X).then_inc(pre_top, 1)
                dve.wait_ge(pre_top, 8 * s + 9)
                dve.tensor_scalar(minus_max[:], top[:], -1.0, None, ALU.mult).then_inc(cf_minus, 1)
                dve.wait_ge(shift_in, 16 * s + 16)
                dve.tensor_copy(shift[:], psum2[:, 0]).then_inc(cf_shift, 1)
                for j in range(ST):
                    dve.wait_ge(cf_scores, ST * s + j + 1)
                    dve.wait_ge(pre_pv, ST * s + j + 1)
                    dve.tensor_scalar(prob[:, 0], sc[:, 2], CLAMP, None, ALU.min).then_inc(pre_clamped, 1)
                    dve.wait_ge(cf_exp, ST * s + j + 1)
                    dve.tensor_tensor(prob[:, 0], prob[:, 0],
                                      edge[:, 0, j, :].unsqueeze(1).broadcast_to([P, 2, CH]),
                                      ALU.mult).then_inc(cf_masked, 1)
                for k in range(FINISH):
                    finish_op(dve, s, k, s // NC, cf_fin, cf_den_all, cf_out_sb, pre_ctx)

        def branch(eng, bounded, careful):
            flag = eng.value_load(keep["bounded_i"][0:1, 0:1], min_val=0, max_val=1)
            with eng.If(flag > 0):
                bounded(eng)
            with eng.Else():
                careful(eng)

        block = ctx.enter_context(nc.Block())

        @block.sync
        def _(sp):
            branch(sp, bounded_sync, careful_sync)

        @block.gpsimd
        def _(pool):
            pool.memset(ones[:], 1.0).then_inc(consts_ok, 1)

            hold_w = start_holds(consts_ok, 1)

            def split_pieces(first, count, src, hi, lo):
                with pool.Fori(0, count) as i:
                    n = first + i
                    pool.dma_start(w_raw[:], src(i)).then_inc(w_raw_in, 16)
                    hold_w(pool, w_raw_in, 16 * n + 16)
                    pool.tensor_copy(w_hi[:], w_raw[:]).then_inc(w_hi_ok, 1)
                    hold_w(pool, w_hi_ok, n + 1)
                    pool.tensor_tensor(w_lo[:], w_raw[:], w_hi[:].bitcast(F32), ALU.subtract).then_inc(w_lo_ok, 1)
                    pool.dma_start(hi(i), w_hi[:].bitcast(F32)).then_inc(w_out, 16)
                    hold_w(pool, w_lo_ok, n + 1)
                    pool.dma_start(lo(i), w_lo[:].bitcast(F32)).then_inc(w_out, 16)
                    hold_w(pool, w_out, 32 * n + 32)

            for k in range(KT):
                split_pieces(F // CH * k, F // CH, *(lambda i, t=t, k=k: t[k * P:(k + 1) * P, bass.ts(i, CH)]
                                                     for t in (io["W1"], scr["w1_hi"], scr["w1_lo"])))
            split_pieces(KT * F // CH, FT, *(lambda i, t=t: t[bass.ts(i, P), :] for t in (io["W2"], scr["w2_hi"], scr["w2_lo"])))

        @block.scalar
        def _(act):
            branch(act, bounded_scalar, careful_scalar)

        @block.vector
        def _(dve):
            dve.memset(ones_sq[:], 1.0 / P).then_inc(pick_ok, 1)
            dve.wait_ge(pick_ok, 1)
            dve.tensor_copy(spread[:], ones_sq[:]).then_inc(pick_ok, 1)
            dve.memset(pick[:], 0.0).then_inc(pick_ok, 1)
            dve.wait_ge(pick_ok, 3)
            for i in range(4):
                h = i % 2
                dve.memset(pick[32 * i:32 * i + 1, h * HD:(h + 1) * HD], 1.0).then_inc(pick_ok, 1)
            branch(dve, bounded_vector, careful_vector)

        @block.tensor
        def _(pe):
            pe.wait_ge(consts_ok, 1)
            pe.wait_ge(pick_ok, 7)
            branch(pe, bounded_tensor, careful_tensor)


DLAG = 3
GR4 = 4


def feed(nc, io, scr, keep):
    with ExitStack() as ctx:
        def sb(name, shape, dt):
            return ctx.enter_context(nc.sbuf_tensor(name, shape, dt))

        def ps(name, shape, dt):
            return ctx.enter_context(nc.psum_tensor(name, shape, dt))

        sem = nc.alloc_semaphore

        wo = sb("wo", [P, KT, D], F32)
        w1_hi, w1_lo = (sb(n, [P, KT, F], F32R) for n in ("w1_hi", "w1_lo"))
        w2_hi, w2_lo = (sb(n, [P, FT, D], F32R) for n in ("w2_hi", "w2_lo"))
        bo_b, scale_b, bias_b = (sb(n, [P, D], F32) for n in ("bo_b", "ln2_scale_b", "ln2_bias_b"))
        nm_i = sb("nodemask2_i", [P, ST], I32)
        nm = sb("nodemask2_f", [P, ST], F32)
        ident = sb("ident2", [P, P], F32)
        minus_half = sb("minus_half2", [P, QT], F32)
        eps_t = sb("eps2", [P, QT], F32)
        ctxt = sb("ctx_in", [P, 2, KT, P], F32)
        rows = sb("rows", [P, 2, QT, D], F32)
        xr = sb("x_rows", [P, QT, D], F32)
        h2t_hi, h2t_lo = (sb(n, [P, KT, CH], F32R) for n in ("h2t_hi", "h2t_lo"))
        g32 = sb("gelu", [P, 2, CH], F32)
        g_hi, g_lo = (sb(n, [P, GR4, CH], F32R) for n in ("gelu_hi", "gelu_lo"))
        stats = sb("stats2", [P, 2, QT, 6], F32)
        mv = sb("mv2", [P, 2, QT, 2], F32)
        var_e = sb("var_e2", [P, 2, QT], F32)
        rstd = sb("rstd2", [P, 2, QT], F32)
        rstd_m = sb("rstd_m2", [P, QT], F32)

        attn_ps = ps("attn_ps", [P, D], F32)
        turn_ps = ps("turn2_ps", [P, KT, P], F32)
        up_ps = ps("up_ps", [P, 2, CH], F32)
        down_ps = ps("down_ps", [P, QT, D], F32)

        consts_in = sem("f_consts_in")
        w_in = [sem(f"w_in{g}") for g in range(4)]
        ctx_in = [sem(f"ctx_in{i}") for i in range(2)]
        ht_in, xr_in = sem("ht_in"), sem("xr_in")
        ident_zero, ident_ok, consts_ok = sem("f_ident_zero"), sem("f_ident_ok"), sem("f_consts_ok")
        attn_ok, h1_step, h1_ok, h2_step, h2_ok = (sem(n) for n in ("attn_ok", "h1_step", "h1_ok", "h2_step", "h2_ok"))
        stats_ok, mv_ok, var_ok, rstd_ok = (sem("f_" + n) for n in ("stats_ok", "mv_ok", "var_ok", "rstd_ok"))
        turned, h2t_hi_ok, h2t_lo_ok, up_ok, gelu_ok, g_lo_ok, down_ok = (sem(n) for n in (
            "f_turned", "h2t_hi_ok", "h2t_lo_ok", "up_ok", "gelu_ok", "g_lo_ok", "down_ok"))
        y_taken, y_ok, out_ok, out_done = (sem(n) for n in ("y_taken", "y_ok", "out_ok", "out_done"))

        x_rows = io["x"].rearrange("(c q p) d -> c p q d", p=P, q=QT)
        ht_rows = scr["ht"].rearrange("(c q p) d -> c p q d", p=P, q=QT)
        out_rows = io["out"].rearrange("(c q p) d -> c p q d", p=P, q=QT)
        ctx_tiles = scr["ctx"].rearrange("(k p) t -> p k t", p=P)

        def wait(eng, s, value):
            if not isinstance(value, int) or value > 0:
                eng.wait_ge(s, value)

        def is_first(c):
            return isinstance(c, int) and c == 0

        def is_last(c):
            return isinstance(c, int) and c == NC - 1

        def over_chunks(eng, body):
            body(0, 0)
            body(1, 1)
            with eng.Fori(1, NC // 2 - 1) as i:
                body(2 * i, 0)
                body(2 * i + 1, 1)
            body(NC - 2, 0)
            body(NC - 1, 1)

        def order_h1(c):
            return 0 if is_first(c) else 2 * c - 1

        def order_y(c):
            return 2 * NC - 1 if is_last(c) else 2 * c + 2

        block = ctx.enter_context(nc.Block())
        hold = start_holds(consts_in, 16 * 5)

        @block.sync
        def _(sp):
            def load_ctx(c, q):
                sp.dma_start(ctxt[:, q % 2], ctx_tiles[:, :, bass.ts(QT * c + q, P)]).then_inc(ctx_in[q % 2], 16)

            def load_ht(c, b):
                sp.dma_start(rows[:, b], ht_rows[c]).then_inc(ht_in, 16)

            def load_x(c):
                sp.dma_start(xr[:], x_rows[c]).then_inc(xr_in, 16)

            load_ctx(0, 0)
            sp.dma_start(wo[:], io["Wo"].rearrange("(k p) n -> p k n", p=P)).then_inc(consts_in, 16)
            load_ctx(0, 1)
            load_ht(0, 0)
            sp.dma_start(bo_b[:], io["bo"].partition_broadcast(P)).then_inc(consts_in, 16)
            sp.dma_start(nm_i[:], io["nodemask"].rearrange("(t p) -> p t", p=P), allow_slow_non_contiguous=True).then_inc(consts_in, 16)
            sp.dma_start(scale_b[:], io["ln2_scale"].partition_broadcast(P)).then_inc(consts_in, 16)
            sp.dma_start(bias_b[:], io["ln2_bias"].partition_broadcast(P)).then_inc(consts_in, 16)
            for g in range(4):
                cols, tiles = bass.ts(g, F // 4), slice(g * FT // 4, (g + 1) * FT // 4)
                for t, n in ((w1_hi, "w1_hi"), (w1_lo, "w1_lo")):
                    src = scr[n].rearrange("(k p) n -> p k n", p=P)
                    sp.dma_start(t[:, :, cols].bitcast(F32), src[:, :, cols]).then_inc(w_in[g], 16)
                for t, n in ((w2_hi, "w2_hi"), (w2_lo, "w2_lo")):
                    src = scr[n].rearrange("(k p) n -> p k n", p=P)
                    sp.dma_start(t[:, tiles].bitcast(F32), src[:, tiles]).then_inc(w_in[g], 16)
                if g == 0:
                    for q in range(2, QT):
                        hold(sp, attn_ok, q - 1)
                        load_ctx(0, q)
            hold(sp, ht_in, 16)
            load_ht(1, 1)
            load_x(0)

            def body(c, b):
                if not is_last(c):
                    for q in range(2):
                        hold(sp, attn_ok, QT * c + q + 3)
                        load_ctx(c + 1, q)
                if not is_first(c):
                    hold(sp, y_ok, QT * c)
                    load_x(c)
                    hold(sp, out_ok, QT * c)
                    sp.dma_start(out_rows[c - 1], rows[:, 1 - b]).then_inc(out_done, 16)
                    if not is_last(c):
                        hold(sp, out_done, 16 * c)
                        load_ht(c + 1, 1 - b)
                if not is_last(c):
                    for q in range(2, QT):
                        hold(sp, attn_ok, QT * (c + 1) + q - 1)
                        load_ctx(c + 1, q)

            over_chunks(sp, body)
            hold(sp, out_ok, QT * NC)
            sp.dma_start(out_rows[NC - 1], rows[:, 1]).then_inc(out_done, 16)
            hold(sp, out_done, 16 * NC)

        @block.gpsimd
        def _(pool):
            pool.memset(ident[:], 0.0).then_inc(ident_zero, 1)
            pool.memset(minus_half[:], -0.5).then_inc(ident_zero, 1)
            pool.memset(eps_t[:], EPS).then_inc(ident_zero, 1)
            pool.wait_ge(ident_zero, 3)
            pool.affine_select(out=ident[:], in_=ident[:], compare_op=ALU.not_equal, fill=1.0, base=0,
                               pattern=[[-1, P]], channel_multiplier=1).then_inc(ident_ok, 1)

            def inverse_std(n, which):
                pool.wait_ge(mv_ok, 4 * n + 4)
                pool.tensor_tensor(var_e[:, which, :], mv[:, which, :, 1], eps_t[:], ALU.add).then_inc(var_ok, 1)
                pool.wait_ge(var_ok, n + 1)
                pool.tensor_tensor(rstd[:, which, :], var_e[:, which, :], minus_half[:], ALU.pow).then_inc(rstd_ok, 1)

            inverse_std(0, 0)

            def body(c, b):
                if not is_first(c):
                    inverse_std(order_y(c - 1), 1)
                if not is_last(c):
                    inverse_std(order_h1(c + 1), 0)

            over_chunks(pool, body)
            inverse_std(order_y(NC - 1), 1)

        @block.scalar
        def _(act):
            def take_turned(c, q):
                act.wait_ge(turned, QT * c + q + 1)
                act.copy(h2t_hi[:, :, q * P:(q + 1) * P], turn_ps[:]).then_inc(h2t_hi_ok, 1)

            def body(c, b):
                for f in range(FT):
                    act.wait_ge(up_ok, FT * c + f + 1)
                    wait(act, g_lo_ok, FT * c + f - 1)
                    act.activation(g32[:, f % 2, :], up_ps[:, f % 2, :], ACT.Gelu_apprx_tanh)
                    wait(act, down_ok, FT * QT * c + QT * (f - GR4) + QT)
                    act.activation(g_hi[:, f % GR4, :], up_ps[:, f % 2, :], ACT.Gelu_apprx_tanh).then_inc(gelu_ok, 1)
                if not is_last(c):
                    for q in range(QT):
                        take_turned(c + 1, q)

            for q in range(QT):
                take_turned(0, q)
            over_chunks(act, body)

        @block.vector
        def _(dve):
            dve.wait_ge(consts_in, 16 * 5)
            dve.tensor_scalar(nm[:], nm_i[:], 1, None, ALU.is_equal).then_inc(consts_ok, 1)
            dve.wait_ge(consts_ok, 1)

            def moments(n, which, q, b):
                dve.bn_stats(stats[:, which, q, :], rows[:, b, q, :]).then_inc(stats_ok, 1)
                count = 4 * n + q + 1
                if not isinstance(count, int):
                    dve.compute_val(count)
                dve.wait_ge(consts_ok, 1)
                dve.wait_ge(stats_ok, count)
                dve.bn_aggr(mv[:, which, q, :], stats[:, which, q, :]).then_inc(mv_ok, 1)

            def add_attn(c, b, q):
                col = nm[:, bass.ds(c * QT + q, 1)]
                if q == 0:
                    dve.wait_ge(ht_in, 16 * (c + 1))
                dve.wait_ge(attn_ok, QT * c + q + 1)
                dve.scalar_tensor_tensor(rows[:, b, q, :], attn_ps[:], col, rows[:, b, q, :],
                                         ALU.mult, ALU.add).then_inc(h1_step, 1)
                dve.wait_ge(h1_step, QT * c + q + 1)
                dve.scalar_tensor_tensor(rows[:, b, q, :], bo_b[:], col, rows[:, b, q, :],
                                         ALU.mult, ALU.add).then_inc(h1_ok, 1)
                dve.wait_ge(h1_ok, QT * c + q + 1)
                moments(order_h1(c), 0, q, b)

            def norm_h1(c, b, q):
                if q == 0:
                    dve.wait_ge(rstd_ok, order_h1(c) + 1)
                    dve.tensor_tensor(rstd_m[:], rstd[:, 0, :], nm[:, bass.ts(c, QT)], ALU.mult).then_inc(h2_step, 1)
                dve.wait_ge(h2_step, 9 * c + 2 * q + 1)
                dve.tensor_scalar(rows[:, b, q, :], rows[:, b, q, :], mv[:, 0, q, 0:1],
                                  rstd_m[:, q:q + 1], ALU.subtract, ALU.mult).then_inc(h2_step, 1)
                dve.wait_ge(h2_step, 9 * c + 2 * q + 2)
                dve.tensor_tensor(rows[:, b, q, :], rows[:, b, q, :], scale_b[:], ALU.mult).then_inc(h2_step, 1)
                dve.wait_ge(h2_step, 9 * c + 2 * q + 3)
                dve.scalar_tensor_tensor(rows[:, b, q, :], bias_b[:], nm[:, bass.ds(c * QT + q, 1)],
                                         rows[:, b, q, :], ALU.mult, ALU.add).then_inc(h2_ok, 1)

            def turned_lo(c, q):
                dve.wait_ge(h2t_hi_ok, QT * c + q + 1)
                cols = slice(q * P, (q + 1) * P)
                dve.tensor_tensor(h2t_lo[:, :, cols], turn_ps[:], h2t_hi[:, :, cols].bitcast(F32),
                                  ALU.subtract).then_inc(h2t_lo_ok, 1)

            def take_y(c, b, q):
                dve.wait_ge(down_ok, FT * QT * c + QT * (FT - 1) + q + 1)
                dve.tensor_tensor(rows[:, b, q, :], down_ps[:, q, :], rows[:, b, q, :], ALU.add).then_inc(y_taken, 1)

            def add_x(c, b, q):
                if q == 0:
                    dve.wait_ge(xr_in, 16 * (c + 1))
                dve.wait_ge(y_taken, QT * c + q + 1)
                dve.tensor_tensor(rows[:, b, q, :], rows[:, b, q, :], xr[:, q, :], ALU.add).then_inc(y_ok, 1)
                dve.wait_ge(y_ok, QT * c + q + 1)
                moments(order_y(c), 1, q, b)

            def norm_y(c, b, q):
                if q == 0:
                    dve.wait_ge(rstd_ok, order_y(c) + 1)
                dve.tensor_scalar(rows[:, b, q, :], rows[:, b, q, :], mv[:, 1, q, 0:1], rstd[:, 1, q:q + 1],
                                  ALU.subtract, ALU.mult).then_inc(out_ok, 1)

            def body(c, b):
                for f in range(FT):
                    dve.wait_ge(gelu_ok, FT * c + f + 1)
                    dve.tensor_tensor(g_lo[:, f % GR4, :], g32[:, f % 2, :], g_hi[:, f % GR4, :].bitcast(F32),
                                      ALU.subtract).then_inc(g_lo_ok, 1)
                    if not is_first(c):
                        if f < 4:
                            add_x(c - 1, 1 - b, f)
                        elif f < 6:
                            norm_y(c - 1, 1 - b, 2 * (f - 4))
                            norm_y(c - 1, 1 - b, 2 * (f - 4) + 1)
                    if not is_last(c):
                        if 8 <= f < 12:
                            add_attn(c + 1, 1 - b, f - 8)
                        elif f >= 12:
                            norm_h1(c + 1, 1 - b, f - 12)
                if not is_last(c):
                    for q in range(QT):
                        turned_lo(c + 1, q)
                for q in range(QT):
                    take_y(c, b, q)

            for q in range(QT):
                add_attn(0, 0, q)
            for q in range(QT):
                norm_h1(0, 0, q)
            for q in range(QT):
                turned_lo(0, q)
            over_chunks(dve, body)
            for q in range(QT):
                add_x(NC - 1, 1, q)
            for q in range(QT):
                norm_y(NC - 1, 1, q)

        @block.tensor
        def _(pe):
            def attn(c, q):
                pe.wait_ge(ctx_in[q % 2], 16 * (2 * c + q // 2 + 1))
                wait(pe, h1_step, QT * c + q)
                for k in range(KT):
                    last = pe.matmul(attn_ps[:], ctxt[:, q % 2, k, :], wo[:, k, :],
                                     start=(k == 0), stop=(k == KT - 1))
                last.then_inc(attn_ok, 1)

            def turn(c, b, q):
                pe.wait_ge(h2_ok, QT * c + q + 1)
                wait(pe, h2t_lo_ok, QT * c + q)
                for k in range(KT):
                    last = pe.transpose(turn_ps[:, k, :], rows[:, b, q, k * P:(k + 1) * P], ident[:])
                last.then_inc(turned, 1)

            def up(c, f):
                if f == 0:
                    pe.wait_ge(h2t_lo_ok, QT * c + QT)
                if is_first(c) and f % 4 == 0:
                    pe.wait_ge(w_in[f // 4], 64)
                wait(pe, gelu_ok, FT * c + f - 1)
                cols = slice(f * P, (f + 1) * P)
                for k in range(KT):
                    for i, (w, h) in enumerate(((w1_hi, h2t_hi), (w1_hi, h2t_lo), (w1_lo, h2t_hi))):
                        last = pe.matmul(up_ps[:, f % 2, :], w[:, k, cols], h[:, k, :],
                                         start=(k == 0 and i == 0), stop=(k == KT - 1 and i == 2))
                last.then_inc(up_ok, 1)

            def down(c, f):
                pe.wait_ge(g_lo_ok, FT * c + f + 1)
                for q in range(QT):
                    if f == 0:
                        wait(pe, y_taken, QT * (c - 1) + q + 1)
                    cols = slice(q * P, (q + 1) * P)
                    for i, (g, w) in enumerate(((g_hi, w2_hi), (g_hi, w2_lo), (g_lo, w2_hi))):
                        last = pe.matmul(down_ps[:, q, :], g[:, f % GR4, cols], w[:, f, :],
                                         start=(f == 0 and i == 0), stop=(f == FT - 1 and i == 2))
                    last.then_inc(down_ok, 1)

            def body(c, b):
                for f in range(FT):
                    up(c, f)
                    if 7 <= f < 11 and not is_last(c):
                        attn(c + 1, f - 7)
                    if f >= DLAG:
                        down(c, f - DLAG)
                for i in range(DLAG):
                    if not is_last(c):
                        turn(c + 1, 1 - b, i)
                    down(c, FT - DLAG + i)
                if not is_last(c):
                    turn(c + 1, 1 - b, DLAG)

            pe.wait_ge(ident_ok, 1)
            pe.wait_ge(consts_in, 16 * 5)
            for q in range(QT):
                attn(0, q)
            for q in range(QT):
                turn(0, 0, q)
            over_chunks(pe, body)


def program(nc, io):
    def scratch(name, shape, dt=F32):
        return nc.dram_tensor(name, shape, dt, kind="Internal").ap()

    scr = {n: scratch("scr_" + n, (D, N)) for n in ("k_hi", "k_lo", "q_hi", "q_lo", "ctx")}
    scr["v"] = scratch("scr_v", (N, D))
    scr["ht"] = scratch("scr_ht", (N, D))
    scr.update({n: scratch("scr_" + n, (D, F)) for n in ("w1_hi", "w1_lo")})
    scr.update({n: scratch("scr_" + n, (F, D)) for n in ("w2_hi", "w2_lo")})
    scr["shift"] = scratch("scr_shift", (2, QT, P))
    scr["edge_t"] = scratch("scr_edge_t", (NC, P, ST, CH), U8)
    with ExitStack() as ctx:
        keep = {"v_tot": ctx.enter_context(nc.sbuf_tensor("v_tot", [P, PAIRS], F32)),
                "minus_bound": ctx.enter_context(nc.sbuf_tensor("minus_bound", [P, 1], F32)),
                "bounded_f": ctx.enter_context(nc.sbuf_tensor("bounded_f", [1, 1], F32)),
                "bounded_i": ctx.enter_context(nc.sbuf_tensor("bounded_i", [1, 1], I32))}
        project(nc, io, scr, keep)
        attend(nc, io, scr, keep)
        feed(nc, io, scr, keep)


_INS = ["x", "adj", "nodemask", "h_target", "ln1_scale", "ln1_bias", "Wq", "bq", "Wk", "bk", "Wv", "bv",
        "Wo", "bo", "ln2_scale", "ln2_bias", "W1", "W2"]


def kernel(**inputs):
    import numpy as np
    import concourse.bacc as bacc
    from concourse.bass_utils import run_bass_kernel_spmd

    nc = bacc.Bacc("TRN2", target_bir_lowering=False, num_devices=1)
    arrays, io = {}, {}
    for name in _INS:
        a = np.ascontiguousarray(inputs.get(name, inputs.get("L0_gnn_" + name)))
        arrays["in_" + name] = a
        io[name] = nc.dram_tensor("in_" + name, a.shape, mybir.dt.from_np(a.dtype), kind="ExternalInput").ap()
    io["out"] = nc.dram_tensor("out", (N, D), F32, kind="ExternalOutput").ap()
    program(nc, io)
    return run_bass_kernel_spmd(nc, [arrays], core_ids=[0]).results[0]["out"]
```

```python
from contextlib import ExitStack

import concourse.bass as bass
from concourse import mybir

ALU = mybir.AluOpType
ACT = mybir.ActivationFunctionType
AX_X = mybir.AxisListType.X
F32 = mybir.dt.float32
F32R = mybir.dt.float32r
BF16 = mybir.dt.bfloat16
I32 = mybir.dt.int32
U8 = mybir.dt.uint8
RMAX = bass.bass_isa.ReduceOp.max

P = 128
N = 4096
D = 512
H = 8
HD = D // H
F = 4 * D
KT = D // P
CH = 512
NC = N // CH
QT = CH // P
ST = N // P
PAIRS = H // 2
FT = F // P
EPS = 1e-5
NEG = -1e30
QSCALE = HD ** -0.5
BOUND_MAX = 40.0
NORM_SLACK = 1.05
CLAMP = 60.0


def start_holds(ready, count=16):
    def hold(eng, s, value):
        if isinstance(value, int):
            if value > 0:
                eng.wait_ge(s, value)
            return
        eng.compute_val(value)
        eng.wait_ge(ready, count)
        eng.wait_ge(s, value)
    return hold


KS = 4
MASKS_K = [(), (), (), (0,)]
MASKS_V = [(1, 2), (3, 4), (5, 6), (7,)]
MASKS_Q = [(8, 9), (10, 11), (12, 13), (14, 15)]
NLAG = 3


def project(nc, io, scr, keep):
    with ExitStack() as ctx:
        def sb(name, shape, dt):
            return ctx.enter_context(nc.sbuf_tensor(name, shape, dt))

        def ps(name, shape, dt):
            return ctx.enter_context(nc.psum_tensor(name, shape, dt))

        sem = nc.alloc_semaphore

        wk, wv, wq = ([sb(f"{n}_{part}", [P, KT, D], F32R) for part in ("hi", "lo")] for n in ("wk", "wv", "wq"))
        scale_b, bias_b, bv_b = (sb(n, [P, D], F32) for n in ("ln1_scale_b", "ln1_bias_b", "bv_b"))
        bk_col, bq_col, bqs_col = (sb(n, [P, PAIRS], F32) for n in ("bk_col", "bq_col", "bqs_col"))
        nm_i = sb("nodemask_i", [P, ST], I32)
        nm = sb("nodemask_f", [P, ST], F32)
        ident = sb("ident", [P, P], F32)
        ident_h = sb("ident_h", [P, P], BF16)
        halves = sb("halves", [P, P], BF16)
        minus_half = sb("minus_half", [P, QT], F32)
        eps_t = sb("eps", [P, QT], F32)
        z = [sb(f"z{s}", [P, QT, D], F32) for s in range(2)]
        zt_hi, zt_lo = ([sb(f"zt_{part}{s}", [P, KT, CH], F32R) for s in range(2)] for part in ("hi", "lo"))
        stats = sb("stats", [P, 2, QT, 6], F32)
        mv = sb("mv", [P, 2, QT, 2], F32)
        var_e = sb("var_e", [P, 2, QT], F32)
        rstd = sb("rstd", [P, 2, QT], F32)
        rstd_m = sb("rstd_m", [P, 2, QT], F32)
        adj = sb("adj_rows", [P, 2, N], I32)
        edge = sb("edge", [P, 2, N], BF16)
        edge_t = sb("edge_t", [P, ST, CH], U8)
        kq = sb("kq", [P, KS, CH], F32)
        kq_hi = sb("kq_hi", [P, KS, CH], F32R)
        kq_lo = sb("kq_lo", [P, KS, CH], F32R)
        kq_sq = sb("kq_sq", [P, KS, CH], BF16)
        norm_max = sb("norm_max", [P, 2, 1], F32)
        norm_new = sb("norm_new", [P, 2], F32)
        vv = sb("vv", [P, QT, D], F32)
        v_sum = sb("v_sum", [P, D], F32)
        one_col = sb("one_col", [P, 1], F32)
        bnd = sb("bnd", [P, 4], F32)
        all_max = sb("all_max", [P, 2], F32)

        early = [edge_t[:, i * ST // 2:(i + 1) * ST // 2].rearrange("p a b -> p (a b)").bitcast(F32) for i in range(2)]
        early.append(edge[:, 1].bitcast(F32))
        wk_raw, wv_raw, wq_raw = (t.rearrange("p (k n) -> p k n", k=KT) for t in early)

        turn_ps = ps("turn_ps", [P, 2, KT, P], F32)
        proj_ps = ps("proj_ps", [P, 2, CH], F32)
        edge_ps = ps("edge_ps", [P, 2, 8, P], BF16)
        norm_ps = ps("norm_ps", [P, 2, CH], F32)

        consts_in = sem("consts_in")
        w_in = [sem(f"wkvq_in{i}") for i in range(3)]
        x_in = [sem(f"x_in{s}") for s in range(2)]
        adj_in = [sem(f"adj_in{b}") for b in range(2)]
        ident_ok, ident_zero = sem("ident_ok"), sem("ident_zero")
        consts_ok, halves_ok = sem("consts_ok"), sem("halves_ok")
        stats_ok, mv_ok, var_ok, rstd_ok, z_step, z_scaled, z_ok = (sem(n) for n in (
            "stats_ok", "mv_ok", "var_ok", "rstd_ok", "z_step", "z_scaled", "z_ok"))
        turned, zt_hi_ok, zt_lo_ok = sem("turned"), sem("zt_hi_ok"), sem("zt_lo_ok")
        wkvq_hi_ok, wk_lo_ok, wvq_lo_ok = sem("wkvq_hi_ok"), sem("wk_lo_ok"), sem("wvq_lo_ok")
        proj_ok, kq_ok, v_ok, lo_ok = sem("proj_ok"), sem("kq_ok"), sem("v_ok"), sem("lo_ok")
        norm_ok, norm_read, norm_max_ok = sem("norm_ok"), sem("norm_read"), sem("norm_max_ok")
        kq_out = [sem(f"kq_out{b}") for b in range(KS)]
        v_out = [sem(f"v_out{b}") for b in range(QT)]
        v_sum_ok = sem("v_sum_ok")
        ht_out = sem("ht_out")
        edge_ok, edge_turned, edge_t_ok, edge_out = (sem(n) for n in (
            "edge_ok", "edge_turned", "edge_t_ok", "edge_out"))
        v_tot_ok, v_tot_kept = sem("v_tot_ok"), sem("v_tot_kept")
        bnd_ok, red_ok, pool_ok = sem("bnd_ok"), sem("red_ok"), sem("pool_ok")

        x_rows = [io["x"].rearrange("(c q p) d -> c p q d", p=P, q=QT),
                  io["h_target"].rearrange("(c q p) d -> c p q d", p=P, q=QT)]
        adj_rows = io["adj"].rearrange("(b p) s -> b p s", p=P)
        ht_rows = scr["ht"].rearrange("(c q p) d -> c p q d", p=P, q=QT)
        v_rows = scr["v"].rearrange("(b p) d -> b p d", p=P)

        def wait(eng, s, value):
            if not isinstance(value, int) or value > 0:
                eng.wait_ge(s, value)

        def over_chunks(eng, body):
            body(0)
            with eng.Fori(1, NC - 1) as c:
                body(c)
            body(NC - 1)

        block = ctx.enter_context(nc.Block())
        hold = start_holds(x_in[0])

        @block.sync
        def _(sp):
            def load_x(c, s):
                sp.dma_start(z[s][:], x_rows[s][c]).then_inc(x_in[s], 16)

            def load_adj(b, slot):
                sp.dma_start(adj[:, slot, :], adj_rows[b]).then_inc(adj_in[slot], 16)

            load_x(0, 0)
            sp.dma_start(nm_i[:], io["nodemask"].rearrange("(t p) -> p t", p=P), allow_slow_non_contiguous=True).then_inc(consts_in, 16)
            sp.dma_start(scale_b[:], io["ln1_scale"].partition_broadcast(P)).then_inc(consts_in, 16)
            sp.dma_start(bias_b[:], io["ln1_bias"].partition_broadcast(P)).then_inc(consts_in, 16)
            sp.dma_start(bk_col[:], io["bk"].rearrange("(m p) -> p m", p=P), allow_slow_non_contiguous=True).then_inc(consts_in, 16)
            sp.dma_start(bq_col[:], io["bq"].rearrange("(m p) -> p m", p=P), allow_slow_non_contiguous=True).then_inc(consts_in, 16)
            sp.dma_start(bv_b[:], io["bv"].partition_broadcast(P)).then_inc(consts_in, 16)
            load_x(0, 1)
            for i, (t, w) in enumerate(((wk_raw, "Wk"), (wv_raw, "Wv"), (wq_raw, "Wq"))):
                sp.dma_start(t, io[w].rearrange("(k p) n -> p k n", p=P)).then_inc(w_in[i], 16)
                if i < 2:
                    load_adj(i, i)

            def store_kq(c, i, side):
                b, m = i % KS, i % PAIRS
                hi, lo = (scr["k_hi"], scr["k_lo"]) if side == 0 else (scr["q_hi"], scr["q_lo"])
                hold(sp, lo_ok, 8 * c + i + 1)
                cols = bass.ts(c, CH)
                sp.dma_start(hi[m * P:(m + 1) * P, cols], kq_hi[:, b, :].bitcast(F32)).then_inc(kq_out[b], 16)
                sp.dma_start(lo[m * P:(m + 1) * P, cols], kq_lo[:, b, :].bitcast(F32)).then_inc(kq_out[b], 16)

            def body(c):
                more = not (isinstance(c, int) and c == NC - 1)
                if more:
                    hold(sp, turned, 8 * c + 4)
                    load_x(c + 1, 0)
                hold(sp, z_ok, 8 * c + 8)
                sp.dma_start(ht_rows[c], z[1][:]).then_inc(ht_out, 16)
                for i in range(2):
                    store_kq(c, i, 0)
                next_adj(c, 3)
                for i in range(2, 4):
                    store_kq(c, i, 0)
                for q in range(QT):
                    hold(sp, v_ok, 4 * c + q + 1)
                    sp.dma_start(v_rows[4 * c + q], vv[:, q, :]).then_inc(v_out[q], 16)
                    if q == 1 and more:
                        next_adj(c, 4)
                        hold(sp, turned, 8 * c + 8)
                        hold(sp, ht_out, 16 * c + 16)
                        load_x(c + 1, 1)
                if more:
                    next_adj(c, 5)
                for i in range(4, 8):
                    store_kq(c, i, 1)
                hold(sp, edge_t_ok, 16 * c + 16)
                sp.dma_start(scr["edge_t"][c], edge_t[:]).then_inc(edge_out, 16)
                if more:
                    next_adj(c, 6)

            def next_adj(c, k):
                hold(sp, edge_ok, 4 * c + k - 1)
                load_adj(4 * c + k, k % 2)

            next_adj(0, 2)
            over_chunks(sp, body)
            for b in range(KS):
                hold(sp, kq_out[b], 2 * 16 * (8 // KS) * NC)
            for q in range(QT):
                hold(sp, v_out[q], 16 * NC)
            for s in (ht_out, edge_out):
                hold(sp, s, 16 * NC)

        @block.gpsimd
        def _(pool):
            for t in (ident, ident_h):
                pool.memset(t[:], 0.0).then_inc(ident_zero, 1)
            pool.memset(minus_half[:], -0.5).then_inc(ident_zero, 1)
            pool.memset(eps_t[:], EPS).then_inc(ident_zero, 1)
            pool.memset(v_sum[:], 0.0).then_inc(ident_zero, 1)
            pool.wait_ge(ident_zero, 5)
            for t in (ident, ident_h):
                pool.affine_select(out=t[:], in_=t[:], compare_op=ALU.not_equal, fill=1.0, base=0,
                                   pattern=[[-1, P]], channel_multiplier=1).then_inc(ident_ok, 1)

            def inverse_std(c, s):
                pool.wait_ge(mv_ok, 8 * c + 4 * s + 4)
                pool.tensor_tensor(var_e[:, s, :], mv[:, s, :, 1], eps_t[:], ALU.add).then_inc(var_ok, 1)
                pool.wait_ge(var_ok, 2 * c + s + 1)
                pool.tensor_tensor(rstd[:, s, :], var_e[:, s, :], minus_half[:], ALU.pow).then_inc(rstd_ok, 1)

            def times_scale(c, s):
                for q in range(QT):
                    pool.wait_ge(z_step, 10 * c + 5 * s + 2 + q)
                    pool.tensor_tensor(z[s][:, q, :], z[s][:, q, :], scale_b[:], ALU.mult).then_inc(z_scaled, 1)

            def add_values(c, tiles):
                for q in tiles:
                    pool.wait_ge(v_ok, 4 * c + q + 1)
                    wait(pool, v_sum_ok, 4 * c + q)
                    pool.tensor_tensor(v_sum[:], v_sum[:], vv[:, q, :], ALU.add).then_inc(v_sum_ok, 1)

            def body(c):
                more = not (isinstance(c, int) and c == NC - 1)
                times_scale(c, 1)
                if more:
                    inverse_std(c + 1, 0)
                add_values(c, range(2))
                if more:
                    times_scale(c + 1, 0)
                add_values(c, range(2, QT))
                if more:
                    inverse_std(c + 1, 1)

            inverse_std(0, 0)
            times_scale(0, 0)
            for i, ((hi, lo), raw) in enumerate(((wv, wv_raw), (wq, wq_raw))):
                pool.wait_ge(wkvq_hi_ok, i + 2)
                pool.tensor_tensor(lo[:], raw, hi[:].bitcast(F32), ALU.subtract).then_inc(wvq_lo_ok, 1)
                if i == 0:
                    inverse_std(0, 1)
            over_chunks(pool, body)
            pool.wait_ge(norm_max_ok, 8 * NC)
            for s in range(2):
                pool.partition_all_reduce(all_max[:, s:s + 1], norm_max[:, s, :], P, RMAX).then_inc(pool_ok, 1)

        @block.scalar
        def _(act):
            def turned_rows(c, s, tiles):
                for q in tiles:
                    n = 4 * s + q
                    act.wait_ge(turned, 8 * c + n + 1)
                    if q == 0:
                        wait(act, proj_ok, 12 * (c - 1) + (8 if s == 0 else 12))
                    act.copy(zt_hi[s][:, :, q * P:(q + 1) * P], turn_ps[:, n % 2, :, :]).then_inc(zt_hi_ok, 1)

            def keys_or_queries(c, s, pairs, masks):
                for m in pairs:
                    i = 4 * s + m
                    b = i % KS
                    act.wait_ge(proj_ok, 12 * c + (m if s == 0 else 8 + m) + 1)
                    wait(act, kq_out[b], 32 * (8 // KS * c + i // KS))
                    bias = bk_col[:, m:m + 1] if s == 0 else bqs_col[:, m:m + 1]
                    scale = 1.0 if s == 0 else QSCALE
                    act.activation(kq[:, b, :], proj_ps[:, i % 2, :], ACT.Identity, bias=bias, scale=scale)
                    act.activation(kq_hi[:, b, :], proj_ps[:, i % 2, :], ACT.Identity, bias=bias, scale=scale)
                    wait(act, norm_ok, 8 * c + i - KS + 1)
                    act.activation(kq_sq[:, b, :], proj_ps[:, i % 2, :], ACT.Square, bias=bias,
                                   scale=scale).then_inc(kq_ok, 1)
                    mask_tiles(c, masks[m - pairs[0]])

            def mask_tiles(c, groups):
                for n in groups:
                    k, g = n // 4, n % 4
                    act.wait_ge(edge_turned, 16 * c + n + 1)
                    if n == 0:
                        wait(act, edge_out, 16 * c)
                        if isinstance(c, int) and c == 0:
                            act.wait_ge(wk_lo_ok, 1)
                            act.wait_ge(wvq_lo_ok, 1)
                    act.copy(edge_t[:, 8 * g:8 * g + 8, k * P:(k + 1) * P],
                             edge_ps[:, n % 2, :, :]).then_inc(edge_t_ok, 1)

            def body(c):
                keys_or_queries(c, 0, range(PAIRS), MASKS_K)
                for q in range(QT):
                    if q % 2 == 0:
                        turned_rows(c, 1, (q, q + 1))
                    mask_tiles(c, MASKS_V[q])
                for m in range(PAIRS):
                    keys_or_queries(c, 1, (m,), MASKS_Q[m:])
                    if m < 2 and not (isinstance(c, int) and c == NC - 1):
                        turned_rows(c + 1, 0, (2 * m, 2 * m + 1))

            def weights_hi(i, w, raw):
                act.wait_ge(w_in[i], 16)
                act.copy(w[0][:], raw).then_inc(wkvq_hi_ok, 1)

            act.wait_ge(consts_ok, 1)
            weights_hi(0, wk, wk_raw)
            turned_rows(0, 0, range(QT))
            weights_hi(1, wv, wv_raw)
            weights_hi(2, wq, wq_raw)
            over_chunks(act, body)
            act.wait_ge(bnd_ok, 1)
            act.activation(bnd[:, 1:2], bnd[:, 0:1], ACT.Sqrt).then_inc(red_ok, 1)

        @block.vector
        def _(dve):
            dve.memset(one_col[:], 1.0)
            dve.memset(halves[:], 0.0).then_inc(halves_ok, 1)
            dve.wait_ge(halves_ok, 1)
            dve.memset(halves[0:HD, 0:HD], 1.0).then_inc(halves_ok, 1)
            dve.memset(halves[HD:P, HD:P], 1.0).then_inc(halves_ok, 1)
            dve.wait_ge(consts_in, 16 * 6)
            dve.tensor_scalar(nm[:], nm_i[:], 1, None, ALU.is_equal)
            dve.memset(norm_max[:], 0.0)
            dve.tensor_scalar(bqs_col[:], bq_col[:], QSCALE, None, ALU.mult).then_inc(consts_ok, 1)
            dve.wait_ge(consts_ok, 1)

            def moments(c, s):
                dve.wait_ge(x_in[s], 16 * (c + 1))
                for q in range(QT):
                    dve.bn_stats(stats[:, s, q, :], z[s][:, q, :]).then_inc(stats_ok, 1)
                for q in range(QT):
                    count = 8 * c + 4 * s + q + 1
                    dve.compute_val(count)
                    dve.wait_ge(consts_ok, 1)
                    dve.wait_ge(stats_ok, count)
                    dve.bn_aggr(mv[:, s, q, :], stats[:, s, q, :]).then_inc(mv_ok, 1)

            def scale_rows(c, s):
                dve.wait_ge(rstd_ok, 2 * c + s + 1)
                dve.tensor_tensor(rstd_m[:, s, :], rstd[:, s, :],
                                  nm[:, bass.ts(c, QT)], ALU.mult).then_inc(z_step, 1)
                dve.wait_ge(z_step, 10 * c + 5 * s + 1)
                for q in range(QT):
                    dve.tensor_scalar(z[s][:, q, :], z[s][:, q, :], mv[:, s, q, 0:1],
                                      rstd_m[:, s, q:q + 1], ALU.subtract, ALU.mult).then_inc(z_step, 1)

            def shift_rows(c, s):
                for q in range(QT):
                    dve.wait_ge(z_scaled, 8 * c + 4 * s + q + 1)
                    dve.scalar_tensor_tensor(z[s][:, q, :], bias_b[:], nm[:, bass.ds(c * QT + q, 1)],
                                             z[s][:, q, :], ALU.mult, ALU.add).then_inc(z_ok, 1)

            def edges(c, k):
                b = k % 2
                if isinstance(c, int) and c == 0 and k == 1:
                    dve.wait_ge(wvq_lo_ok, 2)
                dve.wait_ge(adj_in[b], 16 * (2 * c + k // 2 + 1))
                wait(dve, edge_turned, 4 * (4 * c + k - 1))
                dve.tensor_scalar(edge[:, b, :], adj[:, b, :], 0, None, ALU.not_equal).then_inc(edge_ok, 1)

            def turned_lo(c, s, tiles):
                for q in tiles:
                    n = 4 * s + q
                    cols = slice(q * P, (q + 1) * P)
                    dve.wait_ge(zt_hi_ok, 8 * c + n + 1)
                    dve.tensor_tensor(zt_lo[s][:, :, cols], turn_ps[:, n % 2, :, :],
                                      zt_hi[s][:, :, cols].bitcast(F32), ALU.subtract).then_inc(zt_lo_ok, 1)

            def split(c, s, m):
                i = 4 * s + m
                n, b = 8 * c + i, i % KS
                dve.wait_ge(kq_ok, n + 1)
                dve.tensor_tensor(kq_lo[:, b, :], kq[:, b, :], kq_hi[:, b, :].bitcast(F32),
                                  ALU.subtract).then_inc(lo_ok, 1)
                if not isinstance(n, int) or n >= NLAG:
                    fold_norm(n - NLAG, 0 if NLAG <= i < NLAG + PAIRS else 1, (i - NLAG) % 2)

            def fold_norm(n, which, b):
                dve.wait_ge(norm_ok, n + 1)
                wait(dve, norm_max_ok, n)
                dve.reduce_max(norm_new[:, which:which + 1], norm_ps[:, b, :], AX_X).then_inc(norm_read, 1)
                dve.wait_ge(norm_read, n + 1)
                dve.tensor_tensor(norm_max[:, which, :], norm_max[:, which, :],
                                  norm_new[:, which:which + 1], ALU.max).then_inc(norm_max_ok, 1)

            def value(c, q):
                dve.wait_ge(proj_ok, 12 * c + 4 + q + 1)
                wait(dve, v_out[q], 16 * c)
                wait(dve, v_sum_ok, 4 * (c - 1) + q + 1)
                dve.tensor_tensor(vv[:, q, :], proj_ps[:, q % 2, :], bv_b[:], ALU.add).then_inc(v_ok, 1)

            def body(c):
                more = not (isinstance(c, int) and c == NC - 1)
                scale_rows(c, 1)
                split(c, 0, 0)
                split(c, 0, 1)
                shift_rows(c, 1)
                edges(c, 1)
                split(c, 0, 2)
                split(c, 0, 3)
                turned_lo(c, 1, (0, 1))
                if more:
                    moments(c + 1, 0)
                value(c, 0)
                value(c, 1)
                turned_lo(c, 1, (2, 3))
                edges(c, 2)
                if more:
                    scale_rows(c + 1, 0)
                value(c, 2)
                value(c, 3)
                if more:
                    shift_rows(c + 1, 0)
                for m in range(2):
                    split(c, 1, m)
                    if more:
                        turned_lo(c + 1, 0, (2 * m, 2 * m + 1))
                    if m == 0:
                        edges(c, 3)
                if more:
                    moments(c + 1, 1)
                split(c, 1, 2)
                if more:
                    edges(c + 1, 0)
                split(c, 1, 3)

            moments(0, 0)
            scale_rows(0, 0)
            shift_rows(0, 0)
            dve.wait_ge(wkvq_hi_ok, 1)
            dve.tensor_tensor(wk[1][:], wk_raw, wk[0][:].bitcast(F32), ALU.subtract).then_inc(wk_lo_ok, 1)
            turned_lo(0, 0, range(QT))
            moments(0, 1)
            edges(0, 0)
            over_chunks(dve, body)
            for n in range(8 * NC - NLAG, 8 * NC):
                fold_norm(n, 1, n % 2)
            dve.wait_ge(v_tot_ok, 1)
            dve.tensor_copy(keep["v_tot"][:], norm_ps[:, 0, 0:PAIRS]).then_inc(v_tot_kept, 1)
            dve.wait_ge(pool_ok, 2)
            dve.tensor_tensor(bnd[:, 0:1], all_max[:, 0:1], all_max[:, 1:2], ALU.mult).then_inc(bnd_ok, 1)
            dve.wait_ge(red_ok, 1)
            dve.tensor_scalar(keep["minus_bound"][:], bnd[:, 1:2], -NORM_SLACK, None, ALU.mult).then_inc(bnd_ok, 1)
            dve.wait_ge(bnd_ok, 2)
            dve.tensor_scalar(keep["bounded_f"][:], keep["minus_bound"][0:1, 0:1], -BOUND_MAX, None,
                              ALU.is_ge).then_inc(bnd_ok, 1)
            dve.wait_ge(bnd_ok, 3)
            dve.tensor_copy(keep["bounded_i"][:], keep["bounded_f"][:]).then_inc(bnd_ok, 1)
            dve.wait_ge(bnd_ok, 4)

        @block.tensor
        def _(pe):
            def turn(c, s, tiles):
                for q in tiles:
                    n = 4 * s + q
                    pe.wait_ge(z_ok, 8 * c + n + 1)
                    wait(pe, zt_lo_ok, 8 * c + n - 1)
                    for k in range(KT):
                        last = pe.transpose(turn_ps[:, n % 2, k, :], z[s][:, q, k * P:(k + 1) * P], ident[:])
                    last.then_inc(turned, 1)

            def keys_or_queries(c, s, w, pairs, masks):
                pe.wait_ge(zt_lo_ok, 8 * c + 4 * s + 4)
                if isinstance(c, int) and c == 0:
                    if s == 0:
                        pe.wait_ge(wk_lo_ok, 1)
                    else:
                        pe.wait_ge(wvq_lo_ok, 2)
                for m in pairs:
                    if s == 0:
                        wait(pe, kq_ok, 8 * c + m - 1)
                    elif m < 2:
                        wait(pe, v_ok, 4 * c + 3 + m)
                    else:
                        wait(pe, kq_ok, 8 * c + 3 + m)
                    cols = slice(m * P, (m + 1) * P)
                    for k in range(KT):
                        for i, (wx, zx) in enumerate(((w[0], zt_hi[s]), (w[0], zt_lo[s]), (w[1], zt_hi[s]))):
                            last = pe.matmul(proj_ps[:, m % 2, :], wx[:, k, cols], zx[:, k, :],
                                             start=(k == 0 and i == 0), stop=(k == KT - 1 and i == 2))
                    last.then_inc(proj_ok, 1)
                    n = 8 * c + 4 * s + m
                    if not isinstance(n, int) or n >= NLAG:
                        norms(n - NLAG, (m - NLAG) % KS)
                    turn_edges(c, masks[m - pairs[0]])

            def norms(n, b):
                pe.wait_ge(kq_ok, n + 1)
                wait(pe, norm_read, n - 1)
                pe.matmul(norm_ps[:, b % 2, :], halves[:], kq_sq[:, b, :], start=True, stop=True).then_inc(norm_ok, 1)

            def values(c, tiles):
                if isinstance(c, int) and c == 0:
                    pe.wait_ge(wvq_lo_ok, 1)
                for q in tiles:
                    if q < 2:
                        wait(pe, kq_ok, 8 * c + 3 + q)
                    else:
                        wait(pe, v_ok, 4 * c + q - 1)
                    cols = slice(q * P, (q + 1) * P)
                    for k in range(KT):
                        for i, (zx, wx) in enumerate(((zt_hi[0], wv[0]), (zt_hi[0], wv[1]), (zt_lo[0], wv[0]))):
                            last = pe.matmul(proj_ps[:, q % 2, :], zx[:, k, cols], wx[:, k, :],
                                             start=(k == 0 and i == 0), stop=(k == KT - 1 and i == 2))
                    last.then_inc(proj_ok, 1)
                    turn_edges(c, MASKS_V[q])

            def turn_edges(c, groups):
                for n in groups:
                    k, g = n // 4, n % 4
                    if g == 0:
                        pe.wait_ge(edge_ok, 4 * c + k + 1)
                    wait(pe, edge_t_ok, 16 * c + n - 1)
                    for t in range(8):
                        at = (8 * g + t) * P
                        last = pe.transpose(edge_ps[:, n % 2, t, :], edge[:, k % 2, at:at + P], ident_h[:])
                    last.then_inc(edge_turned, 1)

            def body(c):
                keys_or_queries(c, 0, wk, range(PAIRS), MASKS_K)
                for q in (0, 2):
                    turn(c, 1, (q, q + 1))
                    values(c, (q, q + 1))
                for m in range(PAIRS):
                    keys_or_queries(c, 1, wq, (m,), MASKS_Q[m:])
                    if m < 2 and not (isinstance(c, int) and c == NC - 1):
                        turn(c + 1, 0, (2 * m, 2 * m + 1))

            pe.wait_ge(ident_ok, 2)
            pe.wait_ge(halves_ok, 3)
            turn(0, 0, range(QT))
            over_chunks(pe, body)
            for n in range(8 * NC - NLAG, 8 * NC):
                norms(n, n % KS)
            pe.wait_ge(v_sum_ok, ST)
            pe.wait_ge(norm_read, 8 * NC)
            for m in range(PAIRS):
                last = pe.matmul(norm_ps[:, 0, m:m + 1], v_sum[:, m * P:(m + 1) * P], one_col[:],
                                 start=True, stop=True)
            last.then_inc(v_tot_ok, 1)


LAG = 3
DEN_AT = 5
PR = 8
GR = 4
SUMS = ST // 2 * (GR - 1) // GR


def by_gpsimd(r):
    return r % GR == GR - 1


def sums_upto(r):
    return r + 1 - (r + 1) // GR


def adds_upto(r):
    return max(r, 1) + (r + 1) // GR


ADDS = adds_upto(ST // 2 - 1)


def attend(nc, io, scr, keep):
    STEPS = PAIRS * NC
    with ExitStack() as ctx:
        def sb(name, shape, dt):
            return ctx.enter_context(nc.sbuf_tensor(name, shape, dt))

        def ps(name, shape, dt):
            return ctx.enter_context(nc.psum_tensor(name, shape, dt))

        sem = nc.alloc_semaphore

        k_st = sb("k_stack", [P, 2, N], F32R)
        v_sb = sb("v_pair", [P, ST, P], F32)
        q_a = sb("q_hi_lo", [P, 2, 2, CH], F32R)
        q_b = sb("q_lo_hi", [P, 2, 2, CH], F32R)
        edge = sb("edge_st", [P, 2, ST, CH], U8)
        prob = sb("prob", [P, PR, 2, CH], F32)
        pair_sum = sb("pair_sum", [P, GR - 1, 2, CH], F32)
        step_sum = sb("step_sum", [P, 2, 2, CH], F32)
        out_sb = sb("out_sb", [P, CH], F32)
        den_all = sb("den_all", [P, CH], F32)
        lone = sb("lone", [P, CH], F32)
        rden = sb("rden", [P, CH], F32)
        ctx_sb = sb("ctx_sb", [P, CH], F32)
        ones = sb("ones", [P, HD], F32)
        w_raw = sb("w_raw", [P, CH], F32)
        w_hi, w_lo = (sb(n, [P, CH], F32R) for n in ("w_hi", "w_lo"))

        ones_sq = sb("ones_sq", [P, P], F32)
        spread = sb("spread", [P, P], F32R)
        shift = sb("shift", [P, 2, CH], F32R)
        part_max = sb("part_max", [P, N // CH], F32)
        top = sb("top", [P, 2, QT], F32)
        minus_max = sb("minus_max", [P, 2, QT], F32)
        adj_rows = prob[:, PR // 2:PR].rearrange("p a b c -> p (a b c)").bitcast(I32)
        bias = edge[:, 1].rearrange("p a b -> p (a b)").bitcast(F32)

        sc = ps("scores", [P, 3, 2, CH], F32)
        po = ps("pv", [P, CH], F32)
        pl = ps("den", [P, CH], F32)

        consts_ok, spread_ok = sem("a_consts_ok"), sem("spread_ok")
        w_raw_in, w_hi_ok, w_lo_ok, w_out = (sem(n) for n in ("w_raw_in", "w_hi_ok", "w_lo_ok", "w_out"))
        k_in = [sem(f"k_in{i}") for i in range(4)]
        v_in = [sem(f"v_in{i}") for i in range(4)]
        q_in = [sem(f"q_in{b}") for b in range(2)]
        edge_in = [sem(f"edge_in{b}") for b in range(2)]
        scores_ok, exp_ok, masked_ok, sums_ok, summed_ok, pv_ok, den_ok = (sem(n) for n in (
            "scores_ok", "exp_ok", "masked_ok", "sums_ok", "summed_ok", "pv_ok", "den_ok"))
        out_copied, den_taken, finish_step, ctx_ok, ctx_out = (sem(n) for n in (
            "out_copied", "den_taken", "finish_step", "ctx_ok", "ctx_out"))

        cf = {n: sem(n) for n in (
            "cf_in", "cf_adj", "cf_rough", "cf_minus", "shift_out", "shift_in", "cf_shift", "cf_scores", "cf_exp",
            "cf_masked", "cf_out_sb", "cf_den_all", "cf_fin", "cf_out", "pre_bias", "pre_added",
            "pre_max", "pre_top", "pre_clamped", "pre_pv", "pre_ctx")}
        (cf_in, cf_adj, cf_rough, cf_minus, shift_out, shift_in, cf_shift, cf_scores, cf_exp, cf_masked, cf_out_sb,
         cf_den_all, cf_fin, cf_out, pre_bias, pre_added, pre_max, pre_top, pre_clamped, pre_pv,
         pre_ctx) = cf.values()

        qk = {n: scr[n].rearrange("(m h d) t -> m d h t", m=PAIRS, h=2) for n in ("k_hi", "k_lo", "q_hi", "q_lo")}
        v_rows = scr["v"].rearrange("(t p) (m c) -> m p t c", p=P, m=PAIRS)
        ctx_rows = scr["ctx"].rearrange("(m p) t -> m p t", p=P)
        adj_blocks = io["adj"].rearrange("(b p) s -> b p s", p=P)
        shift_row = scr["shift"].rearrange("h q p -> h (q p)")
        shift_cols = scr["shift"].rearrange("h q p -> p h q")

        def wait(eng, s, value):
            if not isinstance(value, int) or value > 0:
                eng.wait_ge(s, value)

        def over_steps(eng, body):
            body(0, 0)
            body(1, 1)
            with eng.Fori(1, STEPS // 2) as i:
                body(2 * i, 0)
                body(2 * i + 1, 1)

        hold = start_holds(k_in[0])

        def load_k(sp, m, i):
            cols = slice(i * N // 4, (i + 1) * N // 4)
            sp.dma_start(k_st[0:HD, :, cols].bitcast(F32), qk["k_hi"][m][:, :, cols]).then_inc(k_in[i], 16)
            sp.dma_start(k_st[HD:P, :, cols].bitcast(F32), qk["k_lo"][m][:, :, cols]).then_inc(k_in[i], 16)

        def load_v(sp, m, i):
            t = slice(i * ST // 4, (i + 1) * ST // 4)
            sp.dma_start(v_sb[:, t, :], v_rows[m][:, t, :]).then_inc(v_in[i], 16)

        def load_q(sp, m, c, b):
            cols = bass.ts(c, CH)
            for t, top, low in ((q_a, "q_hi", "q_lo"), (q_b, "q_lo", "q_hi")):
                sp.dma_start(t[0:HD, b].bitcast(F32), qk[top][m][:, :, cols]).then_inc(q_in[b], 16)
                sp.dma_start(t[HD:P, b].bitcast(F32), qk[low][m][:, :, cols]).then_inc(q_in[b], 16)

        def load_edge(sp, c, b):
            sp.dma_start(edge[:, b], scr["edge_t"][c]).then_inc(edge_in[b], 16)

        FINISH = 8
        FINISH_AT = {7: (0, 1), 14: (2,), 15: (3,), 22: (4,), 23: (5,), 30: (6, 7)}

        def finish_op(dve, s, k, pair, fin, den_sem, out_sem, done):
            base = (FINISH - 1) * s
            if k == 0:
                dve.wait_ge(den_sem, s + 1)
                dve.tensor_scalar(lone[:], den_all[:], 0.0, None, ALU.is_equal).then_inc(fin, 1)
            elif k == 1:
                dve.wait_ge(fin, base + 1)
                dve.scalar_tensor_tensor(den_all[:], lone[:], float(N), den_all[:], ALU.mult, ALU.add).then_inc(fin, 1)
            elif k < 6:
                q = slice((k - 2) * P, (k - 1) * P)
                dve.wait_ge(fin, base + 2)
                dve.reciprocal(rden[:, q], den_all[:, q]).then_inc(fin, 1)
            elif k == 6:
                dve.wait_ge(out_sem, s + 1)
                dve.scalar_tensor_tensor(out_sb[:], lone[:], keep["v_tot"][:, bass.ds(pair, 1)], out_sb[:],
                                         ALU.mult, ALU.add).then_inc(fin, 1)
            else:
                dve.wait_ge(fin, base + 7)
                if not (isinstance(s, int) and s == 0) and done is ctx_ok:
                    dve.wait_ge(ctx_out, 16 * s)
                dve.tensor_tensor(ctx_sb[:], out_sb[:], rden[:], ALU.mult).then_inc(done, 1)

        def load_for_feed(sp):
            sp.dma_start(keep["wo"][:], io["Wo"].rearrange("(k p) n -> p k n", p=P)).then_inc(keep["consts_in"], 16)
            for t, n in (("bo_b", "bo"), ("ln2_scale_b", "ln2_scale"), ("ln2_bias_b", "ln2_bias")):
                sp.dma_start(keep[t][:], io[n].partition_broadcast(P)).then_inc(keep["consts_in"], 16)
            sp.dma_start(keep["nodemask"][:], io["nodemask"].rearrange("(t p) -> p t", p=P),
                         allow_slow_non_contiguous=True).then_inc(keep["consts_in"], 16)
            sp.dma_start(keep["rows"][:, 0], scr["ht"].rearrange("(c q p) d -> c p q d", p=P, q=QT)[0]).then_inc(keep["ht_in"], 16)
            for q in range(2):
                sp.dma_start(keep["ctx_in"][:, q], scr["ctx"].rearrange("(k p) t -> p k t", p=P)[:, :, q * P:(q + 1) * P]
                             ).then_inc(keep["ctx_in_sems"][q], 16)

        def bounded_sync(sp):
            for i in range(4):
                load_k(sp, 0, i)
                if i == 0:
                    load_q(sp, 0, 0, 0)
                    load_edge(sp, 0, 0)
                load_v(sp, 0, i)

            def step(m, c, b):
                s = NC * m + c
                first = isinstance(s, int) and s == 0
                last = isinstance(s, int) and s == STEPS - 1
                ends_pair = isinstance(c, int) and c == NC - 1
                if not last:
                    nm, ncn = (m + 1, 0) if ends_pair else (m, c + 1)
                    hold(sp, scores_ok, ST * s)
                    load_q(sp, nm, ncn, 1 - b)
                    hold(sp, masked_ok, ST * s)
                    load_edge(sp, ncn, 1 - b)
                if not first:
                    pm, pc = (m - 1, NC - 1) if isinstance(c, int) and c == 0 else (m, c - 1)
                    hold(sp, ctx_ok, s)
                    sp.dma_start(ctx_rows[pm][:, bass.ts(pc, CH)], ctx_sb[:]).then_inc(ctx_out, 16)
                if ends_pair and not last:
                    for i in range(4):
                        hold(sp, scores_ok, ST * s + 8 * (i + 1))
                        load_k(sp, m + 1, i)
                        hold(sp, pv_ok, ST * s + 8 * (i + 1))
                        load_v(sp, m + 1, i)

            def pair(m):
                step(m, 0, 0)
                step(m, 1, 1)
                with sp.Fori(1, NC // 2 - 1) as i:
                    step(m, 2 * i, 0)
                    step(m, 2 * i + 1, 1)
                step(m, NC - 2, 0)
                step(m, NC - 1, 1)

            pair(0)
            with sp.Fori(1, PAIRS - 1) as m:
                pair(m)
            pair(PAIRS - 1)
            hold(sp, ctx_out, 16 * (STEPS - NC + 1))
            load_for_feed(sp)
            hold(sp, ctx_ok, STEPS)
            sp.dma_start(ctx_rows[PAIRS - 1][:, (NC - 1) * CH:], ctx_sb[:]).then_inc(ctx_out, 16)
            hold(sp, ctx_out, 16 * STEPS)

        def bounded_tensor(pe):
            def pv(s, b, j):
                pe.wait_ge(masked_ok, ST * s + j + 1)
                if j % 8 == 0:
                    pe.wait_ge(v_in[j // 8], 16 * (s // NC + 1))
                if j == 0:
                    wait(pe, out_copied, s)
                for h in range(2):
                    last = pe.matmul(po[h * HD:(h + 1) * HD, :], v_sb[:, j, h * HD:(h + 1) * HD],
                                     prob[:, j % PR, h, :], start=(j == 0), stop=(j == ST - 1))
                last.then_inc(pv_ok, 1)

            def denominators(s, b):
                pe.wait_ge(summed_ok, ADDS * s + ADDS)
                wait(pe, den_taken, s)
                for h in range(2):
                    last = pe.matmul(pl[h * HD:(h + 1) * HD, :], ones[:], step_sum[:, b, h, :], start=True, stop=True)
                last.then_inc(den_ok, 1)

            def body(s, b):
                first = isinstance(s, int) and s == 0
                for j in range(ST):
                    if j == 0:
                        pe.wait_ge(q_in[b], 64 * (s // 2 + 1))
                    if j % 8 == 0:
                        pe.wait_ge(k_in[j // 8], 32 * (s // NC + 1))
                    wait(pe, exp_ok, ST * s + (j - 2 if j >= 2 else j - 1))
                    for h in range(2):
                        k_tile = k_st[:, h, j * P:(j + 1) * P]
                        pe.matmul(sc[:, j % 3, h, :], k_tile, q_a[:, b, h, :], start=True, stop=False)
                        last = pe.matmul(sc[:, j % 3, h, :], k_tile, q_b[:, b, h, :], start=False, stop=True)
                    last.then_inc(scores_ok, 1)
                    if j == LAG + 1:
                        pv(s, b, 0)
                    if j > LAG:
                        pv(s, b, j - LAG)
                    elif j < LAG and not first:
                        pv(s - 1, 1 - b, ST + j - LAG)
                    if j == DEN_AT and not first:
                        denominators(s - 1, 1 - b)

            over_steps(pe, body)
            for j in range(ST - LAG, ST):
                pv(STEPS - 1, 1, j)
            denominators(STEPS - 1, 1)

        def bounded_scalar(act):
            def take_products(s):
                act.wait_ge(pv_ok, ST * s + ST)
                wait(act, ctx_ok, s)
                act.copy(out_sb[:], po[:]).then_inc(out_copied, 1)

            def take_denominators(s):
                act.wait_ge(den_ok, s + 1)
                wait(act, ctx_ok, s)
                act.copy(den_all[:], pl[:]).then_inc(den_taken, 1)

            def body(s, b):
                first = isinstance(s, int) and s == 0
                for j in range(ST):
                    act.wait_ge(scores_ok, ST * s + j + 1)
                    wait(act, pv_ok, ST * s + j - PR + 1)
                    ps, pj = (s, j - PR) if j >= PR else (s - 1, j - PR + ST)
                    r = pj // 2
                    if isinstance(ps, int) and ps < 0:
                        pass
                    elif by_gpsimd(r):
                        act.wait_ge(summed_ok, ADDS * ps + adds_upto(r) - 1 + pj % 2)
                    else:
                        act.wait_ge(sums_ok, SUMS * ps + sums_upto(r))
                    act.activation(prob[:, j % PR], sc[:, j % 3], ACT.Exp,
                                   bias=keep["minus_bound"][:, 0:1]).then_inc(exp_ok, 1)
                    if j == LAG - 1 and not first:
                        take_products(s - 1)
                    if j == DEN_AT and not first:
                        take_denominators(s - 1)

            over_steps(act, body)
            take_products(STEPS - 1)
            take_denominators(STEPS - 1)

        def bounded_vector(dve):
            def finish(s, k):
                finish_op(dve, s, k, s // NC, finish_step, den_taken, out_copied, ctx_ok)

            def body(s, b):
                first = isinstance(s, int) and s == 0
                dve.wait_ge(edge_in[b], 16 * (s // 2 + 1))
                for j in range(ST):
                    dve.wait_ge(exp_ok, ST * s + j + 1)
                    dve.tensor_tensor(prob[:, j % PR], prob[:, j % PR],
                                      edge[:, b, j, :].unsqueeze(1).broadcast_to([P, 2, CH]),
                                      ALU.mult).then_inc(masked_ok, 1)
                    r = j // 2
                    if j % 2 == 1 and not by_gpsimd(r):
                        dve.wait_ge(masked_ok, ST * s + j + 1)
                        if r >= GR:
                            dve.wait_ge(summed_ok, ADDS * s + adds_upto(r - GR))
                        elif not first:
                            dve.wait_ge(summed_ok, ADDS * (s - 1) + adds_upto(r - GR + ST // 2))
                        dve.tensor_tensor(pair_sum[:, r % GR], prob[:, (j - 1) % PR], prob[:, j % PR],
                                          ALU.add).then_inc(sums_ok, 1)
                    if not first:
                        for k in FINISH_AT.get(j, ()):
                            finish(s - 1, k)

            over_steps(dve, body)
            for k in range(FINISH):
                finish(STEPS - 1, k)

        W_PIECES = STEPS // 2
        w_raws = [t.rearrange("(n r) (a c) -> n (r a) c", n=W_PIECES, c=CH) for t in (io["W1"], io["W2"])]
        w_his, w_los = ([scr[f"w{i}_{part}"].rearrange("(n r) (a c) -> n (r a) c", n=W_PIECES, c=CH) for i in (1, 2)]
                        for part in ("hi", "lo"))
        hold_w = start_holds(consts_ok, 1)

        def load_piece(pool, w, s):
            hold_w(pool, w_lo_ok, s)
            pool.dma_start(w_raw[:], w_raws[w][s - W_PIECES * w]).then_inc(w_raw_in, 16)

        def piece_hi(pool, s):
            hold_w(pool, w_raw_in, 16 * s + 16)
            hold_w(pool, w_out, 32 * s)
            pool.tensor_copy(w_hi[:], w_raw[:]).then_inc(w_hi_ok, 1)

        def piece_lo(pool, w, s):
            hold_w(pool, w_hi_ok, s + 1)
            pool.tensor_tensor(w_lo[:], w_raw[:], w_hi[:].bitcast(F32), ALU.subtract).then_inc(w_lo_ok, 1)
            pool.dma_start(w_his[w][s - W_PIECES * w], w_hi[:].bitcast(F32)).then_inc(w_out, 16)
            hold_w(pool, w_lo_ok, s + 1)
            pool.dma_start(w_los[w][s - W_PIECES * w], w_lo[:].bitcast(F32)).then_inc(w_out, 16)

        def bounded_gpsimd(pool):
            def body(w, s, b):
                load_piece(pool, w, s)
                for r in range(1, ST // 2):
                    if by_gpsimd(r):
                        terms = [prob[:, (2 * r + i) % PR] for i in range(2)]
                    else:
                        terms = [pair_sum[:, r % GR]]
                    for i, term in enumerate(terms):
                        if by_gpsimd(r):
                            pool.wait_ge(masked_ok, ST * s + 2 * r + i + 1)
                        else:
                            pool.wait_ge(sums_ok, SUMS * s + sums_upto(r))
                        if r == 1:
                            wait(pool, den_ok, s - 1)
                            a = pair_sum[:, 0]
                        else:
                            pool.wait_ge(summed_ok, ADDS * s + adds_upto(r) - len(terms) + i)
                            a = step_sum[:, b]
                        pool.tensor_tensor(step_sum[:, b], a, term, ALU.add).then_inc(summed_ok, 1)
                    if r == GR:
                        piece_hi(pool, s)
                    elif r == GR + 1:
                        piece_lo(pool, w, s)

            body(0, 0, 0)
            body(0, 1, 1)
            for w in range(2):
                with pool.Fori(1 - w + W_PIECES // 2 * w, W_PIECES // 2 * (w + 1)) as i:
                    body(w, 2 * i, 0)
                    body(w, 2 * i + 1, 1)
            hold_w(pool, w_out, 32 * STEPS)

        def careful_gpsimd(pool):
            def piece(w, s):
                load_piece(pool, w, s)
                piece_hi(pool, s)
                piece_lo(pool, w, s)

            piece(0, 0)
            for w in range(2):
                with pool.Fori(1 - w + W_PIECES * w, W_PIECES * (w + 1)) as s:
                    piece(w, s)
            hold_w(pool, w_out, 32 * STEPS)

        hold_cf = start_holds(spread_ok, 1)

        def careful_sync(sp):
            with sp.Fori(0, PAIRS) as m:
                with sp.Fori(0, NC) as c:
                    s = NC * m + c
                    for half, part in ((slice(0, HD), "k_hi"), (slice(HD, P), "k_lo")):
                        sp.dma_start(k_st[half].bitcast(F32), qk[part][m]).then_inc(cf_in, 16)
                    for t, top, low in ((q_a, "q_hi", "q_lo"), (q_b, "q_lo", "q_hi")):
                        for half, part in ((slice(0, HD), top), (slice(HD, P), low)):
                            sp.dma_start(t[half, 0].bitcast(F32),
                                         qk[part][m][:, :, bass.ts(c, CH)]).then_inc(cf_in, 16)
                    sp.dma_start(v_sb[:], v_rows[m]).then_inc(cf_in, 16)
                    sp.dma_start(edge[:, 0], scr["edge_t"][c]).then_inc(cf_in, 16)
                    for q in range(QT):
                        hold_cf(sp, pre_bias, QT * s + q + 1)
                        sp.dma_start(adj_rows, adj_blocks[QT * c + q]).then_inc(cf_adj, 16)
                    hold_cf(sp, cf_minus, s + 1)
                    sp.dma_start(shift_cols, minus_max[:], allow_slow_non_contiguous=True).then_inc(shift_out, 16)
                    hold_cf(sp, shift_out, 16 * s + 16)
                    sp.dma_start(pair_sum[:, 0], shift_row.partition_broadcast(P)).then_inc(shift_in, 16)
                    hold_cf(sp, pre_ctx, s + 2)
                    sp.dma_start(ctx_rows[m][:, bass.ts(c, CH)], ctx_sb[:]).then_inc(cf_out, 16)
                    hold_cf(sp, cf_out, 16 * s + 16)
            load_for_feed(sp)

        def careful_tensor(pe):
            with pe.Fori(0, STEPS) as s:
                pe.wait_ge(cf_in, 128 * s + 128)
                for q in range(QT):
                    for h in range(2):
                        for n in range(N // CH):
                            at = (2 * q + h) * (N // CH) + n
                            pe.wait_ge(pre_added, 64 * s + at + 1)
                            pe.matmul(sc[:, n % 2, 0, :], q_a[:, 0, h, q * P:(q + 1) * P],
                                      k_st[:, h, n * CH:(n + 1) * CH], start=True, stop=True).then_inc(cf_rough, 1)
                pe.wait_ge(cf_shift, s + 1)
                for j in range(ST):
                    pe.wait_ge(pre_clamped, ST * s + j + 1)
                    for h in range(2):
                        k_tile = k_st[:, h, j * P:(j + 1) * P]
                        pe.matmul(sc[:, 2, h, :], k_tile, q_a[:, 0, h, :], start=True, stop=False)
                        pe.matmul(sc[:, 2, h, :], k_tile, q_b[:, 0, h, :], start=False, stop=False)
                        last = pe.matmul(sc[:, 2, h, :], spread[:], shift[:, h, :], start=False, stop=True)
                    last.then_inc(cf_scores, 1)
                    pe.wait_ge(cf_masked, ST * s + j + 1)
                    for h in range(2):
                        pe.matmul(po[h * HD:(h + 1) * HD, :], v_sb[:, j, h * HD:(h + 1) * HD], prob[:, 0, h, :],
                                  start=(j == 0), stop=(j == ST - 1))
                        last = pe.matmul(pl[h * HD:(h + 1) * HD, :], ones[:], prob[:, 0, h, :],
                                         start=(j == 0), stop=(j == ST - 1))
                    last.then_inc(pre_pv, 1)

        def careful_scalar(act):
            with act.Fori(0, STEPS) as s:
                for j in range(ST):
                    act.wait_ge(pre_clamped, ST * s + j + 2)
                    act.activation(prob[:, 0], prob[:, 0], ACT.Exp).then_inc(cf_exp, 1)
                act.wait_ge(pre_pv, ST * s + ST + 1)
                act.copy(out_sb[:], po[:]).then_inc(cf_out_sb, 1)
                act.copy(den_all[:], pl[:]).then_inc(cf_den_all, 1)

        def careful_vector(dve):
            for t, count in ((pre_bias, 1), (pre_added, 2), (pre_max, 1), (pre_top, 1), (pre_clamped, 1), (pre_pv, 1),
                             (pre_ctx, 1)):
                dve.sem_inc(t, count)
            with dve.Fori(0, STEPS) as s:
                for q in range(QT):
                    dve.wait_ge(cf_adj, 16 * QT * s + 16 * q + 16)
                    dve.wait_ge(pre_added, 64 * s + 16 * q + 2)
                    dve.tensor_scalar(bias[:], adj_rows, 0, NEG, ALU.is_equal, ALU.mult).then_inc(pre_bias, 1)
                    dve.wait_ge(pre_bias, QT * s + q + 2)
                    for h in range(2):
                        i = 2 * q + h
                        for n in range(N // CH):
                            at = i * (N // CH) + n
                            dve.wait_ge(cf_rough, 64 * s + at + 1)
                            dve.wait_ge(pre_max, 64 * s + at + 1)
                            dve.tensor_tensor(pair_sum[:, 1, 0, :], sc[:, n % 2, 0, :], bias[:, n * CH:(n + 1) * CH],
                                              ALU.add).then_inc(pre_added, 1)
                            dve.wait_ge(pre_added, 64 * s + at + 3)
                            if n == 0:
                                dve.wait_ge(pre_top, 8 * s + i + 1)
                            dve.reduce_max(part_max[:, n:n + 1], pair_sum[:, 1, 0, :], AX_X).then_inc(pre_max, 1)
                        dve.wait_ge(pre_max, 64 * s + 8 * i + 9)
                        dve.reduce_max(top[:, h, q:q + 1], part_max[:], AX_X).then_inc(pre_top, 1)
                dve.wait_ge(pre_top, 8 * s + 9)
                dve.tensor_scalar(minus_max[:], top[:], -1.0, None, ALU.mult).then_inc(cf_minus, 1)
                dve.wait_ge(shift_in, 16 * s + 16)
                dve.tensor_copy(shift[:], pair_sum[:, 0]).then_inc(cf_shift, 1)
                for j in range(ST):
                    dve.wait_ge(cf_scores, ST * s + j + 1)
                    dve.wait_ge(pre_pv, ST * s + j + 1)
                    dve.tensor_scalar(prob[:, 0], sc[:, 2], CLAMP, None, ALU.min).then_inc(pre_clamped, 1)
                    dve.wait_ge(cf_exp, ST * s + j + 1)
                    dve.tensor_tensor(prob[:, 0], prob[:, 0],
                                      edge[:, 0, j, :].unsqueeze(1).broadcast_to([P, 2, CH]),
                                      ALU.mult).then_inc(cf_masked, 1)
                for k in range(FINISH):
                    finish_op(dve, s, k, s // NC, cf_fin, cf_den_all, cf_out_sb, pre_ctx)

        def branch(eng, bounded, careful):
            flag = eng.value_load(keep["bounded_i"][0:1, 0:1], min_val=0, max_val=1)
            with eng.If(flag > 0):
                bounded(eng)
            with eng.Else():
                careful(eng)

        block = ctx.enter_context(nc.Block())

        @block.sync
        def _(sp):
            branch(sp, bounded_sync, careful_sync)

        @block.gpsimd
        def _(pool):
            pool.memset(ones[:], 1.0).then_inc(consts_ok, 1)

            branch(pool, bounded_gpsimd, careful_gpsimd)

        @block.scalar
        def _(act):
            branch(act, bounded_scalar, careful_scalar)

        @block.vector
        def _(dve):
            dve.memset(ones_sq[:], 1.0 / P).then_inc(spread_ok, 1)
            dve.wait_ge(spread_ok, 1)
            dve.tensor_copy(spread[:], ones_sq[:]).then_inc(spread_ok, 1)
            branch(dve, bounded_vector, careful_vector)

        @block.tensor
        def _(pe):
            pe.wait_ge(consts_ok, 1)
            pe.wait_ge(spread_ok, 2)
            branch(pe, bounded_tensor, careful_tensor)


DLAG = 3
GR4 = 4


def feed(nc, io, scr, keep):
    with ExitStack() as ctx:
        def sb(name, shape, dt):
            return ctx.enter_context(nc.sbuf_tensor(name, shape, dt))

        def ps(name, shape, dt):
            return ctx.enter_context(nc.psum_tensor(name, shape, dt))

        sem = nc.alloc_semaphore

        wo, bo_b, scale_b, bias_b, nm_i, ctxt, rows = (keep[n] for n in (
            "wo", "bo_b", "ln2_scale_b", "ln2_bias_b", "nodemask", "ctx_in", "rows"))
        w1_hi, w1_lo = (sb(n, [P, KT, F], F32R) for n in ("w1_hi", "w1_lo"))
        w2_hi, w2_lo = (sb(n, [P, FT, D], F32R) for n in ("w2_hi", "w2_lo"))
        nm = sb("nodemask2_f", [P, ST], F32)
        ident = sb("ident2", [P, P], F32)
        minus_half = sb("minus_half2", [P, QT], F32)
        eps_t = sb("eps2", [P, QT], F32)
        xr = sb("x_rows", [P, QT, D], F32)
        h2t_hi, h2t_lo = (sb(n, [P, KT, CH], F32R) for n in ("h2t_hi", "h2t_lo"))
        g32 = sb("gelu", [P, 2, CH], F32)
        g_hi, g_lo = (sb(n, [P, GR4, CH], F32R) for n in ("gelu_hi", "gelu_lo"))
        stats = sb("stats2", [P, 2, QT, 6], F32)
        mv = sb("mv2", [P, 2, QT, 2], F32)
        var_e = sb("var_e2", [P, 2, QT], F32)
        rstd = sb("rstd2", [P, 2, QT], F32)
        rstd_m = sb("rstd_m2", [P, QT], F32)

        attn_ps = ps("attn_ps", [P, D], F32)
        turn_ps = ps("turn2_ps", [P, KT, P], F32)
        up_ps = ps("up_ps", [P, 2, CH], F32)
        down_ps = ps("down_ps", [P, QT, D], F32)

        consts_in, ht_in, ctx_in = keep["consts_in"], keep["ht_in"], keep["ctx_in_sems"]
        w_in = [sem(f"w_in{g}") for g in range(4)]
        xr_in = sem("xr_in")
        ident_zero, ident_ok, consts_ok = sem("f_ident_zero"), sem("f_ident_ok"), sem("f_consts_ok")
        attn_ok, h1_step, h1_ok, h2_step, h2_ok = (sem(n) for n in ("attn_ok", "h1_step", "h1_ok", "h2_step", "h2_ok"))
        stats_ok, mv_ok, var_ok, rstd_ok = (sem("f_" + n) for n in ("stats_ok", "mv_ok", "var_ok", "rstd_ok"))
        turned, h2t_hi_ok, h2t_lo_ok, up_ok, gelu_ok, g_lo_ok, down_ok = (sem(n) for n in (
            "f_turned", "h2t_hi_ok", "h2t_lo_ok", "up_ok", "gelu_ok", "g_lo_ok", "down_ok"))
        y_taken, y_ok, out_ok, out_done = (sem(n) for n in ("y_taken", "y_ok", "out_ok", "out_done"))

        x_rows = io["x"].rearrange("(c q p) d -> c p q d", p=P, q=QT)
        ht_rows = scr["ht"].rearrange("(c q p) d -> c p q d", p=P, q=QT)
        out_rows = io["out"].rearrange("(c q p) d -> c p q d", p=P, q=QT)
        ctx_tiles = scr["ctx"].rearrange("(k p) t -> p k t", p=P)

        def wait(eng, s, value):
            if not isinstance(value, int) or value > 0:
                eng.wait_ge(s, value)

        def is_first(c):
            return isinstance(c, int) and c == 0

        def is_last(c):
            return isinstance(c, int) and c == NC - 1

        def attn_bank(c, q):
            return down_ps[:, q, :] if is_first(c) else attn_ps[:]

        def over_chunks(eng, body):
            body(0, 0)
            body(1, 1)
            with eng.Fori(1, NC // 2 - 1) as i:
                body(2 * i, 0)
                body(2 * i + 1, 1)
            body(NC - 2, 0)
            body(NC - 1, 1)

        def order_h1(c):
            return 0 if is_first(c) else 2 * c - 1

        def order_y(c):
            return 2 * NC - 1 if is_last(c) else 2 * c + 2

        block = ctx.enter_context(nc.Block())
        hold = start_holds(consts_in, 16 * 5)

        @block.sync
        def _(sp):
            def load_ctx(c, q):
                sp.dma_start(ctxt[:, q % 2], ctx_tiles[:, :, bass.ts(QT * c + q, P)]).then_inc(ctx_in[q % 2], 16)

            def load_ht(c, b):
                sp.dma_start(rows[:, b], ht_rows[c]).then_inc(ht_in, 16)

            def load_x(c):
                sp.dma_start(xr[:], x_rows[c]).then_inc(xr_in, 16)

            for g in range(4):
                cols, tiles = bass.ts(g, F // 4), slice(g * FT // 4, (g + 1) * FT // 4)
                for t, n in ((w1_hi, "w1_hi"), (w1_lo, "w1_lo")):
                    src = scr[n].rearrange("(k p) n -> p k n", p=P)
                    sp.dma_start(t[:, :, cols].bitcast(F32), src[:, :, cols]).then_inc(w_in[g], 16)
                for t, n in ((w2_hi, "w2_hi"), (w2_lo, "w2_lo")):
                    src = scr[n].rearrange("(k p) n -> p k n", p=P)
                    sp.dma_start(t[:, tiles].bitcast(F32), src[:, tiles]).then_inc(w_in[g], 16)
                if g == 0:
                    for q in range(2, QT):
                        hold(sp, attn_ok, q - 1)
                        load_ctx(0, q)
            hold(sp, ht_in, 16)
            load_ht(1, 1)
            load_x(0)

            def body(c, b):
                if not is_last(c):
                    for q in range(2):
                        hold(sp, attn_ok, QT * c + q + 3)
                        load_ctx(c + 1, q)
                if not is_first(c):
                    hold(sp, y_ok, QT * c)
                    load_x(c)
                    hold(sp, out_ok, QT * c)
                    sp.dma_start(out_rows[c - 1], rows[:, 1 - b]).then_inc(out_done, 16)
                    if not is_last(c):
                        hold(sp, out_done, 16 * c)
                        load_ht(c + 1, 1 - b)
                if not is_last(c):
                    for q in range(2, QT):
                        hold(sp, attn_ok, QT * (c + 1) + q - 1)
                        load_ctx(c + 1, q)

            over_chunks(sp, body)
            hold(sp, out_ok, QT * NC)
            sp.dma_start(out_rows[NC - 1], rows[:, 1]).then_inc(out_done, 16)
            hold(sp, out_done, 16 * NC)

        @block.gpsimd
        def _(pool):
            pool.memset(ident[:], 0.0).then_inc(ident_zero, 1)
            pool.memset(minus_half[:], -0.5).then_inc(ident_zero, 1)
            pool.memset(eps_t[:], EPS).then_inc(ident_zero, 1)
            pool.wait_ge(ident_zero, 3)
            pool.affine_select(out=ident[:], in_=ident[:], compare_op=ALU.not_equal, fill=1.0, base=0,
                               pattern=[[-1, P]], channel_multiplier=1).then_inc(ident_ok, 1)

            def inverse_std(n, which):
                pool.wait_ge(mv_ok, 4 * n + 4)
                pool.tensor_tensor(var_e[:, which, :], mv[:, which, :, 1], eps_t[:], ALU.add).then_inc(var_ok, 1)
                pool.wait_ge(var_ok, n + 1)
                pool.tensor_tensor(rstd[:, which, :], var_e[:, which, :], minus_half[:], ALU.pow).then_inc(rstd_ok, 1)

            inverse_std(0, 0)

            def body(c, b):
                if not is_first(c):
                    inverse_std(order_y(c - 1), 1)
                if not is_last(c):
                    inverse_std(order_h1(c + 1), 0)

            over_chunks(pool, body)
            inverse_std(order_y(NC - 1), 1)

        @block.scalar
        def _(act):
            def take_turned(c, q):
                act.wait_ge(turned, QT * c + q + 1)
                act.copy(h2t_hi[:, :, q * P:(q + 1) * P], turn_ps[:]).then_inc(h2t_hi_ok, 1)

            def body(c, b):
                for f in range(FT):
                    act.wait_ge(up_ok, FT * c + f + 1)
                    wait(act, g_lo_ok, FT * c + f - 1)
                    act.activation(g32[:, f % 2, :], up_ps[:, f % 2, :], ACT.Gelu_apprx_tanh)
                    wait(act, down_ok, FT * QT * c + QT * (f - GR4) + QT)
                    act.activation(g_hi[:, f % GR4, :], up_ps[:, f % 2, :], ACT.Gelu_apprx_tanh).then_inc(gelu_ok, 1)
                if not is_last(c):
                    for q in range(QT):
                        take_turned(c + 1, q)

            for q in range(QT):
                take_turned(0, q)
            over_chunks(act, body)

        @block.vector
        def _(dve):
            dve.wait_ge(consts_in, 16 * 5)
            dve.tensor_scalar(nm[:], nm_i[:], 1, None, ALU.is_equal).then_inc(consts_ok, 1)
            dve.wait_ge(consts_ok, 1)

            def moments(n, which, q, b):
                dve.bn_stats(stats[:, which, q, :], rows[:, b, q, :]).then_inc(stats_ok, 1)
                count = 4 * n + q + 1
                if not isinstance(count, int):
                    dve.compute_val(count)
                dve.wait_ge(consts_ok, 1)
                dve.wait_ge(stats_ok, count)
                dve.bn_aggr(mv[:, which, q, :], stats[:, which, q, :]).then_inc(mv_ok, 1)

            def add_attn(c, b, q):
                col = nm[:, bass.ds(c * QT + q, 1)]
                if q == 0:
                    dve.wait_ge(ht_in, 16 * (c + 1))
                dve.wait_ge(attn_ok, QT * c + q + 1)
                dve.scalar_tensor_tensor(rows[:, b, q, :], attn_bank(c, q), col, rows[:, b, q, :],
                                         ALU.mult, ALU.add).then_inc(h1_step, 1)
                dve.wait_ge(h1_step, QT * c + q + 1)
                dve.scalar_tensor_tensor(rows[:, b, q, :], bo_b[:], col, rows[:, b, q, :],
                                         ALU.mult, ALU.add).then_inc(h1_ok, 1)
                dve.wait_ge(h1_ok, QT * c + q + 1)
                moments(order_h1(c), 0, q, b)

            def norm_h1(c, b, q):
                if q == 0:
                    dve.wait_ge(rstd_ok, order_h1(c) + 1)
                    dve.tensor_tensor(rstd_m[:], rstd[:, 0, :], nm[:, bass.ts(c, QT)], ALU.mult).then_inc(h2_step, 1)
                dve.wait_ge(h2_step, 9 * c + 2 * q + 1)
                dve.tensor_scalar(rows[:, b, q, :], rows[:, b, q, :], mv[:, 0, q, 0:1],
                                  rstd_m[:, q:q + 1], ALU.subtract, ALU.mult).then_inc(h2_step, 1)
                dve.wait_ge(h2_step, 9 * c + 2 * q + 2)
                dve.tensor_tensor(rows[:, b, q, :], rows[:, b, q, :], scale_b[:], ALU.mult).then_inc(h2_step, 1)
                dve.wait_ge(h2_step, 9 * c + 2 * q + 3)
                dve.scalar_tensor_tensor(rows[:, b, q, :], bias_b[:], nm[:, bass.ds(c * QT + q, 1)],
                                         rows[:, b, q, :], ALU.mult, ALU.add).then_inc(h2_ok, 1)

            def turned_lo(c, q):
                dve.wait_ge(h2t_hi_ok, QT * c + q + 1)
                cols = slice(q * P, (q + 1) * P)
                dve.tensor_tensor(h2t_lo[:, :, cols], turn_ps[:], h2t_hi[:, :, cols].bitcast(F32),
                                  ALU.subtract).then_inc(h2t_lo_ok, 1)

            def take_y(c, b, q):
                dve.wait_ge(down_ok, FT * QT * c + QT * (FT - 1) + q + 1)
                dve.tensor_tensor(rows[:, b, q, :], down_ps[:, q, :], rows[:, b, q, :], ALU.add).then_inc(y_taken, 1)

            def add_x(c, b, q):
                if q == 0:
                    dve.wait_ge(xr_in, 16 * (c + 1))
                dve.wait_ge(y_taken, QT * c + q + 1)
                dve.tensor_tensor(rows[:, b, q, :], rows[:, b, q, :], xr[:, q, :], ALU.add).then_inc(y_ok, 1)
                dve.wait_ge(y_ok, QT * c + q + 1)
                moments(order_y(c), 1, q, b)

            def norm_y(c, b, q):
                if q == 0:
                    dve.wait_ge(rstd_ok, order_y(c) + 1)
                dve.tensor_scalar(rows[:, b, q, :], rows[:, b, q, :], mv[:, 1, q, 0:1], rstd[:, 1, q:q + 1],
                                  ALU.subtract, ALU.mult).then_inc(out_ok, 1)

            def body(c, b):
                for f in range(FT):
                    if not is_last(c) and 8 <= f < 12:
                        add_attn(c + 1, 1 - b, f - 8)
                    dve.wait_ge(gelu_ok, FT * c + f + 1)
                    dve.tensor_tensor(g_lo[:, f % GR4, :], g32[:, f % 2, :], g_hi[:, f % GR4, :].bitcast(F32),
                                      ALU.subtract).then_inc(g_lo_ok, 1)
                    if not is_first(c):
                        if f < 4:
                            add_x(c - 1, 1 - b, f)
                        elif f < 6:
                            norm_y(c - 1, 1 - b, 2 * (f - 4))
                            norm_y(c - 1, 1 - b, 2 * (f - 4) + 1)
                    if not is_last(c) and f >= 12:
                        norm_h1(c + 1, 1 - b, f - 12)
                if not is_last(c):
                    for q in range(QT):
                        turned_lo(c + 1, q)
                for q in range(QT):
                    take_y(c, b, q)

            for q in range(QT):
                add_attn(0, 0, q)
            for q in range(QT):
                norm_h1(0, 0, q)
                if q > 0:
                    turned_lo(0, q - 1)
            turned_lo(0, QT - 1)
            over_chunks(dve, body)
            for q in range(QT):
                add_x(NC - 1, 1, q)
            for q in range(QT):
                norm_y(NC - 1, 1, q)

        @block.tensor
        def _(pe):
            def attn(c, q):
                pe.wait_ge(ctx_in[q % 2], 16 * (2 * c + q // 2 + 1))
                if not is_first(c):
                    pe.wait_ge(h1_step, QT * c + q)
                for k in range(KT):
                    last = pe.matmul(attn_bank(c, q), ctxt[:, q % 2, k, :], wo[:, k, :],
                                     start=(k == 0), stop=(k == KT - 1))
                last.then_inc(attn_ok, 1)

            def turn(c, b, q):
                pe.wait_ge(h2_ok, QT * c + q + 1)
                wait(pe, h2t_lo_ok, QT * c + q)
                for k in range(KT):
                    last = pe.transpose(turn_ps[:, k, :], rows[:, b, q, k * P:(k + 1) * P], ident[:])
                last.then_inc(turned, 1)

            def up(c, f):
                if f == 0:
                    pe.wait_ge(h2t_lo_ok, QT * c + QT)
                if is_first(c) and f % 4 == 0:
                    pe.wait_ge(w_in[f // 4], 64)
                wait(pe, gelu_ok, FT * c + f - 1)
                cols = slice(f * P, (f + 1) * P)
                for k in range(KT):
                    for i, (w, h) in enumerate(((w1_hi, h2t_hi), (w1_hi, h2t_lo), (w1_lo, h2t_hi))):
                        last = pe.matmul(up_ps[:, f % 2, :], w[:, k, cols], h[:, k, :],
                                         start=(k == 0 and i == 0), stop=(k == KT - 1 and i == 2))
                last.then_inc(up_ok, 1)

            def down(c, f):
                pe.wait_ge(g_lo_ok, FT * c + f + 1)
                for q in range(QT):
                    if f == 0:
                        wait(pe, y_taken, QT * (c - 1) + q + 1)
                    cols = slice(q * P, (q + 1) * P)
                    for i, (g, w) in enumerate(((g_hi, w2_hi), (g_hi, w2_lo), (g_lo, w2_hi))):
                        last = pe.matmul(down_ps[:, q, :], g[:, f % GR4, cols], w[:, f, :],
                                         start=(f == 0 and i == 0), stop=(f == FT - 1 and i == 2))
                    last.then_inc(down_ok, 1)

            def body(c, b):
                for f in range(FT):
                    up(c, f)
                    if 7 <= f < 11 and not is_last(c):
                        attn(c + 1, f - 7)
                    if f >= DLAG:
                        down(c, f - DLAG)
                    if f == FT - 2 and not is_last(c):
                        turn(c + 1, 1 - b, 0)
                for i in range(DLAG):
                    if not is_last(c):
                        turn(c + 1, 1 - b, i + 1)
                    down(c, FT - DLAG + i)

            pe.wait_ge(ident_ok, 1)
            pe.wait_ge(consts_in, 16 * 5)
            for q in range(QT):
                attn(0, q)
            for q in range(QT):
                turn(0, 0, q)
            over_chunks(pe, body)


def program(nc, io):
    def scratch(name, shape, dt=F32):
        return nc.dram_tensor(name, shape, dt, kind="Internal").ap()

    scr = {n: scratch("scr_" + n, (D, N)) for n in ("k_hi", "k_lo", "q_hi", "q_lo", "ctx")}
    scr["v"] = scratch("scr_v", (N, D))
    scr["ht"] = scratch("scr_ht", (N, D))
    scr.update({n: scratch("scr_" + n, (D, F)) for n in ("w1_hi", "w1_lo")})
    scr.update({n: scratch("scr_" + n, (F, D)) for n in ("w2_hi", "w2_lo")})
    scr["shift"] = scratch("scr_shift", (2, QT, P))
    scr["edge_t"] = scratch("scr_edge_t", (NC, P, ST, CH), U8)
    with ExitStack() as ctx:
        keep = {"v_tot": ctx.enter_context(nc.sbuf_tensor("v_tot", [P, PAIRS], F32)),
                "minus_bound": ctx.enter_context(nc.sbuf_tensor("minus_bound", [P, 1], F32)),
                "bounded_f": ctx.enter_context(nc.sbuf_tensor("bounded_f", [1, 1], F32)),
                "bounded_i": ctx.enter_context(nc.sbuf_tensor("bounded_i", [1, 1], I32))}
        project(nc, io, scr, keep)
        def early(name, shape, dt=F32):
            return ctx.enter_context(nc.sbuf_tensor(name, shape, dt))

        keep.update({n: early(n, [P, D]) for n in ("bo_b", "ln2_scale_b", "ln2_bias_b")})
        keep["wo"] = early("wo", [P, KT, D])
        keep["nodemask"] = early("nodemask", [P, ST], I32)
        keep["ctx_in"] = early("ctx_in", [P, 2, KT, P])
        keep["rows"] = early("rows", [P, 2, QT, D])
        keep.update({n: nc.alloc_semaphore("f_" + n) for n in ("consts_in", "ht_in")})
        keep["ctx_in_sems"] = [nc.alloc_semaphore(f"ctx_in{i}") for i in range(2)]
        attend(nc, io, scr, keep)
        feed(nc, io, scr, keep)


_INS = ["x", "adj", "nodemask", "h_target", "ln1_scale", "ln1_bias", "Wq", "bq", "Wk", "bk", "Wv", "bv",
        "Wo", "bo", "ln2_scale", "ln2_bias", "W1", "W2"]


def kernel(**inputs):
    import numpy as np
    import concourse.bacc as bacc
    from concourse.bass_utils import run_bass_kernel_spmd

    nc = bacc.Bacc("TRN2", target_bir_lowering=False, num_devices=1)
    arrays, io = {}, {}
    for name in _INS:
        a = np.ascontiguousarray(inputs.get(name, inputs.get("L0_gnn_" + name)))
        arrays["in_" + name] = a
        io[name] = nc.dram_tensor("in_" + name, a.shape, mybir.dt.from_np(a.dtype), kind="ExternalInput").ap()
    io["out"] = nc.dram_tensor("out", (N, D), F32, kind="ExternalOutput").ap()
    program(nc, io)
    return run_bass_kernel_spmd(nc, [arrays], core_ids=[0]).results[0]["out"]
```
